# Optimizing a Trainium2 kernel written in Bass

```python
import numpy as np
import jax
import jax.numpy as jnp

def _softmax(x, axis=-1):
    return jax.nn.softmax(x, axis=axis)
def _gelu(x):
    return jax.nn.gelu(x, approximate=True)
def _silu(x):
    return jax.nn.silu(x)
def _sigmoid(x):
    return jax.nn.sigmoid(x)
def _layernorm(x, axis=-1, eps=1e-5):
    m = jnp.mean(x, axis=axis, keepdims=True)
    v = jnp.var(x, axis=axis, keepdims=True)
    return (x - m) / jnp.sqrt(v + eps)
def _scatter_add(tgt, idx, src, axis=0):
    return tgt.at[idx].add(src)
def _segment_sum(src, seg, n):
    return jax.ops.segment_sum(src, seg, n)

kernel_name = 'mk_adj_preln_d4_adj_256_df95b5'

def setup_inputs(seed: int = 0):
    np.random.seed(seed)
    _w = jnp.asarray
    def _rec_inputs():
        import jax
        import jax.numpy as jnp
        _gk = jax.random.key(seed)
        x = -0.0006128 + 1 * jax.random.normal(jax.random.fold_in(_gk, 1), (16, 1024, 256), jnp.float32)
        _a = jax.random.bernoulli(jax.random.fold_in(_gk, 2), 0.015625, (16, 1024, 1024))
        _a = jnp.logical_or(_a, jnp.swapaxes(_a, -1, -2))
        _a = jnp.logical_or(_a, jnp.eye(1024, dtype=bool))
        adj = _a.astype(jnp.int32)
        return x, adj
    x, adj = _rec_inputs()
    def _L0_gnn_setup():
        import jax, jax.numpy as jnp
        import numpy as np
        D = 256
        H = 8
        HD = D // H
        key = jax.random.key(seed)
        ks = jax.random.split(key, 10)
        BT, N = (32, 400)
        s = 1.0 / np.sqrt(D)
        return {'x': jax.random.normal(ks[0], (BT, N, D), dtype=jnp.float32), 'adj': jax.random.randint(ks[1], (BT, N, N), 0, 2, dtype=jnp.int32), 'Wq': jax.random.normal(ks[2], (D, D), dtype=jnp.float32) * s, 'bq': jnp.zeros((D,), dtype=jnp.float32), 'Wk': jax.random.normal(ks[3], (D, D), dtype=jnp.float32) * s, 'bk': jnp.zeros((D,), dtype=jnp.float32), 'Wv': jax.random.normal(ks[4], (D, D), dtype=jnp.float32) * s, 'bv': jnp.zeros((D,), dtype=jnp.float32), 'Wo': jax.random.normal(ks[5], (D, D), dtype=jnp.float32) * s, 'bo': jnp.zeros((D,), dtype=jnp.float32)}
    _L0_gnn_all = _L0_gnn_setup()
    _L0_gnn_in = {k: v for k, v in _L0_gnn_all.items() if k in ('Wq', 'bq', 'Wk', 'bk', 'Wv', 'bv', 'Wo', 'bo', )}
    del _L0_gnn_all

    def _L1_gnn_setup():
        import jax, jax.numpy as jnp
        import numpy as np
        key = jax.random.key(seed)
        k1, k2, k3, k4 = jax.random.split(key, 4)
        B, N, F, U = (8, 2048, 256, 256)
        x = jax.random.normal(k1, (B, N, F), dtype=jnp.float32)
        adj = jax.random.randint(k2, (B, N, N), 0, 2, dtype=jnp.int32)
        W_msg = jax.random.normal(k3, (F, U), dtype=jnp.float32) / np.sqrt(F)
        W_upd = jax.random.normal(k4, (F, U), dtype=jnp.float32) / np.sqrt(F)
        bias = jnp.zeros((U,), dtype=jnp.float32)
        return {'x': x, 'adj': adj, 'W_msg': W_msg, 'W_upd': W_upd, 'bias': bias}
    _L1_gnn_all = _L1_gnn_setup()
    _L1_gnn_in = {k: v for k, v in _L1_gnn_all.items() if k in ('W_msg', 'W_upd', 'bias', )}
    del _L1_gnn_all

    def _L2_gnn_setup():
        import jax, jax.numpy as jnp
        import numpy as np
        B, N, IN_F, OUT_F, H, NUM_EDGE_TYPES = (16, 512, 256, 256, 8, 50)
        HEAD_DIM = OUT_F // H
        LN_EPS = 1e-05
        key = jax.random.key(seed)
        ks = jax.random.split(key, 8)
        x = jax.random.normal(ks[0], (B, N, IN_F), dtype=jnp.float32)
        adj = jax.random.randint(ks[1], (B, N, N), 0, 2, dtype=jnp.int32)
        edge_types = jax.random.randint(ks[2], (B, N, N), 0, NUM_EDGE_TYPES, dtype=jnp.int32)
        W = jax.random.normal(ks[3], (IN_F, OUT_F), dtype=jnp.float32) / np.sqrt(IN_F)
        a1 = jax.random.normal(ks[4], (HEAD_DIM,), dtype=jnp.float32) / np.sqrt(HEAD_DIM)
        a2 = jax.random.normal(ks[5], (HEAD_DIM,), dtype=jnp.float32) / np.sqrt(HEAD_DIM)
        edge_emb = jax.random.normal(ks[6], (NUM_EDGE_TYPES, H), dtype=jnp.float32) * 0.02
        edge_emb = edge_emb.at[0].set(0.0)
        ln_gamma = jnp.ones((OUT_F,), dtype=jnp.float32)
        ln_beta = jnp.zeros((OUT_F,), dtype=jnp.float32)
        return {'x': x, 'adj': adj, 'edge_types': edge_types, 'W': W, 'a1': a1, 'a2': a2, 'edge_emb': edge_emb, 'ln_gamma': ln_gamma, 'ln_beta': ln_beta}
    _L2_gnn_all = _L2_gnn_setup()
    _L2_gnn_in = {k: v for k, v in _L2_gnn_all.items() if k in ('W', 'a1', 'a2', 'edge_emb', 'ln_gamma', 'ln_beta', )}
    del _L2_gnn_all

    def _L3_gnn_setup():
        import jax, jax.numpy as jnp
        import numpy as np
        ALPHA = 0.2
        NEG_BIG = -9000000000000000.0
        key = jax.random.key(seed)
        k1, k2, k3, k4 = jax.random.split(key, 4)
        bs, N, Fin, Fout = (4, 4096, 256, 256)
        inp = jax.random.normal(k1, (bs, N, Fin), dtype=jnp.float32)
        adj = jax.random.randint(k2, (bs, N, N), 0, 2, dtype=jnp.int32)
        W = jax.random.normal(k3, (Fin, Fout), dtype=jnp.float32) * (1.414 / np.sqrt(Fin))
        a = jax.random.normal(k4, (2 * Fout, 1), dtype=jnp.float32) * 0.1
        return {'input': inp, 'adj': adj, 'W': W, 'a': a}
    _L3_gnn_all = _L3_gnn_setup()
    _L3_gnn_in = {k: v for k, v in _L3_gnn_all.items() if k in ('W', 'a', )}
    del _L3_gnn_all

    return {
        "x": x,
        "adj": adj,
        "L0_gnn_Wq": _L0_gnn_in["Wq"],
        "L0_gnn_bq": _L0_gnn_in["bq"],
        "L0_gnn_Wk": _L0_gnn_in["Wk"],
        "L0_gnn_bk": _L0_gnn_in["bk"],
        "L0_gnn_Wv": _L0_gnn_in["Wv"],
        "L0_gnn_bv": _L0_gnn_in["bv"],
        "L0_gnn_Wo": _L0_gnn_in["Wo"],
        "L0_gnn_bo": _L0_gnn_in["bo"],
        "L1_gnn_W_msg": _L1_gnn_in["W_msg"],
        "L1_gnn_W_upd": _L1_gnn_in["W_upd"],
        "L1_gnn_bias": _L1_gnn_in["bias"],
        "L2_gnn_W": _L2_gnn_in["W"],
        "L2_gnn_a1": _L2_gnn_in["a1"],
        "L2_gnn_a2": _L2_gnn_in["a2"],
        "L2_gnn_edge_emb": _L2_gnn_in["edge_emb"],
        "L2_gnn_ln_gamma": _L2_gnn_in["ln_gamma"],
        "L2_gnn_ln_beta": _L2_gnn_in["ln_beta"],
        "L3_gnn_W": _L3_gnn_in["W"],
        "L3_gnn_a": _L3_gnn_in["a"],
    }

def reference(x, adj, L0_gnn_Wq, L0_gnn_bq, L0_gnn_Wk, L0_gnn_bk, L0_gnn_Wv, L0_gnn_bv, L0_gnn_Wo, L0_gnn_bo, L1_gnn_W_msg, L1_gnn_W_upd, L1_gnn_bias, L2_gnn_W, L2_gnn_a1, L2_gnn_a2, L2_gnn_edge_emb, L2_gnn_ln_gamma, L2_gnn_ln_beta, L3_gnn_W, L3_gnn_a):
    import jax
    import jax.numpy as jnp
    def _L0_gnn_ref(x, adj, Wq, bq, Wk, bk, Wv, bv, Wo, bo):
        import jax, jax.numpy as jnp
        import numpy as np
        D = 256
        H = 8
        HD = D // H
        BT, N, _ = x.shape

        def heads(t):
            return t.reshape(BT, N, H, HD).transpose(0, 2, 1, 3)
        q = heads(x @ Wq + bq)
        k = heads(x @ Wk + bk)
        v = heads(x @ Wv + bv)
        scores = jnp.einsum('bhnd,bhmd->bhnm', q, k) / np.sqrt(HD)
        mask = (adj == 0)[:, None, :, :]
        scores = jnp.where(mask, -jnp.inf, scores)
        attn = jax.nn.softmax(scores, axis=-1)
        ctx = jnp.einsum('bhnm,bhmd->bhnd', attn, v)
        ctx = ctx.transpose(0, 2, 1, 3).reshape(BT, N, D)
        return ctx @ Wo + bo

    def _L1_gnn_ref(x, adj, W_msg, W_upd, bias):
        import jax, jax.numpy as jnp
        import numpy as np
        a = adj.astype(x.dtype)
        h = jnp.einsum('bnf,fu->bnu', x, W_msg)
        msg_sum = jnp.einsum('bij,biu->bju', a, h)
        deg = jnp.sum(a, axis=1)
        messages = jnp.where(deg[..., None] > 0, msg_sum / jnp.maximum(deg, 1.0)[..., None], 0.0)
        out = jnp.einsum('bnf,fu->bnu', x, W_upd) + messages + bias
        return jax.nn.relu(out)

    def _L2_gnn_ref(x, adj, edge_types, W, a1, a2, edge_emb, ln_gamma, ln_beta):
        import jax, jax.numpy as jnp
        import numpy as np
        B, N, IN_F, OUT_F, H, NUM_EDGE_TYPES = (16, 512, 256, 256, 8, 50)
        HEAD_DIM = OUT_F // H
        LN_EPS = 1e-05
        Bx, Nx, _ = x.shape
        Wh = (x @ W).reshape(Bx, Nx, H, HEAD_DIM)
        s1 = jnp.einsum('bnhd,d->bnh', Wh, a1)
        s2 = jnp.einsum('bnhd,d->bnh', Wh, a2)
        e = s1[:, :, None, :] + s2[:, None, :, :] + edge_emb[edge_types]
        e = jnp.where(e > 0, e, 0.2 * e)
        e = jnp.where((adj == 0)[..., None], jnp.float32(-1000000000.0), e)
        alpha = jax.nn.softmax(e, axis=2)
        h = jnp.einsum('bijh,bjhd->bihd', alpha, Wh).reshape(Bx, Nx, OUT_F)
        mu = jnp.mean(h, axis=-1, keepdims=True)
        var = jnp.mean(jnp.square(h - mu), axis=-1, keepdims=True)
        hn = (h - mu) * jax.lax.rsqrt(var + LN_EPS) * ln_gamma + ln_beta
        return jax.nn.elu(hn)

    def _L3_gnn_ref(input, adj, W, a):
        import jax, jax.numpy as jnp
        import numpy as np
        ALPHA = 0.2
        NEG_BIG = -9000000000000000.0
        h = jnp.matmul(input, W)
        Fout = W.shape[1]
        a1 = a[:Fout, 0]
        a2 = a[Fout:, 0]
        f1 = jnp.einsum('bnf,f->bn', h, a1)
        f2 = jnp.einsum('bnf,f->bn', h, a2)
        e = jax.nn.leaky_relu(f1[:, :, None] + f2[:, None, :], negative_slope=ALPHA)
        logits = jnp.where(adj > 0, e, NEG_BIG)
        attention = jax.nn.softmax(logits, axis=1)
        h_prime = jnp.matmul(attention, h)
        return jax.nn.elu(h_prime)

    h = jnp.maximum(_layernorm(x, axis=-1), 0.0)
    x = x + _L0_gnn_ref(h, adj, L0_gnn_Wq, L0_gnn_bq, L0_gnn_Wk, L0_gnn_bk, L0_gnn_Wv, L0_gnn_bv, L0_gnn_Wo, L0_gnn_bo)
    h = jnp.maximum(_layernorm(x, axis=-1), 0.0)
    x = x + _L1_gnn_ref(h, adj, L1_gnn_W_msg, L1_gnn_W_upd, L1_gnn_bias)
    h = jnp.maximum(_layernorm(x, axis=-1), 0.0)
    x = x + _L2_gnn_ref(h, adj, adj, L2_gnn_W, L2_gnn_a1, L2_gnn_a2, L2_gnn_edge_emb, L2_gnn_ln_gamma, L2_gnn_ln_beta)
    h = jnp.maximum(_layernorm(x, axis=-1), 0.0)
    x = x + _L3_gnn_ref(h, adj, L3_gnn_W, L3_gnn_a)
    return x


_drawn_inputs = setup_inputs


def setup_inputs(seed=0):
    import zlib

    import numpy as np

    out = dict(_drawn_inputs(seed))
    spreads = {'L0_gnn_bq': (0.0, 0.8),
     'L0_gnn_bk': (0.0, 2.0),
     'L0_gnn_bv': (0.0, 0.1),
     'L0_gnn_bo': (0.0, 0.1),
     'L1_gnn_bias': (0.0, 0.1),
     'L2_gnn_ln_gamma': (1.0, 0.2),
     'L2_gnn_ln_beta': (0.0, 0.1)}
    factors = {'L2_gnn_edge_emb': 64.0, 'L2_gnn_a1': 2.667}
    for name, (base, spread) in spreads.items():
        noise = np.random.default_rng([zlib.crc32(name.encode()), seed]).standard_normal(out[name].shape)
        drawn = base * np.exp(spread * noise) if base else spread * noise
        out[name] = jnp.asarray(drawn.astype(out[name].dtype))
    for name, factor in factors.items():
        out[name] = (out[name] * factor).astype(out[name].dtype)
    return out
```

```python
from contextlib import ExitStack

import numpy as np

import concourse.bass as bass
from concourse import mybir


class Steps:

    def __init__(self, engine, semaphore):
        self.engine, self.semaphore, self.count = engine, semaphore, 0

    def did(self, instruction):
        instruction.then_inc(self.semaphore, 1)
        self.count += 1
        return self.count

    def after(self, count):
        self.engine.wait_ge(self.semaphore, count)


def build_program(nc, x_dram, adj_dram, w, out_dram):
    f32, f16, bf16, i32 = mybir.dt.float32, mybir.dt.float16, mybir.dt.bfloat16, mybir.dt.int32
    ALU, ACT, AX = mybir.AluOpType, mybir.ActivationFunctionType, mybir.AxisListType

    B, N, D = x_dram.shape
    P = 128
    NT = N // P
    DT = D // P
    H = 8
    HD = D // H
    HG = 4
    NG = H // HG
    NH = N // 512
    QSCALE = float(1.0 / np.sqrt(HD))
    EPS = 1e-5
    MASKED = -1e30
    SLOPE = 0.2
    STEEP = 1.0 - SLOPE
    GMAX = 100.0
    UNITS = NT * H
    GROUPS = UNITS // HG

    ctx = ExitStack()
    with ctx:
        def sb(name, shape, dt):
            return ctx.enter_context(nc.sbuf_tensor(name, shape, dt))

        def sem(name):
            return ctx.enter_context(nc.semaphore(name))

        x = sb("x", [P, NT, D], f32)
        hT = sb("hT", [P, DT, N], f32)
        adjN = sb("adjN", [P, NT, N], f16)
        adjT = sb("adjT", [P, NT, N], f16)
        maskN = sb("maskN", [P, NT, N], bf16)
        headpairs = sb("headpairs", [P, 8192], f32)
        qkparts = sb("qkparts", [P, 4096], f32)
        wide = sb("wide", [P, 8192], f32)
        V = sb("V", [P, NT, D], f32)
        zbuf = sb("zbuf", [P, 3, N], f32)
        pbuf = sb("pbuf", [P, 3, N], f32)

        pairs16 = headpairs[:, :].bitcast(f16)
        QP = pairs16[:, 0:H * N].rearrange("p (h n) -> p h n", h=H)
        KP = pairs16[:, H * N:2 * H * N].rearrange("p (h n) -> p h n", h=H)
        MHW = 258
        msgH = pairs16[:, 0:NT * MHW].rearrange("p (t d) -> p t d", t=NT)
        msgL = pairs16[:, NT * MHW:NT * MHW + NT * D].rearrange("p (t d) -> p t d", t=NT)
        steepT = headpairs[:, :].rearrange("p (h n) -> p h n", h=H)
        parts16 = qkparts[:, :].bitcast(f16)
        QH, QL, KH, KL = (parts16[:, k * DT * N:(k + 1) * DT * N].rearrange("p (t n) -> p t n", t=DT)
                          for k in range(4))
        xn = qkparts[:, 0:NT * D].rearrange("p (t d) -> p t d", t=NT)
        vmH, vmL = (parts16[:, (2 + k) * NT * D:(3 + k) * NT * D].rearrange("p (t d) -> p t d", t=NT)
                    for k in range(2))
        x_next = qkparts[:, NT * D:2 * NT * D].rearrange("p (t d) -> p t d", t=NT)
        vm_wide = pbuf[:, 0:2, :].rearrange("p a (t d) -> p (a t) d", d=D)
        whole = pbuf[:, 0:2, :].rearrange("p a (t d) -> p (a t) d", d=512)
        adj_int = headpairs[:, :].bitcast(i32).rearrange("p (t n) -> p t n", t=NT)
        PT = wide[:, :].rearrange("p (b r t n) -> p b r t n", b=2, r=HG, t=NT)
        R = wide[:, :].rearrange("p (b r n) -> p b r n", b=2, r=HG)
        PU = wide[:, :].rearrange("p (t n) -> p t n", t=NT)

        wq, wk, wv, wo, wmsg, wupd, w2, w3 = (sb(n, [P, DT, D], f32) for n in
                                             ("wq", "wk", "wv", "wo", "wmsg", "wupd", "w2", "w3"))
        wa2 = sb("wa2", [P, DT, 2, H], f32)
        wa3 = sb("wa3", [P, DT, 2], f32)
        bv_b, bo_b, b1_b, gam_b, bet_b = (sb(n, [P, D], f32) for n in
                                          ("bv_b", "bo_b", "b1_b", "gam_b", "bet_b"))
        bq_c, bk_c = sb("bq_c", [P, DT], f32), sb("bk_c", [P, DT], f32)
        a2_b = sb("a2_b", [P, 2, HD], f32)
        edge_b = sb("edge_b", [P, H], f32)
        both = sb("both", [P, H], f32)
        ones_b = sb("ones_b", [P, D], f32)
        identF = sb("identF", [P, P], f32)
        identH = sb("identH", [P, P], f16)
        nhalf = sb("nhalf", [P, NT], f32)

        stats = sb("stats", [P, NT, 6], f32)
        meanvar = sb("meanvar", [P, NT, 2], f32)
        vareps = sb("vareps", [P, NT], f32)
        rstd = sb("rstd", [P, NT], f32)
        nmax = sb("nmax", [P, UNITS], f32)
        den = sb("den", [P, UNITS], f32)
        rden = sb("rden", [P, UNITS], f32)
        bcS = sb("bcS", [P, 2, P], f32)
        deg = sb("deg", [P, NT, 2], f32)
        gmax = sb("gmax", [P, 2], f32)
        gmaxB = sb("gmaxB", [P, 2 * H], f32)
        kexp = sb("kexp", [P, 3, H], f32)
        t2 = sb("t2", [P, 2, NT * H], f32)
        b2 = sb("b2", [P, NT, H], f32)
        v2 = sb("v2", [P, NT, H], f32)
        kv = sb("kv", [P, NT, H], f32)
        kvHL = sb("kvHL", [P, NT, 2 * H], f16)
        sums, rsums = sb("sums", [P, NT, H], f32), sb("rsums", [P, NT, H], f32)
        e3 = sb("e3", [P, 3, NT], f32)
        b3, k3, den3, rden3 = (sb(n, [P, NT], f32) for n in ("b3", "k3", "den3", "rden3"))
        f3 = sb("f3", [P, 4], f32)

        pair = [ctx.enter_context(nc.psum_tensor(f"pair{i}", [P, 1024], f32)) for i in range(4)]
        bank = [pair[i // 2][:, (i % 2) * 512:(i % 2) * 512 + 512] for i in range(8)]

        steep_dram = nc.dram_tensor("steep_rows", (H, N), f32, kind="Internal").ap()

        w_in, w_small, ident_set, setup_steps = (sem(n) for n in
                                                 ("w_in", "w_small", "ident_set", "setup_steps"))
        with nc.Block() as block:
            @block.sync
            def _(sp):
                for name, dst in (("L0_gnn_Wq", wq), ("L0_gnn_Wk", wk), ("L0_gnn_Wv", wv),
                                  ("L0_gnn_Wo", wo), ("L1_gnn_W_msg", wmsg), ("L1_gnn_W_upd", wupd),
                                  ("L2_gnn_W", w2), ("L3_gnn_W", w3)):
                    sp.dma_start(dst[:, :, :], w[name].rearrange("(t p) n -> p t n", p=P)).then_inc(w_in, 16)
                sp.wait_ge(w_in, 8 * 16)

            @block.scalar
            def _(act):
                small = 0
                for dst, src in ((bv_b[:, :], w["L0_gnn_bv"].partition_broadcast(P)),
                                 (bo_b[:, :], w["L0_gnn_bo"].partition_broadcast(P)),
                                 (b1_b[:, :], w["L1_gnn_bias"].partition_broadcast(P)),
                                 (gam_b[:, :], w["L2_gnn_ln_gamma"].partition_broadcast(P)),
                                 (bet_b[:, :], w["L2_gnn_ln_beta"].partition_broadcast(P)),
                                 (a2_b[:, 0, :], w["L2_gnn_a1"].partition_broadcast(P)),
                                 (a2_b[:, 1, :], w["L2_gnn_a2"].partition_broadcast(P)),
                                 (zbuf[:, 0, 0:2 * D], w["L3_gnn_a"].rearrange("n o -> (n o)").partition_broadcast(P)),
                                 (edge_b[:, :], w["L2_gnn_edge_emb"][1, :].partition_broadcast(P)),
                                 (bq_c[:, :], w["L0_gnn_bq"].rearrange("(t p) -> p t", p=P)),
                                 (bk_c[:, :], w["L0_gnn_bk"].rearrange("(t p) -> p t", p=P))):
                    act.dma_start(dst, src, allow_slow_non_contiguous=True).then_inc(w_small, 16)
                    small += 16
                act.wait_ge(w_small, small)

            @block.gpsimd
            def _(pool):
                nc.gpsimd.memset(nhalf[:, :], -0.5)
                nc.gpsimd.memset(ones_b[:, :], 1.0)
                nc.gpsimd.memset(identF[:, :], 0.0).then_inc(ident_set, 1)
                nc.gpsimd.memset(identH[:, :], 0.0).then_inc(ident_set, 1)
                pool.wait_ge(ident_set, 2)
                for m in (identF, identH):
                    nc.gpsimd.affine_select(out=m[:, :], in_=m[:, :], compare_op=ALU.not_equal, fill=1.0,
                                            base=0, pattern=[[-1, P]], channel_multiplier=1).then_inc(ident_set, 1)
                pool.wait_ge(ident_set, 4)

            @block.vector
            def _(dve):
                steps = Steps(dve, setup_steps)
                dve.wait_ge(w_in, 8 * 16)
                dve.wait_ge(w_small, 11 * 16)
                nc.vector.tensor_scalar(bq_c[:, :], bq_c[:, :], QSCALE, None, ALU.mult)
                dve.wait_ge(ident_set, 4)
                nc.vector.tensor_tensor(both[:, :], identF[:, 0:H], identF[:, H:2 * H], ALU.add)
                for c in range(DT):
                    for k in range(2):
                        n = steps.did(nc.vector.tensor_tensor(
                            pbuf[:, c, k * D:(k + 1) * D].rearrange("p (h d) -> p h d", h=H),
                            w2[:, c, :].rearrange("p (h d) -> p h d", h=H),
                            a2_b[:, k, :].unsqueeze(1).to_broadcast([P, H, HD]), ALU.mult))
                        n = steps.did(nc.vector.tensor_tensor(
                            pbuf[:, c, (2 + k) * D:(3 + k) * D],
                            w3[:, c, :], zbuf[:, 0, k * D:(k + 1) * D], ALU.mult))
                steps.after(n)
                for c in range(DT):
                    for k in range(2):
                        nc.vector.tensor_reduce(wa2[:, c, k, :],
                                                pbuf[:, c, k * D:(k + 1) * D].rearrange("p (h d) -> p h d", h=H),
                                                AX.X, ALU.add)
                        n = steps.did(nc.vector.tensor_reduce(wa3[:, c, k:k + 1],
                                                              pbuf[:, c, (2 + k) * D:(3 + k) * D], AX.X, ALU.add))
                steps.after(n)

        names = ["x_in", "x_out", "x_taken", "q_parts", "k_parts", "v_ready", "qk_psum", "v_psum", "qk_wide",
                 "scores", "z_ready", "p_ready", "turned", "pt_even", "pt_odd", "pv_done", "rden_ready",
                 "sums_spread", "sums_copied", "ctx_ready", "projected",
                 "adj_cast", "mask_ready", "adjT_psum", "adjT_ready",
                 "msg_psum", "msg_hi", "msg_parts", "ones_set", "agg_psum", "upd_psum",
                 "s_rows", "s_cols", "wh_psum", "gmax_ready", "gmax_spread", "t2_ready", "steep_row", "steep_out",
                 "bvexp_ready", "kappa_ready", "kv_ready", "den_cols", "den_cols_read", "wh_scaled", "vm_wide",
                 "vm_hi", "vm_lo", "masked_steep", "r_ready", "group_done", "num_copied", "den_copied",
                 "back_turned", "hout_ready", "y_ready", "y_exp", "x_less_one",
                 "a3_psum", "f3_cols", "wh3_psum", "f3_ready", "a3_ready", "e3_ready", "b3_ready",
                 "wh3_copied", "mu_ready", "pu_ready", "g3_ready", "out3_psum", "o_exp",
                 "x_done0", "x_done1", "x_done2", "x_done3", "dve_steps"]
        names += [f"adj_in{t}" for t in range(NT)] + [f"head_pairs{h}" for h in range(H)]
        names += [f"steep_in{h}" for h in range(H)]
        for L in range(5):
            names += [f"ln_var{L}", f"ln_rstd{L}", f"ln_x{L}", f"ln_psum{L}", f"hT_ready{L}"]
        S = {n: sem(n) for n in names}
        numbers = [S[n].num for n in names]
        assert numbers == list(range(numbers[0], numbers[0] + len(names)))

        def clear_signals():
            nc.gpsimd.sem_clear(range(numbers[0], numbers[0] + len(names)))
            nc.all_engine_barrier()

        def load_batch(sp, index):
            sp.dma_start(x_next[:, :, :], x_dram[index].rearrange("(t p) d -> p t d", p=P)).then_inc(S["x_in"], 16)
            for t in range(NT):
                sp.dma_start(adj_int[:, t, :], adj_dram[index, t * P:(t + 1) * P, :]).then_inc(S[f"adj_in{t}"], 16)

        def cast_adjacency(act, t):
            act.wait_ge(S[f"adj_in{t}"], 16)
            nc.scalar.activation(adjN[:, t, :], adj_int[:, t, :], ACT.Copy).then_inc(S["adj_cast"], 1)

        def make_mask(dve, t):
            dve.wait_ge(S["adj_cast"], t + 1)
            nc.vector.tensor_scalar(maskN[:, t, :], adjN[:, t, :], 0.0, MASKED, ALU.is_equal, ALU.mult)\
                .then_inc(S["mask_ready"], 1)

        def norm_stats(dve, steps, L, t, tile):
            n = steps.did(nc.vector.bn_stats(stats[:, t, :], tile))
            steps.after(n)
            n = steps.did(nc.vector.bn_aggr(meanvar[:, t, :], stats[:, t, :]))
            steps.after(n)
            nc.vector.tensor_scalar(vareps[:, t:t + 1], meanvar[:, t, 1:2], EPS, None, ALU.add)\
                .then_inc(S[f"ln_var{L}"], 1)

        def norm_apply(dve, L, t, tile):
            dve.wait_ge(S[f"ln_rstd{L}"], t + 1)
            nc.vector.tensor_scalar(xn[:, t, :], tile, meanvar[:, t, 0:1], rstd[:, t:t + 1],
                                    ALU.subtract, ALU.mult).then_inc(S[f"ln_x{L}"], 1)

        def norm_roots(pool, L):
            for t in range(NT):
                pool.wait_ge(S[f"ln_var{L}"], t + 1)
                nc.gpsimd.tensor_tensor(rstd[:, t:t + 1], vareps[:, t:t + 1], nhalf[:, 0:1], ALU.pow)\
                    .then_inc(S[f"ln_rstd{L}"], 1)

        with nc.Block() as block:
            @block.sync
            def _(sp):
                load_batch(sp, 0)

            @block.gpsimd
            def _(pool):
                norm_roots(pool, 0)

            @block.scalar
            def _(act):
                for t in range(NT):
                    cast_adjacency(act, t)

            @block.vector
            def _(dve):
                steps = Steps(dve, S["dve_steps"])
                dve.wait_ge(S["x_in"], 16)
                for t in range(NT):
                    norm_stats(dve, steps, 0, t, x_next[:, t, :])
                for t in range(NT):
                    norm_apply(dve, 0, t, x_next[:, t, :])
                for t in range(NT):
                    make_mask(dve, t)
        clear_signals()

        with nc.Fori(0, B) as b:
            with nc.Block() as block:
                @block.sync
                def _(sp):
                    for c in range(DT):
                        sp.wait_ge(S["q_parts"], 2 * (c + 1) * NH)
                        sp.wait_ge(S["k_parts"], 2 * (c + 1) * NH)
                        for r in range(HG):
                            h = c * HG + r
                            rows = slice(r * HD, (r + 1) * HD)
                            for quarter, (qs, ks) in enumerate(((QH, KH), (QH, KL), (QL, KH), (QL, KL))):
                                to = slice(quarter * HD, (quarter + 1) * HD)
                                sp.dma_start(QP[to, h, :], qs[rows, c, :]).then_inc(S[f"head_pairs{h}"], 16)
                                sp.dma_start(KP[to, h, :], ks[rows, c, :]).then_inc(S[f"head_pairs{h}"], 16)
                    sp.wait_ge(S["steep_row"], 1)
                    sp.dma_start(steep_dram[:, :], zbuf[0:H, 0, :]).then_inc(S["steep_out"], 16)
                    sp.wait_ge(S["steep_out"], 16)
                    sp.wait_ge(S["agg_psum"], NT)
                    for h in range(H):
                        sp.dma_start(steepT[:, h, :], steep_dram[h, :].partition_broadcast(P))\
                            .then_inc(S[f"steep_in{h}"], 16)
                    sp.wait_ge(S["masked_steep"], UNITS)
                    sp.wait_ge(S["group_done"], GROUPS)
                    load_batch(sp, (b + 1) % B)
                    out_r = out_dram[b].rearrange("(t p) d -> p t d", p=P)
                    for k in range(NT // 2):
                        sp.wait_ge(S["x_done3"], k + 1)
                        sp.dma_start(out_r[:, 2 * k:2 * k + 2, :], x[:, 2 * k:2 * k + 2, :]).then_inc(S["x_out"], 16)
                    sp.wait_ge(S["x_out"], NT // 2 * 16)

                @block.gpsimd
                def _(pool):
                    nc.gpsimd.tensor_tensor(x[:, :, :], x_next[:, :, :],
                                            bo_b[:, :].unsqueeze(1).to_broadcast([P, NT, D]), ALU.add)\
                        .then_inc(S["x_taken"], 1)
                    norm_roots(pool, 1)
                    norm_roots(pool, 2)
                    pool.wait_ge(S["ln_x2"], NT)
                    nc.gpsimd.tensor_tensor(x[:, :, :], x[:, :, :], ones_b[:, :].unsqueeze(1).to_broadcast([P, NT, D]),
                                            ALU.subtract).then_inc(S["x_less_one"], 1)
                    for k in range(2):
                        ts = slice(k * NT // 2, (k + 1) * NT // 2)
                        pool.wait_ge(S["vm_hi"], k + 1)
                        nc.gpsimd.tensor_tensor(vmL[:, ts, :], vm_wide[:, ts, :], vmH[:, ts, :], ALU.subtract)\
                            .then_inc(S["vm_lo"], 1)
                    norm_roots(pool, 4)
                    norm_roots(pool, 3)
                    pool.wait_ge(S["ln_x3"], NT)
                    nc.gpsimd.tensor_tensor(x[:, :, :], x[:, :, :], ones_b[:, :].unsqueeze(1).to_broadcast([P, NT, D]),
                                            ALU.subtract).then_inc(S["x_less_one"], 1)
                    pool.wait_ge(S["a3_ready"], 2)
                    for j in range(NT):
                        if j >= 3:
                            pool.wait_ge(S["pu_ready"], j - 2)
                        nc.gpsimd.tensor_tensor(pbuf[:, j % 3, :], zbuf[:, 1, :], adjT[:, j, :], ALU.mult)\
                            .then_inc(S["mu_ready"], 1)
                    norm_roots(pool, 0)

                @block.scalar
                def _(act):
                    def hT_from_psum(L, first_bank):
                        for k in range(NT // 2):
                            act.wait_ge(S[f"ln_psum{L}"], k + 1)
                            nc.scalar.activation(hT[:, :, 2 * k * P:(2 * k + 2) * P],
                                                 bank[first_bank + k].rearrange("p (c n) -> p c n", c=DT),
                                                 ACT.Relu).then_inc(S[f"hT_ready{L}"], 1)

                    hT_from_psum(0, 0)
                    for p in range(2 * DT * NH):
                        c, isk = p // 4, (p // 2) % 2
                        act.wait_ge(S["qk_psum"], p + 1)
                        if p >= 4:
                            act.wait_ge(S["k_parts" if isk else "q_parts"], 2 * (p % 2 + 1))
                        nc.scalar.activation(whole[:, p % 4, :], bank[4 + p % 4], ACT.Identity,
                                             bias=(bk_c if isk else bq_c)[:, c:c + 1],
                                             scale=1.0 if isk else QSCALE).then_inc(S["qk_wide"], 1)

                    def exp_unit(u):
                        act.wait_ge(S["z_ready"], u + 1)
                        if u >= 3:
                            act.wait_ge(S["turned"], 2 * (u - 3) + 2)
                        if u == 0:
                            act.wait_ge(S["q_parts"], 2 * DT * NH)
                            act.wait_ge(S["k_parts"], 2 * DT * NH)
                        nc.scalar.activation(pbuf[:, u % 3, :], zbuf[:, u % 3, :], ACT.Exp, bias=nmax[:, u:u + 1],
                                             scale=-1.0, accum_out=den[:, u:u + 1]).then_inc(S["p_ready"], 1)

                    def turned_odd(u):
                        g, r = u // HG, u % HG
                        act.wait_ge(S["turned"], 2 * u + 2)
                        if g >= 2:
                            act.wait_ge(S["pv_done"], g - 1)
                        nc.scalar.activation(PT[:, g % 2, r, 4:8, :].rearrange("p t n -> p (t n)"), bank[5],
                                             ACT.Copy).then_inc(S["pt_odd"], 1)

                    def spread_copy(g):
                        act.wait_ge(S["sums_spread"], g + 1)
                        if g >= 2:
                            act.wait_ge(S["ctx_ready"], g - 1)
                        nc.scalar.activation(bcS[:, g % 2, :], bank[6 + g % 2][:, P:2 * P], ACT.Copy)\
                            .then_inc(S["sums_copied"], 1)

                    for u in range(UNITS + 10):
                        if u < UNITS:
                            exp_unit(u)
                        if 2 <= u < UNITS + 2:
                            turned_odd(u - 2)
                        if u >= 10 and (u - 10) % HG == 0:
                            spread_copy((u - 10) // HG)

                    hT_from_psum(1, 0)
                    for t in range(NT):
                        act.wait_ge(S["msg_psum"], t + 1)
                        nc.scalar.activation(msgH[:, t, 0:D], bank[4 + t % 4][:, 0:D], ACT.Copy).then_inc(S["msg_hi"], 1)
                    for a in range(NT):
                        act.wait_ge(S["adjT_psum"], a + 1)
                        nc.scalar.activation(adjT[:, a, :], bank[4 + a % 2].bitcast(f16), ACT.Copy)\
                            .then_inc(S["adjT_ready"], 1)

                    hT_from_psum(2, 4)
                    act.wait_ge(S["gmax_ready"], 1)
                    nc.scalar.activation(zbuf[0:H, 0, :], pair[0][0:H, :], ACT.Exp, bias=gmax[0:H, 1:2],
                                         scale=STEEP).then_inc(S["steep_row"], 1)
                    act.wait_ge(S["t2_ready"], 1)
                    nc.scalar.activation(v2[:, :, :].rearrange("p t h -> p (t h)"), t2[:, 0, :], ACT.Exp, scale=SLOPE)\
                        .then_inc(S["bvexp_ready"], 1)
                    nc.scalar.activation(kexp[:, 1, :], kexp[:, 0, :], ACT.Exp, scale=STEEP).then_inc(S["bvexp_ready"], 1)
                    nc.scalar.activation(b2[:, :, :].rearrange("p t h -> p (t h)"), t2[:, 1, :], ACT.Exp, scale=STEEP)\
                        .then_inc(S["bvexp_ready"], 1)
                    for k in range(2):
                        ts = slice(k * NT // 2, (k + 1) * NT // 2)
                        act.wait_ge(S["vm_wide"], k + 1)
                        nc.scalar.activation(vmH[:, ts, :], vm_wide[:, ts, :], ACT.Copy).then_inc(S["vm_hi"], 1)
                    act.wait_ge(S["kappa_ready"], 1)
                    act.wait_ge(S["bvexp_ready"], 3)

                    def den_copy(hg):
                        act.wait_ge(S["group_done"], NT * (hg + 1))
                        nc.scalar.activation(pbuf[:, 1, :], pair[2 * hg + 1][:, :], ACT.Copy).then_inc(S["den_copied"], 1)

                    for u in range(UNITS):
                        g, r = u // HG, u % HG
                        hg, jt = g // NT, g % NT
                        h = hg * HG + r
                        act.wait_ge(S["masked_steep"], u + 1)
                        if g >= 2:
                            act.wait_ge(S["group_done"], g - 1)
                        nc.scalar.activation(R[:, g % 2, r, :], zbuf[:, u % 3, :], ACT.Relu, bias=kexp[:, 2, h:h + 1],
                                             scale=b2[:, jt, h:h + 1]).then_inc(S["r_ready"], 1)
                        if u == HG * NT + 5:
                            act.wait_ge(S["vm_lo"], 2)
                            den_copy(0)
                    act.wait_ge(S["hout_ready"], 1)
                    den_copy(1)
                    for k in range(NT // 2):
                        act.wait_ge(S["y_ready"], 2 * k + 2)
                        nc.scalar.activation(zbuf[:, k // 2, (k % 2) * 2 * D:(k % 2 + 1) * 2 * D],
                                             xn[:, 2 * k:2 * k + 2, :].rearrange("p t d -> p (t d)"), ACT.Exp)\
                            .then_inc(S["y_exp"], 1)

                    hT_from_psum(3, 4)
                    act.wait_ge(S["f3_ready"], 1)
                    nc.scalar.activation(zbuf[:, 0, :], pair[0][:, :], ACT.Exp, bias=f3[:, 1:2], scale=STEEP)\
                        .then_inc(S["a3_ready"], 1)
                    nc.scalar.activation(zbuf[:, 1, :], pair[0][:, :], ACT.Exp, bias=f3[:, 2:3], scale=SLOPE)\
                        .then_inc(S["a3_ready"], 1)
                    act.wait_ge(S["e3_ready"], 1)
                    nc.scalar.activation(b3[:, :], e3[:, 1, :], ACT.Exp, scale=STEEP).then_inc(S["b3_ready"], 1)
                    nc.scalar.activation(k3[:, :], e3[:, 2, :], ACT.Exp, scale=-STEEP).then_inc(S["b3_ready"], 1)
                    for t in range(NT):
                        act.wait_ge(S["wh3_psum"], t + 1)
                        nc.scalar.activation(V[:, t, :], bank[4 + t % 4][:, 0:D], ACT.Copy).then_inc(S["wh3_copied"], 1)
                    for t in range(NT):
                        cast_adjacency(act, t)
                    for k in range(NT // 2):
                        act.wait_ge(S["out3_psum"], k + 1)
                        nc.scalar.activation(zbuf[:, k // 2, (k % 2) * 512:(k % 2 + 1) * 512], bank[k], ACT.Exp)\
                            .then_inc(S["o_exp"], 1)

                @block.tensor
                def _(pe):
                    def ln_transposes(L, first_bank):
                        for t in range(NT):
                            if L > 0:
                                pe.wait_ge(S[f"ln_x{L}"], t + 1)
                            for c in range(DT):
                                last = nc.tensor.transpose(
                                    bank[first_bank + t // 2][:, c * 256 + (t % 2) * P:c * 256 + (t % 2 + 1) * P],
                                    xn[:, t, c * P:(c + 1) * P], identF[:, :])
                            if t % 2 == 1:
                                last.then_inc(S[f"ln_psum{L}"], 1)

                    def project(out, L, t, weights):
                        pe.wait_ge(S[f"hT_ready{L}"], t // 2 + 1)
                        for c in range(DT):
                            last = nc.tensor.matmul(out, hT[:, c, t * P:(t + 1) * P], weights[:, c, :],
                                                    start=(c == 0), stop=(c == DT - 1))
                        return last

                    ln_transposes(0, 0)
                    for p in range(2 * DT * NH):
                        c, isk, nh = p // 4, (p // 2) % 2, p % 2
                        pe.wait_ge(S["hT_ready0"], 2 * (nh + 1))
                        if p >= 4:
                            pe.wait_ge(S["qk_wide"], p - 3)
                        for k in range(DT):
                            last = nc.tensor.matmul(bank[4 + p % 4], (wk if isk else wq)[:, k, c * P:(c + 1) * P],
                                                    hT[:, k, nh * 512:(nh + 1) * 512], start=(k == 0), stop=(k == DT - 1))
                        last.then_inc(S["qk_psum"], 1)
                    for t in range(NT):
                        if t < 4:
                            pe.wait_ge(S["qk_wide"], 2 * DT * NH - 3 + t)
                        else:
                            pe.wait_ge(S["v_ready"], t - 3)
                        project(bank[4 + t % 4][:, 0:D], 0, t, wv).then_inc(S["v_psum"], 1)

                    def scores(u):
                        h, it = u // (HG * NT) * HG + u % HG, u // HG % NT
                        if it == 0:
                            pe.wait_ge(S[f"head_pairs{h}"], 8 * 16)
                        if u >= 2:
                            pe.wait_ge(S["z_ready"], u - 1)
                        for nh in range(NH):
                            last = nc.tensor.matmul(pair[u % 2][:, nh * 512:(nh + 1) * 512], QP[:, h, it * P:(it + 1) * P],
                                                    KP[:, h, nh * 512:(nh + 1) * 512], start=True, stop=True)
                        last.then_inc(S["scores"], 1)

                    def turn(u):
                        pe.wait_ge(S["p_ready"], u + 1)
                        for half in range(2):
                            if u >= 1:
                                pe.wait_ge(S["pt_odd" if half else "pt_even"], u)
                            for q in range(4):
                                j = half * 4 + q
                                last = nc.tensor.transpose(bank[4 + half][:, q * P:(q + 1) * P],
                                                           pbuf[:, u % 3, j * P:(j + 1) * P], identF[:, :])
                            last.then_inc(S["turned"], 1)

                    def weigh_values(g, quarter):
                        hg = g // NT
                        if quarter == 0:
                            pe.wait_ge(S["pt_even"], HG * g + HG)
                            pe.wait_ge(S["pt_odd"], HG * g + HG)
                            if g >= 2:
                                pe.wait_ge(S["ctx_ready"], g - 1)
                            if g >= NT + 2:
                                pe.wait_ge(S["x_done0"], g - NT - 1)
                        for j in (2 * quarter, 2 * quarter + 1):
                            for r in range(HG):
                                h = hg * HG + r
                                last = nc.tensor.matmul(bank[6 + g % 2][r * HD:(r + 1) * HD, 0:P],
                                                        V[:, j, h * HD:(h + 1) * HD], PT[:, g % 2, r, j, :],
                                                        start=(j == 0), stop=(j == NT - 1))
                        if quarter == 3:
                            last.then_inc(S["pv_done"], 1)
                            pe.wait_ge(S["rden_ready"], g + 1)
                            for r in range(HG):
                                last = nc.tensor.matmul(bank[6 + g % 2][r * HD:(r + 1) * HD, P:2 * P],
                                                        rden[:, HG * g + r:HG * g + r + 1].to_broadcast([P, HD]),
                                                        identF[:, :], start=True, stop=True)
                            last.then_inc(S["sums_spread"], 1)

                    def project_out(g):
                        it = g - NT
                        pe.wait_ge(S["ctx_ready"], g + 1)
                        for c in range(NG):
                            last = nc.tensor.matmul(bank[6 + g % 2][:, 256:256 + D], hT[:, c, it * P:(it + 1) * P],
                                                    wo[:, c, :], start=(c == 0), stop=(c == NG - 1))
                        last.then_inc(S["projected"], 1)

                    pe.wait_ge(S["v_ready"], NT)
                    scores(0)
                    for u in range(UNITS + 13):
                        if 2 <= u < UNITS + 2:
                            turn(u - 2)
                        if u + 1 < UNITS:
                            scores(u + 1)
                        if u >= 12 and (u - 12) % HG == 0 and NT <= (u - 12) // HG < GROUPS:
                            project_out((u - 12) // HG)
                        if u >= 6 and (u - 6) // HG < GROUPS:
                            weigh_values((u - 6) // HG, (u - 6) % HG)

                    ln_transposes(1, 0)
                    for t in range(NT):
                        if t >= 4:
                            pe.wait_ge(S["msg_parts"], t - 3)
                        project(bank[4 + t % 4][:, 0:D], 1, t, wmsg).then_inc(S["msg_psum"], 1)
                    pe.wait_ge(S["ones_set"], 1)
                    for j in range(NT):
                        if j >= 2:
                            pe.wait_ge(S["x_done1"], j - 1)
                        for i in range(NT):
                            if j == 0:
                                pe.wait_ge(S["msg_parts"], i + 1)
                            nc.tensor.matmul(bank[j % 2][:, 0:D + 1], adjN[:, i, j * P:(j + 1) * P], msgH[:, i, 0:D + 1],
                                             start=(i == 0), stop=False)
                            last = nc.tensor.matmul(bank[j % 2][:, 0:D], adjN[:, i, j * P:(j + 1) * P], msgL[:, i, :],
                                                    start=False, stop=(i == NT - 1))
                        last.then_inc(S["agg_psum"], 1)
                        project(bank[2 + j % 2][:, 0:D], 1, j, wupd).then_inc(S["upd_psum"], 1)
                        if j >= 2:
                            pe.wait_ge(S["adjT_ready"], j - 1)
                        for i in range(NT):
                            last = nc.tensor.transpose(bank[4 + j % 2].bitcast(f16)[:, i * P:(i + 1) * P],
                                                       adjN[:, i, j * P:(j + 1) * P], identH[:, :])
                        last.then_inc(S["adjT_psum"], 1)

                    pe.wait_ge(S["adjT_ready"], NT)
                    ln_transposes(2, 4)
                    pe.wait_ge(S["hT_ready2"], NT // 2)
                    pe.wait_ge(S["x_done1"], NT)
                    for nh in range(NH):
                        for c in range(DT):
                            last = nc.tensor.matmul(pair[0][0:2 * H, nh * 512:(nh + 1) * 512],
                                                    wa2[:, c, :, :].rearrange("p k h -> p (k h)"),
                                                    hT[:, c, nh * 512:(nh + 1) * 512], start=(c == 0), stop=(c == DT - 1))
                    last.then_inc(S["s_rows"], 1)
                    for t in range(NT):
                        for c in range(DT):
                            last = nc.tensor.matmul(bank[2][:, t * H:(t + 1) * H], hT[:, c, t * P:(t + 1) * P],
                                                    wa2[:, c, 1, :], start=(c == 0), stop=(c == DT - 1))
                    last.then_inc(S["s_cols"], 1)
                    for t in range(4):
                        project(bank[4 + t % 4][:, 0:D], 2, t, w2).then_inc(S["wh_psum"], 1)
                    pe.wait_ge(S["gmax_ready"], 1)
                    nc.tensor.matmul(bank[3][:, 0:H], gmax[0:2 * H, 0:1].to_broadcast([2 * H, P]),
                                     identF[0:2 * H, H:2 * H], start=True, stop=True)
                    nc.tensor.matmul(bank[3][:, H:2 * H], gmax[0:2 * H, 0:1].to_broadcast([2 * H, P]),
                                     both[0:2 * H, :], start=True, stop=True).then_inc(S["gmax_spread"], 1)
                    for t in range(4, NT):
                        pe.wait_ge(S["wh_scaled"], t - 3)
                        project(bank[4 + t % 4][:, 0:D], 2, t, w2).then_inc(S["wh_psum"], 1)
                    pe.wait_ge(S["kv_ready"], 1)
                    for t in range(NT):
                        for j in range(NT):
                            last = nc.tensor.matmul(bank[2][:, t * 2 * H:(t + 1) * 2 * H], adjT[:, j, t * P:(t + 1) * P],
                                                    kvHL[:, j, :], start=(j == 0), stop=(j == NT - 1))
                    last.then_inc(S["den_cols"], 1)
                    pe.wait_ge(S["den_cols_read"], 1)
                    pe.wait_ge(S["steep_row"], 1)
                    pe.wait_ge(S["wh_scaled"], NT)
                    pe.wait_ge(S["vm_lo"], 2)

                    def back(hg):
                        pe.wait_ge(S["num_copied"], hg + 1)
                        pe.wait_ge(S["den_copied"], hg + 1)
                        if hg == 1:
                            pe.wait_ge(S["hout_ready"], 1)
                        for t in range(NT):
                            last = nc.tensor.transpose(pair[0][:, t * P:(t + 1) * P], pbuf[:, 0, t * P:(t + 1) * P],
                                                       identF[:, :])
                        for t in range(NT):
                            last = nc.tensor.transpose(pair[1][:, t * P:(t + 1) * P], pbuf[:, 1, t * P:(t + 1) * P],
                                                       identF[:, :])
                        last.then_inc(S["back_turned"], 1)

                    for g in range(GROUPS):
                        hg, jt = g // NT, g % NT
                        num, dnm = pair[2 * hg], pair[2 * hg + 1]
                        first, final = jt == 0, jt == NT - 1
                        for nh in range(NH):
                            n5 = slice(nh * 512, (nh + 1) * 512)
                            for vm in (vmH, vmL):
                                nc.tensor.matmul(num[:, n5], vm[:, jt, hg * P:(hg + 1) * P], adjT[:, jt, n5],
                                                 start=first and vm is vmH, stop=False)
                        pe.wait_ge(S["r_ready"], HG * g + HG)
                        for nh in range(NH):
                            n5 = slice(nh * 512, (nh + 1) * 512)
                            for r in range(HG):
                                h = hg * HG + r
                                nc.tensor.matmul(num[r * HD:(r + 1) * HD, n5], V[:, jt, h * HD:(h + 1) * HD],
                                                 R[:, g % 2, r, n5], start=False, stop=final)
                            for r in range(HG):
                                h = hg * HG + r
                                last = nc.tensor.matmul(dnm[r * HD:(r + 1) * HD, n5],
                                                        v2[:, jt, h:h + 1].to_broadcast([P, HD]),
                                                        R[:, g % 2, r, n5], start=first, stop=final)
                        last.then_inc(S["group_done"], 1)
                        if g == NT + 3:
                            back(0)
                    back(1)

                    ln_transposes(3, 4)
                    pe.wait_ge(S["hT_ready3"], NT // 2)
                    for nh in range(NH):
                        for c in range(DT):
                            last = nc.tensor.matmul(pair[0][:, nh * 512:(nh + 1) * 512], wa3[:, c, 0:1].to_broadcast([P, P]),
                                                    hT[:, c, nh * 512:(nh + 1) * 512], start=(c == 0), stop=(c == DT - 1))
                    last.then_inc(S["a3_psum"], 1)
                    for t in range(NT):
                        for c in range(DT):
                            last = nc.tensor.matmul(bank[2][:, t:t + 1], hT[:, c, t * P:(t + 1) * P],
                                                    wa3[:, c, 1:2], start=(c == 0), stop=(c == DT - 1))
                    last.then_inc(S["f3_cols"], 1)
                    for t in range(NT):
                        if t >= 4:
                            pe.wait_ge(S["wh3_copied"], t - 3)
                        project(bank[4 + t % 4][:, 0:D], 3, t, w3).then_inc(S["wh3_psum"], 1)
                    pe.wait_ge(S["a3_ready"], 2)
                    pe.wait_ge(S["e3_ready"], 1)
                    for j in range(NT):
                        pe.wait_ge(S["g3_ready"], j + 1)
                        for i in range(NT):
                            last = nc.tensor.matmul(pair[i // 4][:, (i % 4) * D:(i % 4 + 1) * D], PU[:, j, i * P:(i + 1) * P],
                                                    V[:, j, :], start=(j == 0 and i % 2 == 0), stop=(j == NT - 1),
                                                    skip_group_check=True)
                            if j == NT - 1 and i % 2 == 1:
                                last.then_inc(S["out3_psum"], 1)

                @block.vector
                def _(dve):
                    steps = Steps(dve, S["dve_steps"])

                    for p in range(2 * DT * NH):
                        c, isk, nh = p // 4, (p // 2) % 2, p % 2
                        hi, lo = (KH, KL) if isk else (QH, QL)
                        ready = S["k_parts" if isk else "q_parts"]
                        n5 = slice(nh * 512, (nh + 1) * 512)
                        if p == 0:
                            dve.wait_ge(S["ln_psum0"], NT // 2)
                            dve.wait_ge(S["x_taken"], 1)
                        dve.wait_ge(S["qk_wide"], p + 1)
                        nc.vector.tensor_copy(hi[:, c, n5], whole[:, p % 4, :]).then_inc(ready, 1)
                        dve.wait_ge(ready, 4 * c + 2 * nh + 1)
                        nc.vector.tensor_tensor(lo[:, c, n5], whole[:, p % 4, :], hi[:, c, n5], ALU.subtract).then_inc(ready, 1)
                    for t in range(NT):
                        dve.wait_ge(S["v_psum"], t + 1)
                        nc.vector.tensor_tensor(V[:, t, :], bank[4 + t % 4][:, 0:D], bv_b[:, :], ALU.add).then_inc(S["v_ready"], 1)

                    def mask_and_max(u):
                        it = u // HG % NT
                        dve.wait_ge(S["scores"], u + 1)
                        if u >= 3:
                            dve.wait_ge(S["p_ready"], u - 2)
                        nc.vector.tensor_tensor_reduce(out=zbuf[:, u % 3, :], in0=pair[u % 2][:, :], in1=maskN[:, it, :],
                                                       scale=-1.0, scalar=3e38, op0=ALU.add, op1=ALU.min,
                                                       accum_out=nmax[:, u:u + 1]).then_inc(S["z_ready"], 1)

                    def turned_even(u):
                        g, r = u // HG, u % HG
                        dve.wait_ge(S["turned"], 2 * u + 1)
                        if g >= 2:
                            dve.wait_ge(S["pv_done"], g - 1)
                        nc.vector.tensor_copy(PT[:, g % 2, r, 0:4, :].rearrange("p t n -> p (t n)"), bank[4])\
                            .then_inc(S["pt_even"], 1)

                    def inverse_sums(g):
                        dve.wait_ge(S["p_ready"], HG * g + HG)
                        nc.vector.reciprocal(rden[:, HG * g:HG * g + HG], den[:, HG * g:HG * g + HG]).then_inc(S["rden_ready"], 1)

                    def context(g):
                        hg, it = g // NT, g % NT
                        dve.wait_ge(S["sums_copied"], g + 1)
                        if g == 0:
                            dve.wait_ge(S["v_psum"], NT)
                        nc.vector.tensor_tensor(hT[:, hg, it * P:(it + 1) * P], bank[6 + g % 2][:, 0:P], bcS[:, g % 2, :],
                                                ALU.mult).then_inc(S["ctx_ready"], 1)

                    def residual0(it):
                        dve.wait_ge(S["projected"], it + 1)
                        nc.vector.tensor_tensor(x[:, it, :], bank[6 + it % 2][:, 256:256 + D], x[:, it, :], ALU.add)\
                            .then_inc(S["x_done0"], 1)
                        if it == 0:
                            for h in range(H):
                                dve.wait_ge(S[f"head_pairs{h}"], 8 * 16)
                        dve.wait_ge(S["x_done0"], it + 1)
                        norm_stats(dve, steps, 1, it, x[:, it, :])

                    for u in range(UNITS + 13):
                        if u < UNITS:
                            mask_and_max(u)
                        if 2 <= u < UNITS + 2:
                            turned_even(u - 2)
                        if u >= 5 and (u - 5) % HG == 0 and (u - 5) // HG < GROUPS:
                            inverse_sums((u - 5) // HG)
                        if u >= 10 and (u - 10) % HG == 0 and (u - 10) // HG < GROUPS:
                            context((u - 10) // HG)
                        if u >= 13 and (u - 13) % HG == 0 and (u - 13) // HG >= NT:
                            residual0((u - 13) // HG - NT)
                        if u >= 15 and (u - 15) % HG == 0 and (u - 15) // HG >= NT:
                            it = (u - 15) // HG - NT
                            norm_apply(dve, 1, it, x[:, it, :])

                    dve.wait_ge(S["scores"], UNITS)
                    nc.vector.memset(msgH[:, :, D:D + 1], 1.0).then_inc(S["ones_set"], 1)
                    for t in range(NT):
                        dve.wait_ge(S["msg_hi"], t + 1)
                        nc.vector.tensor_tensor(msgL[:, t, :], bank[4 + t % 4][:, 0:D], msgH[:, t, 0:D], ALU.subtract)\
                            .then_inc(S["msg_parts"], 1)
                    for j in range(NT):
                        u_j = zbuf[:, j % 2, 0:D]
                        dve.wait_ge(S["agg_psum"], j + 1)
                        n = steps.did(nc.vector.tensor_scalar(deg[:, j, 0:1], bank[j % 2][:, D:D + 1], 1.0, None, ALU.max))
                        dve.wait_ge(S["upd_psum"], j + 1)
                        m = steps.did(nc.vector.tensor_tensor(u_j, bank[2 + j % 2][:, 0:D], b1_b[:, :], ALU.add))
                        steps.after(n)
                        n = steps.did(nc.vector.reciprocal(deg[:, j, 1:2], deg[:, j, 0:1]))
                        steps.after(n)
                        n = steps.did(nc.vector.scalar_tensor_tensor(u_j, bank[j % 2][:, 0:D], deg[:, j, 1:2], u_j,
                                                                     ALU.mult, ALU.add))
                        steps.after(n)
                        nc.vector.scalar_tensor_tensor(x[:, j, :], u_j, 0.0, x[:, j, :], ALU.max, ALU.add)\
                            .then_inc(S["x_done1"], 1)
                        dve.wait_ge(S["x_done1"], j + 1)
                        norm_stats(dve, steps, 2, j, x[:, j, :])
                        if j >= 1:
                            norm_apply(dve, 2, j - 1, x[:, j - 1, :])
                    norm_apply(dve, 2, NT - 1, x[:, NT - 1, :])

                    dve.wait_ge(S["s_rows"], 1)
                    n = steps.did(nc.vector.reduce_max(gmax[0:2 * H, 0:1], pair[0][0:2 * H, :], AX.X))
                    steps.after(n)
                    nc.vector.tensor_scalar(gmax[0:H, 1:2], gmax[0:H, 0:1], -STEEP, None, ALU.mult)\
                        .then_inc(S["gmax_ready"], 1)
                    dve.wait_ge(S["gmax_spread"], 1)
                    n = steps.did(nc.vector.tensor_copy(gmaxB[:, 0:H], bank[3][:, 0:H]))
                    n = steps.did(nc.vector.tensor_tensor(gmaxB[:, H:2 * H], bank[3][:, H:2 * H], edge_b[:, :], ALU.add))
                    steps.after(n)
                    m = steps.did(nc.vector.tensor_scalar(kexp[:, 2, :], gmaxB[:, H:2 * H], GMAX, None, ALU.min))
                    steps.after(m)
                    n = steps.did(nc.vector.tensor_tensor(kexp[:, 0, :], kexp[:, 2, :], gmaxB[:, H:2 * H], ALU.subtract))
                    dve.wait_ge(S["s_cols"], 1)
                    t2v = t2[:, 0, :].rearrange("p (t h) -> p t h", t=NT)
                    t2w = t2[:, 1, :].rearrange("p (t h) -> p t h", t=NT)
                    n = steps.did(nc.vector.tensor_tensor(t2v, bank[2][:, 0:NT * H].rearrange("p (t h) -> p t h", t=NT),
                                                          gmaxB[:, 0:H].unsqueeze(1).to_broadcast([P, NT, H]), ALU.subtract))
                    steps.after(n)
                    nc.vector.tensor_tensor(t2w, t2v, kexp[:, 2, :].unsqueeze(1).to_broadcast([P, NT, H]), ALU.add)\
                        .then_inc(S["t2_ready"], 1)
                    dve.wait_ge(S["bvexp_ready"], 2)
                    n = steps.did(nc.vector.tensor_tensor(kv[:, :, :], v2[:, :, :],
                                                          kexp[:, 1, :].unsqueeze(1).to_broadcast([P, NT, H]), ALU.mult))
                    nc.vector.tensor_scalar(kexp[:, 2, :], kexp[:, 1, :], -1.0, None, ALU.mult).then_inc(S["kappa_ready"], 1)
                    steps.after(n)
                    n = steps.did(nc.vector.tensor_copy(kvHL[:, :, 0:H], kv[:, :, :]))
                    steps.after(n)
                    nc.vector.tensor_tensor(kvHL[:, :, H:2 * H], kv[:, :, :], kvHL[:, :, 0:H], ALU.subtract)\
                        .then_inc(S["kv_ready"], 1)

                    def heads(ap):
                        return ap.rearrange("p (h d) -> p h d", h=H)

                    for t in range(NT):
                        dve.wait_ge(S["wh_psum"], t + 1)
                        nc.vector.tensor_tensor(heads(V[:, t, :]), heads(bank[4 + t % 4][:, 0:D]),
                                                v2[:, t, :].unsqueeze(2).to_broadcast([P, H, HD]), ALU.mult)\
                            .then_inc(S["wh_scaled"], 1)
                        if t % 4 == 3:
                            for q in range(t - 3, t + 1):
                                dve.wait_ge(S["wh_scaled"], q + 1)
                                last = nc.vector.tensor_tensor(heads(vm_wide[:, q, :]), heads(V[:, q, :]),
                                                               kexp[:, 1, :].unsqueeze(2).to_broadcast([P, H, HD]), ALU.mult)
                            last.then_inc(S["vm_wide"], 1)
                    dve.wait_ge(S["den_cols"], 1)
                    n = steps.did(nc.vector.tensor_copy(kv[:, :, :],
                                                        bank[2][:, 0:NT * 2 * H].rearrange("p (t k) -> p t k", t=NT)[:, :, 0:H]))
                    steps.after(n)
                    nc.vector.tensor_tensor(kv[:, :, :], kv[:, :, :],
                                            bank[2][:, 0:NT * 2 * H].rearrange("p (t k) -> p t k", t=NT)[:, :, H:2 * H],
                                            ALU.add).then_inc(S["den_cols_read"], 1)

                    def num_copy(hg):
                        dve.wait_ge(S["group_done"], NT * (hg + 1))
                        if hg == 0:
                            dve.wait_ge(S["vm_lo"], 2)
                        nc.vector.tensor_copy(pbuf[:, 0, :], pair[2 * hg][:, :]).then_inc(S["num_copied"], 1)

                    def hout(hg):
                        dve.wait_ge(S["back_turned"], hg + 1)
                        hs = slice(hg * HG, (hg + 1) * HG)
                        n = steps.did(nc.vector.tensor_tensor(
                            sums[:, :, hs], pair[1][:, :].rearrange("p (t h d) -> p t h d", t=NT, h=HG)[:, :, :, 0],
                            kv[:, :, hs], ALU.add))
                        steps.after(n)
                        n = steps.did(nc.vector.reciprocal(rsums[:, :, hs], sums[:, :, hs]))
                        steps.after(n)
                        for t in range(NT):
                            last = nc.vector.tensor_tensor(
                                xn[:, t, hg * P:(hg + 1) * P].rearrange("p (h d) -> p h d", h=HG),
                                pair[0][:, t * P:(t + 1) * P].rearrange("p (h d) -> p h d", h=HG),
                                rsums[:, t, hs].unsqueeze(2).to_broadcast([P, HG, HD]), ALU.mult)
                        last.then_inc(S["hout_ready"], 1)

                    for u in range(UNITS):
                        g, r = u // HG, u % HG
                        hg, jt = g // NT, g % NT
                        h = hg * HG + r
                        if u == 0:
                            dve.wait_ge(S["steep_out"], 16)
                        if jt == 0:
                            dve.wait_ge(S[f"steep_in{h}"], 16)
                        if u >= 3:
                            dve.wait_ge(S["r_ready"], u - 2)
                        nc.vector.tensor_tensor(zbuf[:, u % 3, :], steepT[:, h, :], adjT[:, jt, :], ALU.mult)\
                            .then_inc(S["masked_steep"], 1)
                        if u == HG * NT + 5:
                            num_copy(0)
                        if u == HG * (NT + 5) + 2:
                            hout(0)
                    dve.wait_ge(S["back_turned"], 1)
                    num_copy(1)
                    hout(1)
                    dve.wait_ge(S["hout_ready"], NG)

                    def y_of(t):
                        dve.wait_ge(S["ln_rstd4"], t + 1)
                        n = steps.did(nc.vector.scalar_tensor_tensor(xn[:, t, :], xn[:, t, :], meanvar[:, t, 0:1], gam_b[:, :],
                                                                     ALU.subtract, ALU.mult))
                        steps.after(n)
                        nc.vector.scalar_tensor_tensor(xn[:, t, :], xn[:, t, :], rstd[:, t:t + 1], bet_b[:, :],
                                                       ALU.mult, ALU.add).then_inc(S["y_ready"], 1)

                    for t in range(NT + 2):
                        if t < NT:
                            norm_stats(dve, steps, 4, t, xn[:, t, :])
                        if t >= 2:
                            y_of(t - 2)
                    dve.wait_ge(S["x_less_one"], 1)
                    for k in range(NT // 2):
                        y = xn[:, 2 * k:2 * k + 2, :].rearrange("p t d -> p (t d)")
                        xh = x[:, 2 * k:2 * k + 2, :].rearrange("p t d -> p (t d)")
                        dve.wait_ge(S["y_exp"], k + 1)
                        n = steps.did(nc.vector.scalar_tensor_tensor(xh, zbuf[:, k // 2, (k % 2) * 2 * D:(k % 2 + 1) * 2 * D],
                                                                     1.0, xh, ALU.min, ALU.add))
                        steps.after(n)
                        nc.vector.scalar_tensor_tensor(xh, y, 0.0, xh, ALU.max, ALU.add).then_inc(S["x_done2"], 1)
                        dve.wait_ge(S["x_done2"], k + 1)
                        for t in (2 * k, 2 * k + 1):
                            norm_stats(dve, steps, 3, t, x[:, t, :])
                        if k >= 1:
                            for t in (2 * k - 2, 2 * k - 1):
                                norm_apply(dve, 3, t, x[:, t, :])
                    for t in (NT - 2, NT - 1):
                        norm_apply(dve, 3, t, x[:, t, :])

                    dve.wait_ge(S["a3_psum"], 1)
                    n = steps.did(nc.vector.reduce_max(f3[:, 0:1], pair[0][:, :], AX.X))
                    steps.after(n)
                    n = steps.did(nc.vector.tensor_scalar(f3[:, 1:2], f3[:, 0:1], -STEEP, None, ALU.mult))
                    nc.vector.tensor_scalar(f3[:, 2:3], f3[:, 0:1], -SLOPE, None, ALU.mult).then_inc(S["f3_ready"], 1)
                    dve.wait_ge(S["f3_cols"], 1)
                    n = steps.did(nc.vector.tensor_scalar(e3[:, 0, :], bank[2][:, 0:NT], f3[:, 0:1], None, ALU.add))
                    steps.after(n)
                    nc.vector.tensor_scalar(e3[:, 1, :], e3[:, 0, :], 0.0, None, ALU.min)
                    nc.vector.tensor_scalar(e3[:, 2, :], e3[:, 0, :], 0.0, None, ALU.max).then_inc(S["e3_ready"], 1)
                    dve.wait_ge(S["a3_ready"], 1)
                    dve.wait_ge(S["b3_ready"], 2)
                    for j in range(NT):
                        n = steps.did(nc.vector.tensor_scalar(PU[:, j, :], zbuf[:, 0, :], b3[:, j:j + 1], k3[:, j:j + 1],
                                                              ALU.mult, ALU.max))
                        steps.after(n)
                        dve.wait_ge(S["mu_ready"], j + 1)
                        nc.vector.tensor_tensor_reduce(out=PU[:, j, :], in0=PU[:, j, :], in1=pbuf[:, j % 3, :], scale=1.0,
                                                       scalar=0.0, op0=ALU.mult, op1=ALU.add,
                                                       accum_out=den3[:, j:j + 1]).then_inc(S["pu_ready"], 1)
                        dve.wait_ge(S["pu_ready"], j + 1)
                        n = steps.did(nc.vector.reciprocal(rden3[:, j:j + 1], den3[:, j:j + 1]))
                        steps.after(n)
                        dve.wait_ge(S["wh3_copied"], j + 1)
                        nc.vector.tensor_scalar(V[:, j, :], V[:, j, :], rden3[:, j:j + 1], None, ALU.mult)\
                            .then_inc(S["g3_ready"], 1)
                        make_mask(dve, j)
                    dve.wait_ge(S["x_in"], 16)
                    dve.wait_ge(S["ln_psum3"], NT // 2)
                    for t in range(NT):
                        norm_stats(dve, steps, 0, t, x_next[:, t, :])
                        if t >= 1:
                            norm_apply(dve, 0, t - 1, x_next[:, t - 1, :])
                    norm_apply(dve, 0, NT - 1, x_next[:, NT - 1, :])
                    dve.wait_ge(S["x_less_one"], 2)
                    for k in range(NT // 2):
                        xh = x[:, 2 * k:2 * k + 2, :].rearrange("p t d -> p (t d)")
                        dve.wait_ge(S["o_exp"], k + 1)
                        n = steps.did(nc.vector.scalar_tensor_tensor(xh, zbuf[:, k // 2, (k % 2) * 512:(k % 2 + 1) * 512],
                                                                     1.0, xh, ALU.min, ALU.add))
                        steps.after(n)
                        nc.vector.scalar_tensor_tensor(xh, bank[k], 0.0, xh, ALU.max, ALU.add).then_inc(S["x_done3"], 1)

            clear_signals()


_WEIGHTS = ["L0_gnn_Wq", "L0_gnn_bq", "L0_gnn_Wk", "L0_gnn_bk", "L0_gnn_Wv", "L0_gnn_bv", "L0_gnn_Wo", "L0_gnn_bo",
            "L1_gnn_W_msg", "L1_gnn_W_upd", "L1_gnn_bias", "L2_gnn_W", "L2_gnn_a1", "L2_gnn_a2", "L2_gnn_edge_emb",
            "L2_gnn_ln_gamma", "L2_gnn_ln_beta", "L3_gnn_W", "L3_gnn_a"]


def kernel(**inputs):
    import concourse.bacc as _bacc
    from concourse.bass_utils import run_bass_kernel_spmd as _run

    nc = _bacc.Bacc("TRN2", target_bir_lowering=False, num_devices=1)
    arrays, args = {}, {}
    for name in ["x", "adj"] + _WEIGHTS:
        a = np.ascontiguousarray(inputs[name])
        arrays[f"in_{name}"] = a
        args[name] = nc.dram_tensor(f"in_{name}", a.shape, mybir.dt.from_np(a.dtype), kind="ExternalInput").ap()
    out = nc.dram_tensor("out", inputs["x"].shape, mybir.dt.float32, kind="ExternalOutput").ap()
    build_program(nc, args["x"], args["adj"], args, out)
    r = _run(nc, [arrays], core_ids=[0])
    return r.results[0]["out"]
```

```python
from contextlib import ExitStack

import numpy as np

import concourse.bass as bass
from concourse import mybir


class Steps:

    def __init__(self, engine, semaphore):
        self.engine, self.semaphore, self.count = engine, semaphore, 0

    def did(self, instruction):
        instruction.then_inc(self.semaphore, 1)
        self.count += 1
        return self.count

    def after(self, count):
        self.engine.wait_ge(self.semaphore, count)


def build_program(nc, x_dram, adj_dram, w, out_dram):
    f32, f16, bf16, i32 = mybir.dt.float32, mybir.dt.float16, mybir.dt.bfloat16, mybir.dt.int32
    ALU, ACT, AX = mybir.AluOpType, mybir.ActivationFunctionType, mybir.AxisListType

    B, N, D = x_dram.shape
    P = 128
    NT = N // P
    DT = D // P
    H = 8
    HD = D // H
    HG = 4
    NG = H // HG
    NH = N // 512
    QSCALE = float(1.0 / np.sqrt(HD))
    EPS = 1e-5
    MASKED = -1e30
    SLOPE = 0.2
    STEEP = 1.0 - SLOPE
    GMAX = 100.0
    UNITS = NT * H
    GROUPS = UNITS // HG
    AHEAD = 3

    ctx = ExitStack()
    with ctx:
        def sb(name, shape, dt):
            return ctx.enter_context(nc.sbuf_tensor(name, shape, dt))

        def sem(name):
            return ctx.enter_context(nc.semaphore(name))

        x = sb("x", [P, NT, D], f32)
        hT = sb("hT", [P, DT, N], f32)
        adjN = sb("adjN", [P, NT, N], f16)
        adjT = sb("adjT", [P, NT, N], f16)
        maskN = sb("maskN", [P, NT, N], bf16)
        headpairs = sb("headpairs", [P, 8192], f32)
        qkparts = sb("qkparts", [P, 4096], f32)
        wide = sb("wide", [P, 8192], f32)
        V = sb("V", [P, NT, D], f32)
        zbuf = sb("zbuf", [P, 3, N], f32)
        pbuf = sb("pbuf", [P, 3, N], f32)

        pairs16 = headpairs[:, :].bitcast(f16)
        QP = pairs16[:, 0:H * N].rearrange("p (h n) -> p h n", h=H)
        KP = pairs16[:, H * N:2 * H * N].rearrange("p (h n) -> p h n", h=H)
        MHW = 258
        msgH = pairs16[:, 0:NT * MHW].rearrange("p (t d) -> p t d", t=NT)
        msgL = pairs16[:, NT * MHW:NT * MHW + NT * D].rearrange("p (t d) -> p t d", t=NT)
        steepT = headpairs[:, :].rearrange("p (h n) -> p h n", h=H)
        parts16 = qkparts[:, :].bitcast(f16)
        QH, QL, KH, KL = (parts16[:, k * DT * N:(k + 1) * DT * N].rearrange("p (t n) -> p t n", t=DT)
                          for k in range(4))
        xn = qkparts[:, 0:NT * D].rearrange("p (t d) -> p t d", t=NT)
        vmH, vmL = (parts16[:, (2 + k) * NT * D:(3 + k) * NT * D].rearrange("p (t d) -> p t d", t=NT)
                    for k in range(2))
        x_next = qkparts[:, NT * D:2 * NT * D].rearrange("p (t d) -> p t d", t=NT)
        vm_wide = pbuf[:, 0:2, :].rearrange("p a (t d) -> p (a t) d", d=D)
        whole = pbuf[:, 0:2, :].rearrange("p a (t d) -> p (a t) d", d=512)
        adj_int = headpairs[:, :].bitcast(i32).rearrange("p (t n) -> p t n", t=NT)
        PT = wide[:, :].rearrange("p (b r t n) -> p b r t n", b=2, r=HG, t=NT)
        R = wide[:, :].rearrange("p (b r n) -> p b r n", b=2, r=HG)
        PU = wide[:, :].rearrange("p (t n) -> p t n", t=NT)

        wq, wk, wv, wo, wmsg, wupd, w2, w3 = (sb(n, [P, DT, D], f32) for n in
                                             ("wq", "wk", "wv", "wo", "wmsg", "wupd", "w2", "w3"))
        wa2 = sb("wa2", [P, DT, 2, H], f32)
        wa3 = sb("wa3", [P, DT, 2], f32)
        bv_b, bo_b, b1_b, gam_b, bet_b = (sb(n, [P, D], f32) for n in
                                          ("bv_b", "bo_b", "b1_b", "gam_b", "bet_b"))
        bq_c, bk_c = sb("bq_c", [P, DT], f32), sb("bk_c", [P, DT], f32)
        a2_b = sb("a2_b", [P, 2, HD], f32)
        edge_b = sb("edge_b", [P, H], f32)
        both = sb("both", [P, H], f32)
        ones_b = sb("ones_b", [P, D], f32)
        identF = sb("identF", [P, P], f32)
        identH = sb("identH", [P, P], f16)
        nhalf = sb("nhalf", [P, NT], f32)

        stats = sb("stats", [P, NT, 6], f32)
        meanvar = sb("meanvar", [P, NT, 2], f32)
        vareps = sb("vareps", [P, NT], f32)
        rstd = sb("rstd", [P, NT], f32)
        shift4 = sb("shift4", [P, NT], f32)
        nmax = sb("nmax", [P, UNITS], f32)
        den = sb("den", [P, UNITS], f32)
        rden = sb("rden", [P, UNITS], f32)
        bcS = sb("bcS", [P, 2, P], f32)
        deg = sb("deg", [P, NT, 2], f32)
        gmax = sb("gmax", [P, 2 + NH], f32)
        gmaxB = sb("gmaxB", [P, 2 * H], f32)
        kexp = sb("kexp", [P, 3, H], f32)
        t2 = sb("t2", [P, 2, NT * H], f32)
        b2 = sb("b2", [P, NT, H], f32)
        v2 = sb("v2", [P, NT, H], f32)
        kv = sb("kv", [P, NT, H], f32)
        kvHL = sb("kvHL", [P, NT, 2 * H], f16)
        sums, rsums = sb("sums", [P, NT, H], f32), sb("rsums", [P, NT, H], f32)
        e3 = sb("e3", [P, 3, NT], f32)
        b3, k3, den3, rden3 = (sb(n, [P, NT], f32) for n in ("b3", "k3", "den3", "rden3"))
        f3 = sb("f3", [P, 3 + NH], f32)

        pair = [ctx.enter_context(nc.psum_tensor(f"pair{i}", [P, 1024], f32)) for i in range(4)]
        bank = [pair[i // 2][:, (i % 2) * 512:(i % 2) * 512 + 512] for i in range(8)]

        steep_dram = nc.dram_tensor("steep_rows", (H, N), f32, kind="Internal").ap()

        w_in, w_small, ident_set, setup_steps = (sem(n) for n in
                                                 ("w_in", "w_small", "ident_set", "setup_steps"))
        with nc.Block() as block:
            @block.sync
            def _(sp):
                for name, dst in (("L0_gnn_Wq", wq), ("L0_gnn_Wk", wk), ("L0_gnn_Wv", wv),
                                  ("L0_gnn_Wo", wo), ("L1_gnn_W_msg", wmsg), ("L1_gnn_W_upd", wupd),
                                  ("L2_gnn_W", w2), ("L3_gnn_W", w3)):
                    sp.dma_start(dst[:, :, :], w[name].rearrange("(t p) n -> p t n", p=P)).then_inc(w_in, 16)
                sp.wait_ge(w_in, 8 * 16)

            @block.scalar
            def _(act):
                small = 0
                for dst, src in ((bv_b[:, :], w["L0_gnn_bv"].partition_broadcast(P)),
                                 (bo_b[:, :], w["L0_gnn_bo"].partition_broadcast(P)),
                                 (b1_b[:, :], w["L1_gnn_bias"].partition_broadcast(P)),
                                 (gam_b[:, :], w["L2_gnn_ln_gamma"].partition_broadcast(P)),
                                 (bet_b[:, :], w["L2_gnn_ln_beta"].partition_broadcast(P)),
                                 (a2_b[:, 0, :], w["L2_gnn_a1"].partition_broadcast(P)),
                                 (a2_b[:, 1, :], w["L2_gnn_a2"].partition_broadcast(P)),
                                 (zbuf[:, 0, 0:2 * D], w["L3_gnn_a"].rearrange("n o -> (n o)").partition_broadcast(P)),
                                 (edge_b[:, :], w["L2_gnn_edge_emb"][1, :].partition_broadcast(P)),
                                 (bq_c[:, :], w["L0_gnn_bq"].rearrange("(t p) -> p t", p=P)),
                                 (bk_c[:, :], w["L0_gnn_bk"].rearrange("(t p) -> p t", p=P))):
                    act.dma_start(dst, src, allow_slow_non_contiguous=True).then_inc(w_small, 16)
                    small += 16
                act.wait_ge(w_small, small)

            @block.gpsimd
            def _(pool):
                nc.gpsimd.memset(nhalf[:, :], -0.5)
                nc.gpsimd.memset(ones_b[:, :], 1.0)
                nc.gpsimd.memset(identF[:, :], 0.0).then_inc(ident_set, 1)
                nc.gpsimd.memset(identH[:, :], 0.0).then_inc(ident_set, 1)
                pool.wait_ge(ident_set, 2)
                for m in (identF, identH):
                    nc.gpsimd.affine_select(out=m[:, :], in_=m[:, :], compare_op=ALU.not_equal, fill=1.0,
                                            base=0, pattern=[[-1, P]], channel_multiplier=1).then_inc(ident_set, 1)
                pool.wait_ge(ident_set, 4)

            @block.vector
            def _(dve):
                steps = Steps(dve, setup_steps)
                dve.wait_ge(w_in, 8 * 16)
                dve.wait_ge(w_small, 11 * 16)
                nc.vector.tensor_scalar(bq_c[:, :], bq_c[:, :], QSCALE, None, ALU.mult)
                dve.wait_ge(ident_set, 4)
                nc.vector.tensor_tensor(both[:, :], identF[:, 0:H], identF[:, H:2 * H], ALU.add)
                for c in range(DT):
                    for k in range(2):
                        n = steps.did(nc.vector.tensor_tensor(
                            pbuf[:, c, k * D:(k + 1) * D].rearrange("p (h d) -> p h d", h=H),
                            w2[:, c, :].rearrange("p (h d) -> p h d", h=H),
                            a2_b[:, k, :].unsqueeze(1).to_broadcast([P, H, HD]), ALU.mult))
                        n = steps.did(nc.vector.tensor_tensor(
                            pbuf[:, c, (2 + k) * D:(3 + k) * D],
                            w3[:, c, :], zbuf[:, 0, k * D:(k + 1) * D], ALU.mult))
                steps.after(n)
                for c in range(DT):
                    for k in range(2):
                        nc.vector.tensor_reduce(wa2[:, c, k, :],
                                                pbuf[:, c, k * D:(k + 1) * D].rearrange("p (h d) -> p h d", h=H),
                                                AX.X, ALU.add)
                        n = steps.did(nc.vector.tensor_reduce(wa3[:, c, k:k + 1],
                                                              pbuf[:, c, (2 + k) * D:(3 + k) * D], AX.X, ALU.add))
                steps.after(n)

        names = ["x_in", "x_out", "x_taken", "q_parts", "k_parts", "v_ready", "qk_psum", "v_psum", "qk_wide",
                 "scores", "z_ready", "p_ready", "turned", "pt_even", "pt_odd", "pv_done", "rden_ready",
                 "sums_spread", "sums_copied", "ctx_ready", "projected",
                 "adj_cast", "mask_ready", "adjT_psum", "adjT_ready",
                 "msg_psum", "msg_hi", "msg_parts", "ones_set", "agg_psum", "upd_psum",
                 "s_rows", "s_cols", "wh_psum", "gmax_ready", "gmax_spread", "t2_ready", "steep_row", "steep_out",
                 "bvexp_ready", "kappa_ready", "kv_ready", "den_cols", "den_cols_read", "wh_scaled", "vm_wide_front", "vm_wide_back",
                 "vm_hi", "vm_lo", "masked_steep", "r_ready", "group_done", "num_copied", "den_copied",
                 "back_turned", "hout_ready", "shift4_ready", "z4_ready", "gamma_done", "y_ready", "y_exp", "x_less_one",
                 "a3_psum", "f3_cols", "wh3_psum", "f3_ready", "a3_ready", "e3_ready", "b3_ready",
                 "wh3_copied", "mu_ready", "pu_ready", "g3_ready", "out3_psum", "o_exp",
                 "x_done0", "x_done1", "x_done2", "x_done3", "dve_steps"]
        names += [f"adj_in{t}" for t in range(NT)] + [f"head_pairs{h}" for h in range(H)]
        names += [f"steep_in{h}" for h in range(H)]
        for L in range(5):
            names += [f"ln_var{L}", f"ln_rstd{L}", f"ln_x{L}", f"ln_psum{L}", f"hT_ready{L}"]
        S = {n: sem(n) for n in names}
        numbers = [S[n].num for n in names]
        assert numbers == list(range(numbers[0], numbers[0] + len(names)))

        def clear_signals():
            nc.gpsimd.sem_clear(range(numbers[0], numbers[0] + len(names)))
            nc.all_engine_barrier()

        def load_batch(sp, index):
            sp.dma_start(x_next[:, :, :], x_dram[index].rearrange("(t p) d -> p t d", p=P)).then_inc(S["x_in"], 16)
            for t in range(NT):
                sp.dma_start(adj_int[:, t, :], adj_dram[index, t * P:(t + 1) * P, :]).then_inc(S[f"adj_in{t}"], 16)

        def cast_adjacency(act, t):
            act.wait_ge(S[f"adj_in{t}"], 16)
            nc.scalar.activation(adjN[:, t, :], adj_int[:, t, :], ACT.Copy).then_inc(S["adj_cast"], 1)

        def make_mask(dve, t):
            dve.wait_ge(S["adj_cast"], t + 1)
            nc.vector.tensor_scalar(maskN[:, t, :], adjN[:, t, :], 0.0, MASKED, ALU.is_equal, ALU.mult)\
                .then_inc(S["mask_ready"], 1)

        def norm_stats(dve, steps, L, k, nodes, between=None):
            for t in (2 * k, 2 * k + 1):
                n = steps.did(nc.vector.bn_stats(stats[:, t, :], nodes[:, t, :]))
            if between:
                between()
            steps.after(n)
            for t in (2 * k, 2 * k + 1):
                n = steps.did(nc.vector.bn_aggr(meanvar[:, t, :], stats[:, t, :]))
            steps.after(n)
            nc.vector.tensor_scalar(vareps[:, 2 * k:2 * k + 2], meanvar[:, 2 * k:2 * k + 2, 1], EPS, None, ALU.add)\
                .then_inc(S[f"ln_var{L}"], 1)

        def norm_apply(dve, L, k, nodes):
            dve.wait_ge(S[f"ln_rstd{L}"], k + 1)
            for t in (2 * k, 2 * k + 1):
                nc.vector.tensor_scalar(xn[:, t, :], nodes[:, t, :], meanvar[:, t, 0:1], rstd[:, t:t + 1],
                                        ALU.subtract, ALU.mult).then_inc(S[f"ln_x{L}"], 1)

        def norm_root(pool, L, k):
            pool.wait_ge(S[f"ln_var{L}"], k + 1)
            nc.gpsimd.tensor_tensor(rstd[:, 2 * k:2 * k + 2], vareps[:, 2 * k:2 * k + 2], nhalf[:, 0:2], ALU.pow)\
                .then_inc(S[f"ln_rstd{L}"], 1)

        def norm_roots(pool, L):
            for k in range(NT // 2):
                norm_root(pool, L, k)

        with nc.Block() as block:
            @block.sync
            def _(sp):
                load_batch(sp, 0)

            @block.gpsimd
            def _(pool):
                norm_roots(pool, 0)

            @block.scalar
            def _(act):
                for t in range(NT):
                    cast_adjacency(act, t)

            @block.vector
            def _(dve):
                steps = Steps(dve, S["dve_steps"])
                dve.wait_ge(S["x_in"], 16)
                for k in range(NT // 2):
                    norm_stats(dve, steps, 0, k, x_next)
                for k in range(NT // 2):
                    norm_apply(dve, 0, k, x_next)
                for t in range(NT):
                    make_mask(dve, t)
        clear_signals()

        with nc.Fori(0, B) as b:
            with nc.Block() as block:
                @block.sync
                def _(sp):
                    for c in range(DT):
                        sp.wait_ge(S["q_parts"], 2 * (c + 1) * NH)
                        sp.wait_ge(S["k_parts"], 2 * (c + 1) * NH)
                        for r in range(HG):
                            h = c * HG + r
                            rows = slice(r * HD, (r + 1) * HD)
                            for quarter, (qs, ks) in enumerate(((QH, KH), (QH, KL), (QL, KH), (QL, KL))):
                                to = slice(quarter * HD, (quarter + 1) * HD)
                                sp.dma_start(QP[to, h, :], qs[rows, c, :]).then_inc(S[f"head_pairs{h}"], 16)
                                sp.dma_start(KP[to, h, :], ks[rows, c, :]).then_inc(S[f"head_pairs{h}"], 16)
                    sp.wait_ge(S["steep_row"], 1)
                    sp.dma_start(steep_dram[:, :], zbuf[0:H, 0, :]).then_inc(S["steep_out"], 16)
                    sp.wait_ge(S["steep_out"], 16)
                    sp.wait_ge(S["agg_psum"], NT)
                    for h in range(H):
                        sp.dma_start(steepT[:, h, :], steep_dram[h, :].partition_broadcast(P))\
                            .then_inc(S[f"steep_in{h}"], 16)
                    sp.wait_ge(S["masked_steep"], UNITS)
                    sp.wait_ge(S["group_done"], GROUPS)
                    load_batch(sp, (b + 1) % B)
                    out_r = out_dram[b].rearrange("(t p) d -> p t d", p=P)
                    for k in range(NT // 2):
                        sp.wait_ge(S["x_done3"], k + 1)
                        sp.dma_start(out_r[:, 2 * k:2 * k + 2, :], x[:, 2 * k:2 * k + 2, :]).then_inc(S["x_out"], 16)
                    sp.wait_ge(S["x_out"], NT // 2 * 16)

                @block.gpsimd
                def _(pool):
                    nc.gpsimd.tensor_tensor(x[:, :, :], x_next[:, :, :],
                                            bo_b[:, :].unsqueeze(1).to_broadcast([P, NT, D]), ALU.add)\
                        .then_inc(S["x_taken"], 1)
                    norm_roots(pool, 1)
                    norm_roots(pool, 2)
                    pool.wait_ge(S["ln_x2"], NT)
                    nc.gpsimd.tensor_tensor(x[:, :, :], x[:, :, :], ones_b[:, :].unsqueeze(1).to_broadcast([P, NT, D]),
                                            ALU.subtract).then_inc(S["x_less_one"], 1)
                    pool.wait_ge(S["bvexp_ready"], 2)
                    for t in range(NT // 2, NT):
                        pool.wait_ge(S["wh_scaled"], t // 2 + 1)
                        last = nc.gpsimd.tensor_tensor(vm_wide[:, t, :].rearrange("p (h d) -> p h d", h=H),
                                                       V[:, t, :].rearrange("p (h d) -> p h d", h=H),
                                                       kexp[:, 1, :].unsqueeze(2).to_broadcast([P, H, HD]), ALU.mult)
                        if t % 2 == 1:
                            last.then_inc(S["vm_wide_back"], 1)
                    for k in range(NT // 2):
                        two = slice(2 * k, 2 * k + 2)
                        pool.wait_ge(S["vm_hi"], k + 1)
                        nc.gpsimd.tensor_tensor(vmL[:, two, :], vm_wide[:, two, :], vmH[:, two, :], ALU.subtract)\
                            .then_inc(S["vm_lo"], 1)
                    def plus_beta(k):
                        two = slice(2 * k, 2 * k + 2)
                        pool.wait_ge(S["gamma_done"], k + 1)
                        nc.gpsimd.tensor_tensor(xn[:, two, :], xn[:, two, :],
                                                bet_b[:, :].unsqueeze(1).to_broadcast([P, 2, D]), ALU.add)\
                            .then_inc(S["y_ready"], 1)

                    for k in range(NT // 2 + 2):
                        if k < NT // 2:
                            norm_root(pool, 4, k)
                        if k >= 2:
                            plus_beta(k - 2)
                    norm_roots(pool, 3)
                    pool.wait_ge(S["ln_x3"], NT)
                    nc.gpsimd.tensor_tensor(x[:, :, :], x[:, :, :], ones_b[:, :].unsqueeze(1).to_broadcast([P, NT, D]),
                                            ALU.subtract).then_inc(S["x_less_one"], 1)
                    pool.wait_ge(S["a3_ready"], 2)
                    for j in range(NT):
                        if j >= 3:
                            pool.wait_ge(S["pu_ready"], j - 2)
                        nc.gpsimd.tensor_tensor(pbuf[:, j % 3, :], zbuf[:, 1, :], adjT[:, j, :], ALU.mult)\
                            .then_inc(S["mu_ready"], 1)
                        if j >= 2 and j % 2 == 0:
                            norm_root(pool, 0, j // 2 - 1)
                    norm_root(pool, 0, NT // 2 - 1)

                @block.scalar
                def _(act):
                    def hT_pair(L, k, b):
                        act.wait_ge(S[f"ln_psum{L}"], k + 1)
                        nc.scalar.activation(hT[:, :, 2 * k * P:(2 * k + 2) * P],
                                             bank[b].rearrange("p (c n) -> p c n", c=DT),
                                             ACT.Relu).then_inc(S[f"hT_ready{L}"], 1)

                    def hT_from_psum(L, first_bank):
                        for k in range(NT // 2):
                            hT_pair(L, k, first_bank + k)
                    hT_from_psum(0, 0)
                    for p in range(2 * DT * NH):
                        c, isk = p // 4, (p // 2) % 2
                        act.wait_ge(S["qk_psum"], p + 1)
                        if p >= 4:
                            act.wait_ge(S["k_parts" if isk else "q_parts"], 2 * (p % 2 + 1))
                        nc.scalar.activation(whole[:, p % 4, :], bank[4 + p % 4], ACT.Identity,
                                             bias=(bk_c if isk else bq_c)[:, c:c + 1],
                                             scale=1.0 if isk else QSCALE).then_inc(S["qk_wide"], 1)

                    def exp_unit(u):
                        act.wait_ge(S["z_ready"], u + 1)
                        if u >= 3:
                            act.wait_ge(S["turned"], 2 * (u - 3) + 2)
                        if u == 0:
                            act.wait_ge(S["q_parts"], 2 * DT * NH)
                            act.wait_ge(S["k_parts"], 2 * DT * NH)
                        nc.scalar.activation(pbuf[:, u % 3, :], zbuf[:, u % 3, :], ACT.Exp, bias=nmax[:, u:u + 1],
                                             scale=-1.0, accum_out=den[:, u:u + 1]).then_inc(S["p_ready"], 1)

                    def turned_odd(u):
                        g, r = u // HG, u % HG
                        act.wait_ge(S["turned"], 2 * u + 2)
                        if g >= 2:
                            act.wait_ge(S["pv_done"], g - 1)
                        nc.scalar.activation(PT[:, g % 2, r, 4:8, :].rearrange("p t n -> p (t n)"), bank[5],
                                             ACT.Copy).then_inc(S["pt_odd"], 1)

                    def spread_copy(g):
                        act.wait_ge(S["sums_spread"], g + 1)
                        if g >= 2:
                            act.wait_ge(S["ctx_ready"], g - 1)
                        nc.scalar.activation(bcS[:, g % 2, :], bank[6 + g % 2][:, P:2 * P], ACT.Copy)\
                            .then_inc(S["sums_copied"], 1)

                    for u in range(UNITS + 10):
                        if 2 <= u < UNITS + 2:
                            turned_odd(u - 2)
                        if u < UNITS:
                            exp_unit(u)
                        if u >= 10 and (u - 10) % HG == 0:
                            spread_copy((u - 10) // HG)

                    hT_from_psum(1, 0)
                    for k in range(NT // 2):
                        act.wait_ge(S["msg_psum"], k + 1)
                        nc.scalar.activation(msgH[:, 2 * k:2 * k + 2, 0:D], bank[4 + k].rearrange("p (t d) -> p t d", t=2),
                                             ACT.Copy).then_inc(S["msg_hi"], 1)
                    for a in range(NT):
                        if a in (NT - 3, NT - 1):
                            hT_pair(2, (a - NT + 3) // 2, 4 + (a - NT + 3) // 2)
                        act.wait_ge(S["adjT_psum"], a + 1)
                        nc.scalar.activation(adjT[:, a, :], bank[6 + a % 2].bitcast(f16), ACT.Copy)\
                            .then_inc(S["adjT_ready"], 1)

                    hT_pair(2, 2, 6)
                    hT_pair(2, 3, 7)
                    act.wait_ge(S["gmax_ready"], 1)
                    nc.scalar.activation(zbuf[0:H, 0, :], pair[0][0:H, :], ACT.Exp, bias=gmax[0:H, 1:2],
                                         scale=STEEP).then_inc(S["steep_row"], 1)
                    act.wait_ge(S["t2_ready"], 1)
                    nc.scalar.activation(v2[:, :, :].rearrange("p t h -> p (t h)"), t2[:, 0, :], ACT.Exp, scale=SLOPE)\
                        .then_inc(S["bvexp_ready"], 1)
                    nc.scalar.activation(kexp[:, 1, :], kexp[:, 0, :], ACT.Exp, scale=STEEP).then_inc(S["bvexp_ready"], 1)
                    nc.scalar.activation(b2[:, :, :].rearrange("p t h -> p (t h)"), t2[:, 1, :], ACT.Exp, scale=STEEP)\
                        .then_inc(S["bvexp_ready"], 1)
                    for k in range(NT // 2):
                        two = slice(2 * k, 2 * k + 2)
                        if k < NT // 4:
                            act.wait_ge(S["vm_wide_front"], 2 * k + 2)
                        else:
                            act.wait_ge(S["vm_wide_back"], k - NT // 4 + 1)
                        nc.scalar.activation(vmH[:, two, :], vm_wide[:, two, :], ACT.Copy).then_inc(S["vm_hi"], 1)
                    act.wait_ge(S["kappa_ready"], 1)
                    act.wait_ge(S["bvexp_ready"], 3)

                    def den_copy(hg):
                        act.wait_ge(S["group_done"], NT * (hg + 1))
                        nc.scalar.activation(pbuf[:, 1, :], pair[2 * hg + 1][:, :], ACT.Copy).then_inc(S["den_copied"], 1)

                    for u in range(UNITS):
                        g, r = u // HG, u % HG
                        hg, jt = g // NT, g % NT
                        h = hg * HG + r
                        act.wait_ge(S["masked_steep"], u + 1)
                        if g >= 2:
                            act.wait_ge(S["group_done"], g - 1)
                        nc.scalar.activation(R[:, g % 2, r, :], zbuf[:, u % 3, :], ACT.Relu, bias=kexp[:, 2, h:h + 1],
                                             scale=b2[:, jt, h:h + 1]).then_inc(S["r_ready"], 1)

                        if u == HG * NT + 5:
                            den_copy(0)
                    act.wait_ge(S["hout_ready"], 1)
                    den_copy(1)
                    def standardise(k):
                        act.wait_ge(S["shift4_ready"], k + 1)
                        for t in (2 * k, 2 * k + 1):
                            nc.scalar.activation(xn[:, t, :], xn[:, t, :], ACT.Identity, bias=shift4[:, t:t + 1],
                                                 scale=rstd[:, t:t + 1]).then_inc(S["z4_ready"], 1)

                    standardise(0)
                    standardise(1)
                    for k in range(NT // 2):
                        if k + 2 < NT // 2:
                            standardise(k + 2)
                        act.wait_ge(S["y_ready"], k + 1)
                        nc.scalar.activation(zbuf[:, k // 2, (k % 2) * 2 * D:(k % 2 + 1) * 2 * D],
                                             xn[:, 2 * k:2 * k + 2, :].rearrange("p t d -> p (t d)"), ACT.Exp)\
                            .then_inc(S["y_exp"], 1)

                    hT_from_psum(3, 4)
                    act.wait_ge(S["f3_ready"], 1)
                    nc.scalar.activation(zbuf[:, 0, :], pair[0][:, :], ACT.Exp, bias=f3[:, 1:2], scale=STEEP)\
                        .then_inc(S["a3_ready"], 1)
                    nc.scalar.activation(zbuf[:, 1, :], pair[0][:, :], ACT.Exp, bias=f3[:, 2:3], scale=SLOPE)\
                        .then_inc(S["a3_ready"], 1)
                    act.wait_ge(S["e3_ready"], 1)
                    nc.scalar.activation(b3[:, :], e3[:, 1, :], ACT.Exp, scale=STEEP).then_inc(S["b3_ready"], 1)
                    nc.scalar.activation(k3[:, :], e3[:, 2, :], ACT.Exp, scale=-STEEP).then_inc(S["b3_ready"], 1)
                    for k in range(NT // 2):
                        act.wait_ge(S["wh3_psum"], k + 1)
                        nc.scalar.activation(V[:, 2 * k:2 * k + 2, :].rearrange("p t d -> p (t d)"), bank[4 + k], ACT.Copy)\
                            .then_inc(S["wh3_copied"], 1)
                    for t in range(NT):
                        cast_adjacency(act, t)
                    for k in range(NT // 2):
                        act.wait_ge(S["out3_psum"], k + 1)
                        nc.scalar.activation(zbuf[:, k // 2, (k % 2) * 512:(k % 2 + 1) * 512], bank[k], ACT.Exp)\
                            .then_inc(S["o_exp"], 1)

                @block.tensor
                def _(pe):
                    def ln_pair(L, k, b):
                        for t in (2 * k, 2 * k + 1):
                            if L > 0:
                                pe.wait_ge(S[f"ln_x{L}"], t + 1)
                            for c in range(DT):
                                last = nc.tensor.transpose(
                                    bank[b][:, c * 256 + (t % 2) * P:c * 256 + (t % 2 + 1) * P],
                                    xn[:, t, c * P:(c + 1) * P], identF[:, :])
                        last.then_inc(S[f"ln_psum{L}"], 1)

                    def project(out, L, t, weights):
                        pe.wait_ge(S[f"hT_ready{L}"], t // 2 + 1)
                        for c in range(DT):
                            last = nc.tensor.matmul(out, hT[:, c, t * P:(t + 1) * P], weights[:, c, :],
                                                    start=(c == 0), stop=(c == DT - 1))
                        return last

                    def project_pair(L, k, weights, done):
                        for t in (2 * k, 2 * k + 1):
                            last = project(bank[4 + k][:, (t % 2) * D:(t % 2 + 1) * D], L, t, weights)
                        last.then_inc(done, 1)
                    for k in range(NT // 2):
                        ln_pair(0, k, k)
                    for p in range(2 * DT * NH):
                        c, isk, nh = p // 4, (p // 2) % 2, p % 2
                        pe.wait_ge(S["hT_ready0"], 2 * (nh + 1))
                        if p >= 4:
                            pe.wait_ge(S["qk_wide"], p - 3)
                        for k in range(DT):
                            last = nc.tensor.matmul(bank[4 + p % 4], (wk if isk else wq)[:, k, c * P:(c + 1) * P],
                                                    hT[:, k, nh * 512:(nh + 1) * 512], start=(k == 0), stop=(k == DT - 1))
                        last.then_inc(S["qk_psum"], 1)
                    for k in range(NT // 2):
                        pe.wait_ge(S["qk_wide"], 2 * DT * NH - 3 + k)
                        project_pair(0, k, wv, S["v_psum"])

                    def scores(u):
                        h, it = u // (HG * NT) * HG + u % HG, u // HG % NT
                        if it == 0:
                            pe.wait_ge(S[f"head_pairs{h}"], 8 * 16)
                        if u >= 2:
                            pe.wait_ge(S["z_ready"], u - 1)
                        for nh in range(NH):
                            last = nc.tensor.matmul(pair[u % 2][:, nh * 512:(nh + 1) * 512], QP[:, h, it * P:(it + 1) * P],
                                                    KP[:, h, nh * 512:(nh + 1) * 512], start=True, stop=True)
                        last.then_inc(S["scores"], 1)

                    def turn(u):
                        pe.wait_ge(S["p_ready"], u + 1)
                        for half in range(2):
                            if u >= 1:
                                pe.wait_ge(S["pt_odd" if half else "pt_even"], u)
                            for q in range(4):
                                j = half * 4 + q
                                last = nc.tensor.transpose(bank[4 + half][:, q * P:(q + 1) * P],
                                                           pbuf[:, u % 3, j * P:(j + 1) * P], identF[:, :])
                            last.then_inc(S["turned"], 1)

                    def weigh_values(g, quarter):
                        hg = g // NT
                        if quarter == 0:
                            pe.wait_ge(S["pt_even"], HG * g + HG)
                            pe.wait_ge(S["pt_odd"], HG * g + HG)
                            if g >= 2:
                                pe.wait_ge(S["ctx_ready"], g - 1)
                            if g >= NT + 2:
                                pe.wait_ge(S["x_done0"], g - NT - 1)
                        for j in (2 * quarter, 2 * quarter + 1):
                            for r in range(HG):
                                h = hg * HG + r
                                last = nc.tensor.matmul(bank[6 + g % 2][r * HD:(r + 1) * HD, 0:P],
                                                        V[:, j, h * HD:(h + 1) * HD], PT[:, g % 2, r, j, :],
                                                        start=(j == 0), stop=(j == NT - 1))
                        if quarter == 3:
                            last.then_inc(S["pv_done"], 1)
                            pe.wait_ge(S["rden_ready"], g + 1)
                            for r in range(HG):
                                last = nc.tensor.matmul(bank[6 + g % 2][r * HD:(r + 1) * HD, P:2 * P],
                                                        rden[:, HG * g + r:HG * g + r + 1].to_broadcast([P, HD]),
                                                        identF[:, :], start=True, stop=True)
                            last.then_inc(S["sums_spread"], 1)

                    def project_out(g):
                        it = g - NT
                        pe.wait_ge(S["ctx_ready"], g + 1)
                        for c in range(NG):
                            last = nc.tensor.matmul(bank[6 + g % 2][:, 256:256 + D], hT[:, c, it * P:(it + 1) * P],
                                                    wo[:, c, :], start=(c == 0), stop=(c == NG - 1))
                        last.then_inc(S["projected"], 1)

                    pe.wait_ge(S["v_ready"], NT // 2)
                    scores(0)
                    for u in range(UNITS + 13):
                        if 2 <= u < UNITS + 2:
                            turn(u - 2)
                        if u + 1 < UNITS:
                            scores(u + 1)
                        if u >= 12 and (u - 12) % HG == 0 and NT <= (u - 12) // HG < GROUPS:
                            project_out((u - 12) // HG)
                        if u >= 6 and (u - 6) // HG < GROUPS:
                            weigh_values((u - 6) // HG, (u - 6) % HG)

                    for k in range(NT // 2 + 1):
                        if k < NT // 2:
                            ln_pair(1, k, k)
                        if k >= 1:
                            project_pair(1, k - 1, wmsg, S["msg_psum"])
                    pe.wait_ge(S["ones_set"], 1)
                    for j in range(NT):
                        if j in (NT - 3, NT - 1):
                            ln_pair(2, (j - NT + 3) // 2, 4 + (j - NT + 3) // 2)
                        if j >= 2:
                            pe.wait_ge(S["x_done1"], j - 1)
                        for i in range(NT):
                            if j == 0:
                                pe.wait_ge(S["msg_parts"], i // 2 + 1)
                            nc.tensor.matmul(bank[j % 2][:, 0:D + 1], adjN[:, i, j * P:(j + 1) * P], msgH[:, i, 0:D + 1],
                                             start=(i == 0), stop=False)
                            last = nc.tensor.matmul(bank[j % 2][:, 0:D], adjN[:, i, j * P:(j + 1) * P], msgL[:, i, :],
                                                    start=False, stop=(i == NT - 1))
                        last.then_inc(S["agg_psum"], 1)
                        project(bank[2 + j % 2][:, 0:D], 1, j, wupd).then_inc(S["upd_psum"], 1)
                        if j >= 2:
                            pe.wait_ge(S["adjT_ready"], j - 1)
                        for i in range(NT):
                            last = nc.tensor.transpose(bank[6 + j % 2].bitcast(f16)[:, i * P:(i + 1) * P],
                                                       adjN[:, i, j * P:(j + 1) * P], identH[:, :])
                        last.then_inc(S["adjT_psum"], 1)


                    def score_rows(nh):
                        for c in range(DT):
                            last = nc.tensor.matmul(pair[0][0:2 * H, nh * 512:(nh + 1) * 512],
                                                    wa2[:, c, :, :].rearrange("p k h -> p (k h)"),
                                                    hT[:, c, nh * 512:(nh + 1) * 512], start=(c == 0), stop=(c == DT - 1))
                        last.then_inc(S["s_rows"], 1)

                    def score_cols(t):
                        for c in range(DT):
                            last = nc.tensor.matmul(bank[2][:, t * H:(t + 1) * H], hT[:, c, t * P:(t + 1) * P],
                                                    wa2[:, c, 1, :], start=(c == 0), stop=(c == DT - 1))
                        return last

                    pe.wait_ge(S["hT_ready2"], NT // 4)
                    pe.wait_ge(S["x_done1"], NT - 1)
                    score_rows(0)
                    for t in range(NT // 2):
                        score_cols(t)
                    pe.wait_ge(S["adjT_ready"], NT - 1)
                    ln_pair(2, 2, 6)
                    pe.wait_ge(S["adjT_ready"], NT)
                    ln_pair(2, 3, 7)
                    pe.wait_ge(S["hT_ready2"], NT // 2 - 1)
                    for t in range(NT // 2, NT - 2):
                        score_cols(t)
                    pe.wait_ge(S["x_done1"], NT)
                    pe.wait_ge(S["hT_ready2"], NT // 2)
                    score_rows(1)
                    for t in range(NT - 2, NT):
                        last = score_cols(t)
                    last.then_inc(S["s_cols"], 1)
                    pe.wait_ge(S["gmax_ready"], 1)
                    nc.tensor.matmul(bank[3][:, 0:H], gmax[0:2 * H, 0:1].to_broadcast([2 * H, P]),
                                     identF[0:2 * H, H:2 * H], start=True, stop=True)
                    nc.tensor.matmul(bank[3][:, H:2 * H], gmax[0:2 * H, 0:1].to_broadcast([2 * H, P]),
                                     both[0:2 * H, :], start=True, stop=True).then_inc(S["gmax_spread"], 1)
                    for k in range(NT // 2):
                        project_pair(2, k, w2, S["wh_psum"])
                    pe.wait_ge(S["kv_ready"], 1)
                    pe.wait_ge(S["wh_scaled"], NT // 2)
                    for t in range(NT):
                        for j in range(NT):
                            last = nc.tensor.matmul(bank[6][:, t * 2 * H:(t + 1) * 2 * H], adjT[:, j, t * P:(t + 1) * P],
                                                    kvHL[:, j, :], start=(j == 0), stop=(j == NT - 1))
                    last.then_inc(S["den_cols"], 1)
                    pe.wait_ge(S["steep_row"], 1)
                    pe.wait_ge(S["t2_ready"], 1)

                    def back(hg):
                        pe.wait_ge(S["num_copied"], hg + 1)
                        pe.wait_ge(S["den_copied"], hg + 1)
                        if hg == 1:
                            pe.wait_ge(S["hout_ready"], 1)
                        for t in range(NT):
                            last = nc.tensor.transpose(pair[0][:, t * P:(t + 1) * P], pbuf[:, 0, t * P:(t + 1) * P],
                                                       identF[:, :])
                        for t in range(NT):
                            last = nc.tensor.transpose(pair[1][:, t * P:(t + 1) * P], pbuf[:, 1, t * P:(t + 1) * P],
                                                       identF[:, :])
                        last.then_inc(S["back_turned"], 1)

                    def steep_share(g):
                        hg, jt = g // NT, g % NT
                        num, dnm = pair[2 * hg], pair[2 * hg + 1]
                        pe.wait_ge(S["r_ready"], HG * g + HG)
                        if g == NT:
                            pe.wait_ge(S["den_cols_read"], 1)
                        for nh in range(NH):
                            n5 = slice(nh * 512, (nh + 1) * 512)
                            for r in range(HG):
                                h = hg * HG + r
                                nc.tensor.matmul(num[r * HD:(r + 1) * HD, n5], V[:, jt, h * HD:(h + 1) * HD],
                                                 R[:, g % 2, r, n5], start=False, stop=(jt == NT - 1))
                            for r in range(HG):
                                h = hg * HG + r
                                last = nc.tensor.matmul(dnm[r * HD:(r + 1) * HD, n5],
                                                        v2[:, jt, h:h + 1].to_broadcast([P, HD]),
                                                        R[:, g % 2, r, n5], start=(jt == 0), stop=(jt == NT - 1))
                        last.then_inc(S["group_done"], 1)

                    def edge_share(g):
                        hg, jt = g // NT, g % NT
                        if hg == 0:
                            pe.wait_ge(S["vm_lo"], jt // 2 + 1)
                        for nh in range(NH):
                            n5 = slice(nh * 512, (nh + 1) * 512)
                            for vm in (vmH, vmL):
                                nc.tensor.matmul(pair[2 * hg][:, n5], vm[:, jt, hg * P:(hg + 1) * P], adjT[:, jt, n5],
                                                 start=(jt == 0 and vm is vmH), stop=False)

                    for g in range(AHEAD):
                        edge_share(g)
                    for g in range(GROUPS):
                        steep_share(g)
                        if g + AHEAD < GROUPS:
                            edge_share(g + AHEAD)
                        if g == NT + 3:
                            back(0)
                    back(1)

                    def first_rows(nh):
                        for c in range(DT):
                            last = nc.tensor.matmul(pair[0][:, nh * 512:(nh + 1) * 512], wa3[:, c, 0:1].to_broadcast([P, P]),
                                                    hT[:, c, nh * 512:(nh + 1) * 512], start=(c == 0), stop=(c == DT - 1))
                        last.then_inc(S["a3_psum"], 1)

                    def second_cols(t):
                        for c in range(DT):
                            last = nc.tensor.matmul(bank[2][:, t:t + 1], hT[:, c, t * P:(t + 1) * P],
                                                    wa3[:, c, 1:2], start=(c == 0), stop=(c == DT - 1))
                        return last

                    for k in range(NT // 2):
                        ln_pair(3, k, 4 + k)
                        if k == 1:
                            project_pair(3, 0, w3, S["wh3_psum"])
                        if k == 2:
                            pe.wait_ge(S["hT_ready3"], NT // 4)
                            first_rows(0)
                        if k == 3:
                            pe.wait_ge(S["hT_ready3"], NT // 2)
                            first_rows(1)
                    for t in range(NT):
                        last = second_cols(t)
                    last.then_inc(S["f3_cols"], 1)
                    for k in range(1, NT // 2):
                        project_pair(3, k, w3, S["wh3_psum"])
                    pe.wait_ge(S["a3_ready"], 2)
                    pe.wait_ge(S["e3_ready"], 1)
                    for j in range(NT):
                        pe.wait_ge(S["g3_ready"], j + 1)
                        for i in range(NT):
                            last = nc.tensor.matmul(pair[i // 4][:, (i % 4) * D:(i % 4 + 1) * D], PU[:, j, i * P:(i + 1) * P],
                                                    V[:, j, :], start=(j == 0 and i % 2 == 0), stop=(j == NT - 1),
                                                    skip_group_check=True)
                            if j == NT - 1 and i % 2 == 1:
                                last.then_inc(S["out3_psum"], 1)

                @block.vector
                def _(dve):
                    steps = Steps(dve, S["dve_steps"])

                    for p in range(2 * DT * NH):
                        c, isk, nh = p // 4, (p // 2) % 2, p % 2
                        hi, lo = (KH, KL) if isk else (QH, QL)
                        ready = S["k_parts" if isk else "q_parts"]
                        n5 = slice(nh * 512, (nh + 1) * 512)
                        if p == 0:
                            dve.wait_ge(S["ln_psum0"], NT // 2)
                            dve.wait_ge(S["x_taken"], 1)
                        dve.wait_ge(S["qk_wide"], p + 1)
                        nc.vector.tensor_copy(hi[:, c, n5], whole[:, p % 4, :]).then_inc(ready, 1)
                        dve.wait_ge(ready, 4 * c + 2 * nh + 1)
                        nc.vector.tensor_tensor(lo[:, c, n5], whole[:, p % 4, :], hi[:, c, n5], ALU.subtract).then_inc(ready, 1)
                    for k in range(NT // 2):
                        dve.wait_ge(S["v_psum"], k + 1)
                        nc.vector.tensor_tensor(V[:, 2 * k:2 * k + 2, :], bank[4 + k].rearrange("p (t d) -> p t d", t=2),
                                                bv_b[:, :].unsqueeze(1).to_broadcast([P, 2, D]), ALU.add)\
                            .then_inc(S["v_ready"], 1)

                    def mask_and_max(u):
                        it = u // HG % NT
                        dve.wait_ge(S["scores"], u + 1)
                        if u >= 3:
                            dve.wait_ge(S["p_ready"], u - 2)
                        nc.vector.tensor_tensor_reduce(out=zbuf[:, u % 3, :], in0=pair[u % 2][:, :], in1=maskN[:, it, :],
                                                       scale=-1.0, scalar=3e38, op0=ALU.add, op1=ALU.min,
                                                       accum_out=nmax[:, u:u + 1]).then_inc(S["z_ready"], 1)

                    def turned_even(u):
                        g, r = u // HG, u % HG
                        dve.wait_ge(S["turned"], 2 * u + 1)
                        if g >= 2:
                            dve.wait_ge(S["pv_done"], g - 1)
                        nc.vector.tensor_copy(PT[:, g % 2, r, 0:4, :].rearrange("p t n -> p (t n)"), bank[4])\
                            .then_inc(S["pt_even"], 1)

                    def inverse_sums(g):
                        dve.wait_ge(S["p_ready"], HG * g + HG)
                        nc.vector.reciprocal(rden[:, HG * g:HG * g + HG], den[:, HG * g:HG * g + HG]).then_inc(S["rden_ready"], 1)

                    def context(g):
                        hg, it = g // NT, g % NT
                        dve.wait_ge(S["sums_copied"], g + 1)
                        if g == 0:
                            dve.wait_ge(S["v_psum"], NT // 2)
                        nc.vector.tensor_tensor(hT[:, hg, it * P:(it + 1) * P], bank[6 + g % 2][:, 0:P], bcS[:, g % 2, :],
                                                ALU.mult).then_inc(S["ctx_ready"], 1)

                    def residual0(it):
                        dve.wait_ge(S["projected"], it + 1)
                        nc.vector.tensor_tensor(x[:, it, :], bank[6 + it % 2][:, 256:256 + D], x[:, it, :], ALU.add)\
                            .then_inc(S["x_done0"], 1)
                        if it == 0:
                            for h in range(H):
                                dve.wait_ge(S[f"head_pairs{h}"], 8 * 16)
                        dve.wait_ge(S["x_done0"], it + 1)
                        if it % 2 == 1:
                            norm_stats(dve, steps, 1, it // 2, x)

                    for u in range(UNITS + 13):
                        if u < UNITS:
                            mask_and_max(u)
                        if 2 <= u < UNITS + 2:
                            turned_even(u - 2)
                        if u >= 5 and (u - 5) % HG == 0 and (u - 5) // HG < GROUPS:
                            inverse_sums((u - 5) // HG)
                        if u >= 10 and (u - 10) % HG == 0 and (u - 10) // HG < GROUPS:
                            context((u - 10) // HG)
                        if u >= 13 and (u - 13) % HG == 0 and (u - 13) // HG >= NT:
                            residual0((u - 13) // HG - NT)
                        if u >= 15 and (u - 15) % HG == 0 and (u - 15) // HG >= NT:
                            it = (u - 15) // HG - NT
                            if it % 2 == 1:
                                norm_apply(dve, 1, it // 2, x)

                    dve.wait_ge(S["scores"], UNITS)
                    nc.vector.memset(msgH[:, :, D:D + 1], 1.0).then_inc(S["ones_set"], 1)
                    for k in range(NT // 2):
                        dve.wait_ge(S["msg_hi"], k + 1)
                        nc.vector.tensor_tensor(msgL[:, 2 * k:2 * k + 2, :], bank[4 + k].rearrange("p (t d) -> p t d", t=2),
                                                msgH[:, 2 * k:2 * k + 2, 0:D], ALU.subtract).then_inc(S["msg_parts"], 1)
                    for j in range(NT):
                        u_j = zbuf[:, j % 2, 0:D]
                        dve.wait_ge(S["agg_psum"], j + 1)
                        n = steps.did(nc.vector.tensor_scalar(deg[:, j, 0:1], bank[j % 2][:, D:D + 1], 1.0, None, ALU.max))
                        dve.wait_ge(S["upd_psum"], j + 1)
                        m = steps.did(nc.vector.tensor_tensor(u_j, bank[2 + j % 2][:, 0:D], b1_b[:, :], ALU.add))
                        steps.after(n)
                        n = steps.did(nc.vector.reciprocal(deg[:, j, 1:2], deg[:, j, 0:1]))
                        steps.after(n)
                        n = steps.did(nc.vector.scalar_tensor_tensor(u_j, bank[j % 2][:, 0:D], deg[:, j, 1:2], u_j,
                                                                     ALU.mult, ALU.add))
                        steps.after(n)
                        nc.vector.scalar_tensor_tensor(x[:, j, :], u_j, 0.0, x[:, j, :], ALU.max, ALU.add)\
                            .then_inc(S["x_done1"], 1)
                        dve.wait_ge(S["x_done1"], j + 1)
                        if j % 2 == 1:
                            norm_stats(dve, steps, 2, j // 2, x)
                        elif j >= 2:
                            norm_apply(dve, 2, j // 2 - 1, x)
                    norm_apply(dve, 2, NT // 2 - 1, x)

                    for nh in range(NH):
                        dve.wait_ge(S["s_rows"], nh + 1)
                        n = steps.did(nc.vector.reduce_max(gmax[0:2 * H, 2 + nh:3 + nh],
                                                           pair[0][0:2 * H, nh * 512:(nh + 1) * 512], AX.X))
                    steps.after(n)
                    n = steps.did(nc.vector.reduce_max(gmax[0:2 * H, 0:1], gmax[0:2 * H, 2:2 + NH], AX.X))
                    steps.after(n)
                    nc.vector.tensor_scalar(gmax[0:H, 1:2], gmax[0:H, 0:1], -STEEP, None, ALU.mult)\
                        .then_inc(S["gmax_ready"], 1)
                    dve.wait_ge(S["gmax_spread"], 1)
                    n = steps.did(nc.vector.tensor_copy(gmaxB[:, 0:H], bank[3][:, 0:H]))
                    n = steps.did(nc.vector.tensor_tensor(gmaxB[:, H:2 * H], bank[3][:, H:2 * H], edge_b[:, :], ALU.add))
                    steps.after(n)
                    m = steps.did(nc.vector.tensor_scalar(kexp[:, 2, :], gmaxB[:, H:2 * H], GMAX, None, ALU.min))
                    steps.after(m)
                    n = steps.did(nc.vector.tensor_tensor(kexp[:, 0, :], kexp[:, 2, :], gmaxB[:, H:2 * H], ALU.subtract))
                    dve.wait_ge(S["s_cols"], 1)
                    t2v = t2[:, 0, :].rearrange("p (t h) -> p t h", t=NT)
                    t2w = t2[:, 1, :].rearrange("p (t h) -> p t h", t=NT)
                    n = steps.did(nc.vector.tensor_tensor(t2v, bank[2][:, 0:NT * H].rearrange("p (t h) -> p t h", t=NT),
                                                          gmaxB[:, 0:H].unsqueeze(1).to_broadcast([P, NT, H]), ALU.subtract))
                    steps.after(n)
                    nc.vector.tensor_tensor(t2w, t2v, kexp[:, 2, :].unsqueeze(1).to_broadcast([P, NT, H]), ALU.add)\
                        .then_inc(S["t2_ready"], 1)
                    dve.wait_ge(S["bvexp_ready"], 2)
                    n = steps.did(nc.vector.tensor_tensor(kv[:, :, :], v2[:, :, :],
                                                          kexp[:, 1, :].unsqueeze(1).to_broadcast([P, NT, H]), ALU.mult))
                    nc.vector.tensor_scalar(kexp[:, 2, :], kexp[:, 1, :], -1.0, None, ALU.mult).then_inc(S["kappa_ready"], 1)
                    steps.after(n)
                    n = steps.did(nc.vector.tensor_copy(kvHL[:, :, 0:H], kv[:, :, :]))
                    steps.after(n)
                    nc.vector.tensor_tensor(kvHL[:, :, H:2 * H], kv[:, :, :], kvHL[:, :, 0:H], ALU.subtract)\
                        .then_inc(S["kv_ready"], 1)

                    def heads(ap, tiles=1):
                        return ap.rearrange("p (h d) -> p h d", h=tiles * H)

                    def wh_scale(k):
                        two = slice(2 * k, 2 * k + 2)
                        dve.wait_ge(S["wh_psum"], k + 1)
                        nc.vector.tensor_tensor(V[:, two, :].rearrange("p t (h d) -> p (t h) d", h=H), heads(bank[4 + k], 2),
                                                v2[:, two, :].rearrange("p t h -> p (t h)").unsqueeze(2)
                                                .to_broadcast([P, 2 * H, HD]), ALU.mult).then_inc(S["wh_scaled"], 1)
                    def edge_sums():
                        dens = bank[6][:, 0:NT * 2 * H].rearrange("p (t k) -> p t k", t=NT)
                        dve.wait_ge(S["den_cols"], 1)
                        n = steps.did(nc.vector.tensor_copy(kv[:, :, :], dens[:, :, 0:H]))
                        steps.after(n)
                        nc.vector.tensor_tensor(kv[:, :, :], kv[:, :, :], dens[:, :, H:2 * H], ALU.add)\
                            .then_inc(S["den_cols_read"], 1)

                    def num_copy(hg):
                        dve.wait_ge(S["group_done"], NT * (hg + 1))
                        nc.vector.tensor_copy(pbuf[:, 0, :], pair[2 * hg][:, :]).then_inc(S["num_copied"], 1)

                    def hout(hg):
                        dve.wait_ge(S["back_turned"], hg + 1)
                        hs = slice(hg * HG, (hg + 1) * HG)
                        n = steps.did(nc.vector.tensor_tensor(
                            sums[:, :, hs], pair[1][:, :].rearrange("p (t h d) -> p t h d", t=NT, h=HG)[:, :, :, 0],
                            kv[:, :, hs], ALU.add))
                        steps.after(n)
                        n = steps.did(nc.vector.reciprocal(rsums[:, :, hs], sums[:, :, hs]))
                        steps.after(n)
                        for t in range(NT):
                            last = nc.vector.tensor_tensor(
                                xn[:, t, hg * P:(hg + 1) * P].rearrange("p (h d) -> p h d", h=HG),
                                pair[0][:, t * P:(t + 1) * P].rearrange("p (h d) -> p h d", h=HG),
                                rsums[:, t, hs].unsqueeze(2).to_broadcast([P, HG, HD]), ALU.mult)
                        last.then_inc(S["hout_ready"], 1)

                    def mask_steep(u):
                        g, r = u // HG, u % HG
                        hg, jt = g // NT, g % NT
                        h = hg * HG + r
                        if u == 0:
                            dve.wait_ge(S["steep_out"], 16)
                        if jt == 0:
                            dve.wait_ge(S[f"steep_in{h}"], 16)
                        if u >= 3:
                            dve.wait_ge(S["r_ready"], u - 2)
                        nc.vector.tensor_tensor(zbuf[:, u % 3, :], steepT[:, h, :], adjT[:, jt, :], ALU.mult)\
                            .then_inc(S["masked_steep"], 1)

                    for k in range(NT // 2):
                        wh_scale(k)
                    for t in range(NT // 2):
                        dve.wait_ge(S["wh_scaled"], t // 2 + 1)
                        nc.vector.tensor_tensor(heads(vm_wide[:, t, :]), heads(V[:, t, :]),
                                                kexp[:, 1, :].unsqueeze(2).to_broadcast([P, H, HD]), ALU.mult)\
                            .then_inc(S["vm_wide_front"], 1)
                    for u in range(UNITS):
                        mask_steep(u)
                        if u == 12:
                            edge_sums()
                        if u == HG * NT + 5:
                            num_copy(0)
                        if u == HG * (NT + 5) + 2:
                            hout(0)
                    dve.wait_ge(S["back_turned"], 1)
                    num_copy(1)
                    hout(1)
                    dve.wait_ge(S["hout_ready"], NG)

                    def shift(k):
                        two = slice(2 * k, 2 * k + 2)
                        dve.wait_ge(S["ln_rstd4"], k + 1)
                        nc.vector.scalar_tensor_tensor(shift4[:, two], meanvar[:, two, 0], -1.0, rstd[:, two],
                                                       ALU.mult, ALU.mult).then_inc(S["shift4_ready"], 1)

                    def times_gamma(k):
                        two = slice(2 * k, 2 * k + 2)
                        dve.wait_ge(S["z4_ready"], 2 * k + 2)
                        nc.vector.tensor_tensor(xn[:, two, :], xn[:, two, :],
                                                gam_b[:, :].unsqueeze(1).to_broadcast([P, 2, D]), ALU.mult)\
                            .then_inc(S["gamma_done"], 1)

                    def residual2(k):
                        y = xn[:, 2 * k:2 * k + 2, :].rearrange("p t d -> p (t d)")
                        xh = x[:, 2 * k:2 * k + 2, :].rearrange("p t d -> p (t d)")
                        dve.wait_ge(S["x_less_one"], 1)
                        dve.wait_ge(S["y_exp"], k + 1)
                        n = steps.did(nc.vector.scalar_tensor_tensor(xh, zbuf[:, k // 2, (k % 2) * 2 * D:(k % 2 + 1) * 2 * D],
                                                                     1.0, xh, ALU.min, ALU.add))
                        steps.after(n)
                        nc.vector.scalar_tensor_tensor(xh, y, 0.0, xh, ALU.max, ALU.add).then_inc(S["x_done2"], 1)

                    HALVES = NT // 2
                    for s in range(HALVES + 5):
                        if s < HALVES:
                            norm_stats(dve, steps, 4, s, xn)
                        if 1 <= s < HALVES + 1:
                            shift(s - 1)
                        if 2 <= s < HALVES + 2:
                            times_gamma(s - 2)
                        if 3 <= s < HALVES + 3:
                            residual2(s - 3)
                        if 5 <= s < HALVES + 5:
                            norm_apply(dve, 3, s - 5, x)
                        if 4 <= s < HALVES + 4:
                            dve.wait_ge(S["x_done2"], s - 3)
                            norm_stats(dve, steps, 3, s - 4, x)

                    for nh in range(NH):
                        dve.wait_ge(S["a3_psum"], nh + 1)
                        n = steps.did(nc.vector.reduce_max(f3[:, 3 + nh:4 + nh], pair[0][:, nh * 512:(nh + 1) * 512], AX.X))
                    steps.after(n)
                    n = steps.did(nc.vector.reduce_max(f3[:, 0:1], f3[:, 3:3 + NH], AX.X))
                    steps.after(n)
                    n = steps.did(nc.vector.tensor_scalar(f3[:, 1:2], f3[:, 0:1], -STEEP, None, ALU.mult))
                    nc.vector.tensor_scalar(f3[:, 2:3], f3[:, 0:1], -SLOPE, None, ALU.mult).then_inc(S["f3_ready"], 1)
                    dve.wait_ge(S["f3_cols"], 1)
                    n = steps.did(nc.vector.tensor_scalar(e3[:, 0, :], bank[2][:, 0:NT], f3[:, 0:1], None, ALU.add))
                    steps.after(n)
                    nc.vector.tensor_scalar(e3[:, 1, :], e3[:, 0, :], 0.0, None, ALU.min)
                    nc.vector.tensor_scalar(e3[:, 2, :], e3[:, 0, :], 0.0, None, ALU.max).then_inc(S["e3_ready"], 1)
                    dve.wait_ge(S["a3_ready"], 1)
                    dve.wait_ge(S["b3_ready"], 2)
                    for j in range(NT):
                        n = steps.did(nc.vector.tensor_scalar(PU[:, j, :], zbuf[:, 0, :], b3[:, j:j + 1], k3[:, j:j + 1],
                                                              ALU.mult, ALU.max))
                        steps.after(n)
                        dve.wait_ge(S["mu_ready"], j + 1)
                        nc.vector.tensor_tensor_reduce(out=PU[:, j, :], in0=PU[:, j, :], in1=pbuf[:, j % 3, :], scale=1.0,
                                                       scalar=0.0, op0=ALU.mult, op1=ALU.add,
                                                       accum_out=den3[:, j:j + 1]).then_inc(S["pu_ready"], 1)
                        dve.wait_ge(S["pu_ready"], j + 1)
                        n = steps.did(nc.vector.reciprocal(rden3[:, j:j + 1], den3[:, j:j + 1]))
                        steps.after(n)
                        dve.wait_ge(S["wh3_copied"], j // 2 + 1)
                        nc.vector.tensor_scalar(V[:, j, :], V[:, j, :], rden3[:, j:j + 1], None, ALU.mult)\
                            .then_inc(S["g3_ready"], 1)
                        make_mask(dve, j)
                        if j == 0:
                            dve.wait_ge(S["x_in"], 16)
                        if j % 2 == 0:
                            norm_stats(dve, steps, 0, j // 2, x_next)
                        elif j >= 3:
                            norm_apply(dve, 0, j // 2 - 1, x_next)
                    norm_apply(dve, 0, NT // 2 - 1, x_next)

                    dve.wait_ge(S["x_less_one"], 2)
                    for k in range(NT // 2):
                        xh = x[:, 2 * k:2 * k + 2, :].rearrange("p t d -> p (t d)")
                        dve.wait_ge(S["o_exp"], k + 1)
                        n = steps.did(nc.vector.scalar_tensor_tensor(xh, zbuf[:, k // 2, (k % 2) * 512:(k % 2 + 1) * 512],
                                                                     1.0, xh, ALU.min, ALU.add))
                        steps.after(n)
                        nc.vector.scalar_tensor_tensor(xh, bank[k], 0.0, xh, ALU.max, ALU.add).then_inc(S["x_done3"], 1)

            clear_signals()


_WEIGHTS = ["L0_gnn_Wq", "L0_gnn_bq", "L0_gnn_Wk", "L0_gnn_bk", "L0_gnn_Wv", "L0_gnn_bv", "L0_gnn_Wo", "L0_gnn_bo",
            "L1_gnn_W_msg", "L1_gnn_W_upd", "L1_gnn_bias", "L2_gnn_W", "L2_gnn_a1", "L2_gnn_a2", "L2_gnn_edge_emb",
            "L2_gnn_ln_gamma", "L2_gnn_ln_beta", "L3_gnn_W", "L3_gnn_a"]


def kernel(**inputs):
    import concourse.bacc as _bacc
    from concourse.bass_utils import run_bass_kernel_spmd as _run

    nc = _bacc.Bacc("TRN2", target_bir_lowering=False, num_devices=1)
    arrays, args = {}, {}
    for name in ["x", "adj"] + _WEIGHTS:
        a = np.ascontiguousarray(inputs[name])
        arrays[f"in_{name}"] = a
        args[name] = nc.dram_tensor(f"in_{name}", a.shape, mybir.dt.from_np(a.dtype), kind="ExternalInput").ap()
    out = nc.dram_tensor("out", inputs["x"].shape, mybir.dt.float32, kind="ExternalOutput").ap()
    build_program(nc, args["x"], args["adj"], args, out)
    r = _run(nc, [arrays], core_ids=[0])
    return r.results[0]["out"]
```

```python
from contextlib import ExitStack

import numpy as np

import concourse.bass as bass
from concourse import mybir


class Steps:

    def __init__(self, engine, semaphore):
        self.engine, self.semaphore, self.count = engine, semaphore, 0

    def did(self, instruction):
        instruction.then_inc(self.semaphore, 1)
        self.count += 1
        return self.count

    def after(self, count):
        self.engine.wait_ge(self.semaphore, count)


def build_program(nc, x_dram, adj_dram, w, out_dram):
    f32, f16, bf16, i32 = mybir.dt.float32, mybir.dt.float16, mybir.dt.bfloat16, mybir.dt.int32
    ALU, ACT, AX = mybir.AluOpType, mybir.ActivationFunctionType, mybir.AxisListType

    B, N, D = x_dram.shape
    P = 128
    NT = N // P
    DT = D // P
    H = 8
    HD = D // H
    HG = 4
    NG = H // HG
    NH = N // 512
    QSCALE = float(1.0 / np.sqrt(HD))
    EPS = 1e-5
    MASKED = -1e30
    SLOPE = 0.2
    STEEP = 1.0 - SLOPE
    GMAX = 100.0
    UNITS = NT * H
    GROUPS = UNITS // HG
    CHUNKS_BEFORE = 2
    AHEAD = 4

    ctx = ExitStack()
    with ctx:
        def sb(name, shape, dt):
            return ctx.enter_context(nc.sbuf_tensor(name, shape, dt))

        def sem(name):
            return ctx.enter_context(nc.semaphore(name))

        x = sb("x", [P, NT, D], f32)
        hT = sb("hT", [P, DT, N], f32)
        adjN = sb("adjN", [P, NT, N], f16)
        adjT = sb("adjT", [P, NT, N], f16)
        maskN = sb("maskN", [P, NT, N], bf16)
        headpairs = sb("headpairs", [P, 8192], f32)
        qkparts = sb("qkparts", [P, 4096], f32)
        wide = sb("wide", [P, 8192], f32)
        V = sb("V", [P, NT, D], f32)
        zbuf = sb("zbuf", [P, 3, N], f32)
        pbuf = sb("pbuf", [P, 3, N], f32)

        pairs16 = headpairs[:, :].bitcast(f16)
        QP = pairs16[:, 0:H * N].rearrange("p (h n) -> p h n", h=H)
        KP = pairs16[:, H * N:2 * H * N].rearrange("p (h n) -> p h n", h=H)
        MHW = 258
        msgH = pairs16[:, 0:NT * MHW].rearrange("p (t d) -> p t d", t=NT)
        msgL = pairs16[:, NT * MHW:NT * MHW + NT * D].rearrange("p (t d) -> p t d", t=NT)
        steepT = headpairs[:, :].rearrange("p (h n) -> p h n", h=H)
        parts16 = qkparts[:, :].bitcast(f16)
        QH, QL, KH, KL = (parts16[:, k * DT * N:(k + 1) * DT * N].rearrange("p (t n) -> p t n", t=DT)
                          for k in range(4))
        xn = qkparts[:, 0:NT * D].rearrange("p (t d) -> p t d", t=NT)
        vmH, vmL = (parts16[:, (2 + k) * NT * D:(3 + k) * NT * D].rearrange("p (t d) -> p t d", t=NT)
                    for k in range(2))
        x_next = qkparts[:, NT * D:2 * NT * D].rearrange("p (t d) -> p t d", t=NT)
        vm_wide = pbuf[:, 0:2, :].rearrange("p a (t d) -> p (a t) d", d=D)
        whole = pbuf[:, 0:2, :].rearrange("p a (t d) -> p (a t) d", d=512)
        adj_int = headpairs[:, :].bitcast(i32).rearrange("p (t n) -> p t n", t=NT)
        PT = wide[:, :].rearrange("p (b r t n) -> p b r t n", b=2, r=HG, t=NT)
        R = wide[:, :].rearrange("p (b r n) -> p b r n", b=2, r=HG)
        PU = wide[:, :].rearrange("p (t n) -> p t n", t=NT)

        wq, wk, wv, wo, wmsg, wupd, w2, w3 = (sb(n, [P, DT, D], f32) for n in
                                             ("wq", "wk", "wv", "wo", "wmsg", "wupd", "w2", "w3"))
        wa2 = sb("wa2", [P, DT, 2, H], f32)
        wa3 = sb("wa3", [P, DT, 2], f32)
        bv_b, bo_b, b1_b, gam_b, bet_b = (sb(n, [P, D], f32) for n in
                                          ("bv_b", "bo_b", "b1_b", "gam_b", "bet_b"))
        bq_c, bk_c = sb("bq_c", [P, DT], f32), sb("bk_c", [P, DT], f32)
        a2_b = sb("a2_b", [P, 2, HD], f32)
        edge_b = sb("edge_b", [P, H], f32)
        both = sb("both", [P, H], f32)
        ones_b = sb("ones_b", [P, D], f32)
        identF = sb("identF", [P, P], f32)
        identH = sb("identH", [P, P], f16)
        nhalf = sb("nhalf", [P, NT], f32)

        stats = sb("stats", [P, NT, 6], f32)
        meanvar = sb("meanvar", [P, NT, 2], f32)
        vareps = sb("vareps", [P, NT], f32)
        rstd = sb("rstd", [P, NT], f32)
        shifts = sb("shifts", [P, NT], f32)
        nmax = sb("nmax", [P, UNITS], f32)
        den = sb("den", [P, UNITS], f32)
        rden = sb("rden", [P, UNITS], f32)
        bcS = sb("bcS", [P, 2, P], f32)
        deg = sb("deg", [P, NT, 2], f32)
        gmax = sb("gmax", [P, 2 + NH], f32)
        gmaxB = sb("gmaxB", [P, 2 * H], f32)
        kexp = sb("kexp", [P, 3, H], f32)
        t2 = sb("t2", [P, 2, NT * H], f32)
        b2 = sb("b2", [P, NT, H], f32)
        v2 = sb("v2", [P, NT, H], f32)
        kv = sb("kv", [P, NT, H], f32)
        kvHL = sb("kvHL", [P, NT, 2 * H], f16)
        sums, rsums = sb("sums", [P, NT, H], f32), sb("rsums", [P, NT, H], f32)
        e3 = sb("e3", [P, 3, NT], f32)
        b3, k3, den3, rden3 = (sb(n, [P, NT], f32) for n in ("b3", "k3", "den3", "rden3"))
        f3 = sb("f3", [P, 3 + NH], f32)

        pair = [ctx.enter_context(nc.psum_tensor(f"pair{i}", [P, 1024], f32)) for i in range(4)]
        bank = [pair[i // 2][:, (i % 2) * 512:(i % 2) * 512 + 512] for i in range(8)]

        steep_dram = nc.dram_tensor("steep_rows", (H, N), f32, kind="Internal").ap()

        w_in, w_small, ident_set, setup_steps = (sem(n) for n in
                                                 ("w_in", "w_small", "ident_set", "setup_steps"))
        with nc.Block() as block:
            @block.sync
            def _(sp):
                for name, dst in (("L0_gnn_Wq", wq), ("L0_gnn_Wk", wk), ("L0_gnn_Wv", wv),
                                  ("L0_gnn_Wo", wo), ("L1_gnn_W_msg", wmsg), ("L1_gnn_W_upd", wupd),
                                  ("L2_gnn_W", w2), ("L3_gnn_W", w3)):
                    sp.dma_start(dst[:, :, :], w[name].rearrange("(t p) n -> p t n", p=P)).then_inc(w_in, 16)
                sp.wait_ge(w_in, 8 * 16)

            @block.scalar
            def _(act):
                small = 0
                for dst, src in ((bv_b[:, :], w["L0_gnn_bv"].partition_broadcast(P)),
                                 (bo_b[:, :], w["L0_gnn_bo"].partition_broadcast(P)),
                                 (b1_b[:, :], w["L1_gnn_bias"].partition_broadcast(P)),
                                 (gam_b[:, :], w["L2_gnn_ln_gamma"].partition_broadcast(P)),
                                 (bet_b[:, :], w["L2_gnn_ln_beta"].partition_broadcast(P)),
                                 (a2_b[:, 0, :], w["L2_gnn_a1"].partition_broadcast(P)),
                                 (a2_b[:, 1, :], w["L2_gnn_a2"].partition_broadcast(P)),
                                 (zbuf[:, 0, 0:2 * D], w["L3_gnn_a"].rearrange("n o -> (n o)").partition_broadcast(P)),
                                 (edge_b[:, :], w["L2_gnn_edge_emb"][1, :].partition_broadcast(P)),
                                 (bq_c[:, :], w["L0_gnn_bq"].rearrange("(t p) -> p t", p=P)),
                                 (bk_c[:, :], w["L0_gnn_bk"].rearrange("(t p) -> p t", p=P))):
                    act.dma_start(dst, src, allow_slow_non_contiguous=True).then_inc(w_small, 16)
                    small += 16
                act.wait_ge(w_small, small)

            @block.gpsimd
            def _(pool):
                nc.gpsimd.memset(nhalf[:, :], -0.5)
                nc.gpsimd.memset(ones_b[:, :], 1.0)
                nc.gpsimd.memset(identF[:, :], 0.0).then_inc(ident_set, 1)
                nc.gpsimd.memset(identH[:, :], 0.0).then_inc(ident_set, 1)
                pool.wait_ge(ident_set, 2)
                for m in (identF, identH):
                    nc.gpsimd.affine_select(out=m[:, :], in_=m[:, :], compare_op=ALU.not_equal, fill=1.0,
                                            base=0, pattern=[[-1, P]], channel_multiplier=1).then_inc(ident_set, 1)
                pool.wait_ge(ident_set, 4)

            @block.vector
            def _(dve):
                steps = Steps(dve, setup_steps)
                dve.wait_ge(w_in, 8 * 16)
                dve.wait_ge(w_small, 11 * 16)
                nc.vector.tensor_scalar(bq_c[:, :], bq_c[:, :], QSCALE, None, ALU.mult)
                dve.wait_ge(ident_set, 4)
                nc.vector.tensor_tensor(both[:, :], identF[:, 0:H], identF[:, H:2 * H], ALU.add)
                for c in range(DT):
                    for k in range(2):
                        n = steps.did(nc.vector.tensor_tensor(
                            pbuf[:, c, k * D:(k + 1) * D].rearrange("p (h d) -> p h d", h=H),
                            w2[:, c, :].rearrange("p (h d) -> p h d", h=H),
                            a2_b[:, k, :].unsqueeze(1).to_broadcast([P, H, HD]), ALU.mult))
                        n = steps.did(nc.vector.tensor_tensor(
                            pbuf[:, c, (2 + k) * D:(3 + k) * D],
                            w3[:, c, :], zbuf[:, 0, k * D:(k + 1) * D], ALU.mult))
                steps.after(n)
                for c in range(DT):
                    for k in range(2):
                        nc.vector.tensor_reduce(wa2[:, c, k, :],
                                                pbuf[:, c, k * D:(k + 1) * D].rearrange("p (h d) -> p h d", h=H),
                                                AX.X, ALU.add)
                        n = steps.did(nc.vector.tensor_reduce(wa3[:, c, k:k + 1],
                                                              pbuf[:, c, (2 + k) * D:(3 + k) * D], AX.X, ALU.add))
                steps.after(n)

        names = ["x_in", "x_taken", "q_parts", "k_parts", "v_ready", "qk_psum", "v_psum", "qk_wide",
                 "scores", "z_ready", "p_ready", "turned", "pt_even", "pt_odd", "pv_done", "rden_ready",
                 "sums_spread", "sums_copied", "ctx_ready", "projected",
                 "adj_cast", "adjT_psum", "adjT_ready",
                 "msg_psum", "msg_hi", "msg_parts", "ones_set", "agg_psum", "upd_psum",
                 "s_rows", "s_cols", "wh_psum", "gmax_ready", "gmax_spread", "t2_ready", "steep_row", "steep_out",
                 "bvexp_ready", "kappa_ready", "kv_ready", "den_cols", "den_cols_read", "wh_scaled", "vm_wide_front", "vm_wide_back",
                 "vm_hi", "vm_lo", "masked_steep", "r_ready", "group_done", "num_copied", "den_copied",
                 "back_turned", "hout_ready", "shift0_ready", "shift3_ready", "shift4_ready", "z4_ready", "gamma_done", "y_ready", "y_exp", "x_less_one",
                 "a3_psum", "f3_cols", "wh3_psum", "f3_ready", "a3_ready", "e3_ready", "b3_ready",
                 "wh3_copied", "mu_ready", "pu_ready", "g3_ready", "out3_psum", "o_exp",
                 "x_done0", "x_done1", "x_done2", "x_done3", "dve_steps"]
        names += [f"adj_in{t}" for t in range(NT)] + [f"{of}_pairs{h}" for of in ("query", "key") for h in range(H)]
        names += [f"steep_in{h}" for h in range(H)]
        for L in range(5):
            names += [f"ln_var{L}", f"ln_rstd{L}", f"ln_x{L}", f"ln_psum{L}", f"hT_ready{L}"]
        S = {n: sem(n) for n in names}
        numbers = [S[n].num for n in names]
        assert numbers == list(range(numbers[0], numbers[0] + len(names)))

        out_written = sem("out_written")
        OUT_WRITTEN = NT // 2 * 16

        def clear_signals():
            nc.gpsimd.sem_clear(range(numbers[0], numbers[0] + len(names)))
            nc.all_engine_barrier()

        def unit(u):
            return (u % 2, u // 2) if u < 2 * HG else (u // HG, u % HG)

        def units_until(g):
            return 2 * HG - 1 if g == 0 else HG * (g + 1)

        def load_batch(sp, index):
            sp.dma_start(x_next[:, :, :], x_dram[index].rearrange("(t p) d -> p t d", p=P)).then_inc(S["x_in"], 16)
            for t in range(NT):
                sp.dma_start(adj_int[:, t, :], adj_dram[index, t * P:(t + 1) * P, :]).then_inc(S[f"adj_in{t}"], 16)

        def stack(engine, to, quarters, h, done):
            rows = slice(h % HG * HD, (h % HG + 1) * HD)
            for k, part in enumerate(quarters):
                engine.dma_start(to[k * HD:(k + 1) * HD, h, :], part[rows, h // HG, :]).then_inc(done, 16)

        def cast_adjacency(act, t):
            act.wait_ge(S[f"adj_in{t}"], 16)
            nc.scalar.activation(adjN[:, t, :], adj_int[:, t, :], ACT.Copy).then_inc(S["adj_cast"], 1)

        def make_mask(dve, t):
            dve.wait_ge(S["adj_cast"], t + 1)
            nc.vector.tensor_scalar(maskN[:, t, :], adjN[:, t, :], 0.0, MASKED, ALU.is_equal, ALU.mult)

        def norm_stats(dve, steps, L, k, nodes):
            for t in (2 * k, 2 * k + 1):
                n = steps.did(nc.vector.bn_stats(stats[:, t, :], nodes[:, t, :]))

            steps.after(n)
            for t in (2 * k, 2 * k + 1):
                n = steps.did(nc.vector.bn_aggr(meanvar[:, t, :], stats[:, t, :]))
            steps.after(n)
            nc.vector.tensor_scalar(vareps[:, 2 * k:2 * k + 2], meanvar[:, 2 * k:2 * k + 2, 1], EPS, None, ALU.add)\
                .then_inc(S[f"ln_var{L}"], 1)

        def norm_apply(dve, L, k, nodes):
            dve.wait_ge(S[f"ln_rstd{L}"], k + 1)
            for t in (2 * k, 2 * k + 1):
                nc.vector.tensor_scalar(xn[:, t, :], nodes[:, t, :], meanvar[:, t, 0:1], rstd[:, t:t + 1],
                                        ALU.subtract, ALU.mult).then_inc(S[f"ln_x{L}"], 1)

        def shift(dve, L, k):
            two = slice(2 * k, 2 * k + 2)
            dve.wait_ge(S[f"ln_rstd{L}"], k + 1)
            nc.vector.scalar_tensor_tensor(shifts[:, two], meanvar[:, two, 0], -1.0, rstd[:, two],
                                           ALU.mult, ALU.mult).then_inc(S[f"shift{L}_ready"], 1)

        def normalise(act, L, k, nodes):
            act.wait_ge(S[f"shift{L}_ready"], k + 1)
            for t in (2 * k, 2 * k + 1):
                nc.scalar.activation(xn[:, t, :], nodes[:, t, :], ACT.Identity, bias=shifts[:, t:t + 1],
                                     scale=rstd[:, t:t + 1]).then_inc(S[f"ln_x{L}"], 1)

        def norm_root(pool, L, k):
            pool.wait_ge(S[f"ln_var{L}"], k + 1)
            nc.gpsimd.tensor_tensor(rstd[:, 2 * k:2 * k + 2], vareps[:, 2 * k:2 * k + 2], nhalf[:, 0:2], ALU.pow)\
                .then_inc(S[f"ln_rstd{L}"], 1)

        def norm_roots(pool, L):
            for k in range(NT // 2):
                norm_root(pool, L, k)

        def ln_pair(pe, L, k, b):
            for t in (2 * k, 2 * k + 1):
                pe.wait_ge(S[f"ln_x{L}"], t + 1)
                for c in range(DT):
                    last = nc.tensor.transpose(bank[b][:, c * 256 + (t % 2) * P:c * 256 + (t % 2 + 1) * P],
                                               xn[:, t, c * P:(c + 1) * P], identF[:, :])
            last.then_inc(S[f"ln_psum{L}"], 1)

        def hT_pair(act, L, k, b):
            act.wait_ge(S[f"ln_psum{L}"], k + 1)
            nc.scalar.activation(hT[:, :, 2 * k * P:(2 * k + 2) * P], bank[b].rearrange("p (c n) -> p c n", c=DT),
                                 ACT.Relu).then_inc(S[f"hT_ready{L}"], 1)

        def query_key_chunk(p):
            c, isk, nh = p // 4, (p // 2) % 2, p % 2
            for k in range(DT):
                last = nc.tensor.matmul(bank[4 + p % 4], (wk if isk else wq)[:, k, c * P:(c + 1) * P],
                                        hT[:, k, nh * 512:(nh + 1) * 512], start=(k == 0), stop=(k == DT - 1))
            return last

        def start_layer0(pe):
            for k in range(NT // 2):
                ln_pair(pe, 0, k, 4 + k)
            for p in range(CHUNKS_BEFORE):
                pe.wait_ge(S["hT_ready0"], 2 * (p + 1))
                query_key_chunk(p)

        with nc.Block() as block:
            @block.sync
            def _(sp):
                load_batch(sp, 0)

            @block.gpsimd
            def _(pool):
                norm_roots(pool, 0)
                nc.gpsimd.memset(x[:, 0, 0:1], 0.0).then_inc(out_written, OUT_WRITTEN)

            @block.scalar
            def _(act):
                for t in range(NT):
                    cast_adjacency(act, t)
                for k in range(NT // 2):
                    hT_pair(act, 0, k, 4 + k)

            @block.vector
            def _(dve):
                steps = Steps(dve, S["dve_steps"])
                dve.wait_ge(S["x_in"], 16)
                for k in range(NT // 2):
                    norm_stats(dve, steps, 0, k, x_next)
                for k in range(NT // 2):
                    norm_apply(dve, 0, k, x_next)
                for t in range(NT):
                    make_mask(dve, t)

            @block.tensor
            def _(pe):
                start_layer0(pe)
        clear_signals()

        with nc.Fori(0, B) as b:
            with nc.Block() as block:
                @block.sync
                def _(sp):
                    sp.wait_ge(S["q_parts"], 2 * NH)
                    for h in range(2):
                        stack(sp, QP, (QH, QH, QL, QL), h, S[f"query_pairs{h}"])
                    sp.wait_ge(S["k_parts"], 2 * NH)
                    for h in range(2):
                        stack(sp, KP, (KH, KL, KH, KL), h, S[f"key_pairs{h}"])
                    for h in range(2, HG):
                        stack(sp, QP, (QH, QH, QL, QL), h, S[f"query_pairs{h}"])
                        stack(sp, KP, (KH, KL, KH, KL), h, S[f"key_pairs{h}"])
                    sp.wait_ge(S["q_parts"], 2 * DT * NH)
                    sp.wait_ge(S["k_parts"], 2 * DT * NH)
                    for h in range(HG, H):
                        stack(sp, QP, (QH, QH, QL, QL), h, S[f"query_pairs{h}"])
                        stack(sp, KP, (KH, KL, KH, KL), h, S[f"key_pairs{h}"])
                    sp.wait_ge(S["steep_row"], 1)
                    sp.dma_start(steep_dram[:, :], zbuf[0:H, 0, :]).then_inc(S["steep_out"], 16)
                    sp.wait_ge(S["steep_out"], 16)
                    sp.wait_ge(S["agg_psum"], NT)
                    for h in range(H):
                        sp.dma_start(steepT[:, h, :], steep_dram[h, :].partition_broadcast(P))\
                            .then_inc(S[f"steep_in{h}"], 16)
                    sp.wait_ge(S["masked_steep"], UNITS)
                    sp.wait_ge(S["group_done"], GROUPS)
                    load_batch(sp, (b + 1) % B)
                    out_r = out_dram[b].rearrange("(t p) d -> p t d", p=P)
                    for k in range(NT // 2):
                        sp.wait_ge(S["x_done3"], k + 1)
                        sp.dma_start(out_r[:, 2 * k:2 * k + 2, :], x[:, 2 * k:2 * k + 2, :]).then_inc(out_written, 16)

                @block.gpsimd
                def _(pool):
                    pool.wait_ge(out_written, OUT_WRITTEN)
                    nc.gpsimd.sem_clear(range(out_written.num, out_written.num + 1))
                    nc.gpsimd.tensor_tensor(x[:, :, :], x_next[:, :, :],
                                            bo_b[:, :].unsqueeze(1).to_broadcast([P, NT, D]), ALU.add)\
                        .then_inc(S["x_taken"], 1)

                    norm_roots(pool, 1)
                    norm_roots(pool, 2)
                    pool.wait_ge(S["ln_x2"], NT)
                    nc.gpsimd.tensor_tensor(x[:, :, :], x[:, :, :], ones_b[:, :].unsqueeze(1).to_broadcast([P, NT, D]),
                                            ALU.subtract).then_inc(S["x_less_one"], 1)
                    pool.wait_ge(S["bvexp_ready"], 2)
                    for t in range(NT // 2, NT):
                        pool.wait_ge(S["wh_scaled"], t // 2 + 1)
                        last = nc.gpsimd.tensor_tensor(vm_wide[:, t, :].rearrange("p (h d) -> p h d", h=H),
                                                       V[:, t, :].rearrange("p (h d) -> p h d", h=H),
                                                       kexp[:, 1, :].unsqueeze(2).to_broadcast([P, H, HD]), ALU.mult)
                        if t % 2 == 1:
                            last.then_inc(S["vm_wide_back"], 1)
                    for k in range(NT // 2):
                        two = slice(2 * k, 2 * k + 2)
                        pool.wait_ge(S["vm_hi"], k + 1)
                        nc.gpsimd.tensor_tensor(vmL[:, two, :], vm_wide[:, two, :], vmH[:, two, :], ALU.subtract)\
                            .then_inc(S["vm_lo"], 1)
                    def plus_beta(k):
                        two = slice(2 * k, 2 * k + 2)
                        pool.wait_ge(S["gamma_done"], k + 1)
                        nc.gpsimd.tensor_tensor(xn[:, two, :], xn[:, two, :],
                                                bet_b[:, :].unsqueeze(1).to_broadcast([P, 2, D]), ALU.add)\
                            .then_inc(S["y_ready"], 1)

                    for k in range(NT // 2 + 2):
                        if k < NT // 2:
                            norm_root(pool, 4, k)
                        if k >= 2:
                            plus_beta(k - 2)
                    norm_roots(pool, 3)
                    pool.wait_ge(S["ln_x3"], NT)
                    nc.gpsimd.tensor_tensor(x[:, :, :], x[:, :, :], ones_b[:, :].unsqueeze(1).to_broadcast([P, NT, D]),
                                            ALU.subtract).then_inc(S["x_less_one"], 1)
                    pool.wait_ge(S["a3_ready"], 1)
                    for j in range(NT):
                        if j >= 3:
                            pool.wait_ge(S["pu_ready"], j - 2)
                        nc.gpsimd.tensor_tensor(pbuf[:, j % 3, :], zbuf[:, 1, :], adjT[:, j, :], ALU.mult)\
                            .then_inc(S["mu_ready"], 1)
                        if j >= 3 and j % 2 == 1:
                            norm_root(pool, 0, j // 2 - 1)
                    norm_root(pool, 0, NT // 2 - 1)

                @block.scalar
                def _(act):
                    for p in range(2 * DT * NH):
                        c, isk = p // 4, (p // 2) % 2
                        if p >= CHUNKS_BEFORE:
                            act.wait_ge(S["qk_psum"], p + 1 - CHUNKS_BEFORE)
                        if p >= 4:
                            act.wait_ge(S["k_parts" if isk else "q_parts"], 2 * (p % 2 + 1))
                        nc.scalar.activation(whole[:, p % 4, :], bank[4 + p % 4], ACT.Identity,
                                             bias=(bk_c if isk else bq_c)[:, c:c + 1],
                                             scale=1.0 if isk else QSCALE).then_inc(S["qk_wide"], 1)

                    def exp_unit(u):
                        g, r = unit(u)
                        act.wait_ge(S["z_ready"], u + 1)
                        if u >= 3:
                            act.wait_ge(S["turned"], 2 * (u - 3) + 2)
                        if u == 0:
                            act.wait_ge(S["q_parts"], 2 * DT * NH)
                            act.wait_ge(S["k_parts"], 2 * DT * NH)
                        nc.scalar.activation(pbuf[:, u % 3, :], zbuf[:, u % 3, :], ACT.Exp, bias=nmax[:, u:u + 1],
                                             scale=-1.0, accum_out=den[:, HG * g + r:HG * g + r + 1])\
                            .then_inc(S["p_ready"], 1)

                    def turned_odd(u):
                        g, r = unit(u)
                        act.wait_ge(S["turned"], 2 * u + 2)
                        if g >= 2:
                            act.wait_ge(S["pv_done"], g - 1)
                        nc.scalar.activation(PT[:, g % 2, r, 4:8, :].rearrange("p t n -> p (t n)"), bank[5],
                                             ACT.Copy).then_inc(S["pt_odd"], 1)

                    def spread_copy(g):
                        act.wait_ge(S["sums_spread"], g + 1)
                        if g >= 2:
                            act.wait_ge(S["ctx_ready"], g - 1)
                        nc.scalar.activation(bcS[:, g % 2, :], bank[6 + g % 2][:, P:2 * P], ACT.Copy)\
                            .then_inc(S["sums_copied"], 1)

                    for u in range(UNITS + 10):
                        if 2 <= u < UNITS + 2:
                            turned_odd(u - 2)
                        if u < UNITS:
                            exp_unit(u)
                        if u >= 10 and (u - 10) % HG == 0 and (u - 10) // HG < GROUPS:
                            spread_copy((u - 10) // HG)

                    for k in range(NT // 2):
                        hT_pair(act, 1, k, k)
                    for k in range(NT // 2):
                        act.wait_ge(S["msg_psum"], k + 1)
                        nc.scalar.activation(msgH[:, 2 * k:2 * k + 2, 0:D], bank[4 + k].rearrange("p (t d) -> p t d", t=2),
                                             ACT.Copy).then_inc(S["msg_hi"], 1)
                    for a in range(NT):
                        if a in (NT - 3, NT - 1):
                            hT_pair(act, 2, (a - NT + 3) // 2, 4 + (a - NT + 3) // 2)
                        act.wait_ge(S["adjT_psum"], a + 1)
                        nc.scalar.activation(adjT[:, a, :], bank[6 + a % 2].bitcast(f16), ACT.Copy)\
                            .then_inc(S["adjT_ready"], 1)

                    hT_pair(act, 2, 2, 6)
                    hT_pair(act, 2, 3, 7)
                    act.wait_ge(S["gmax_ready"], 1)
                    nc.scalar.activation(zbuf[0:H, 0, :], pair[0][0:H, :], ACT.Exp, bias=gmax[0:H, 1:2],
                                         scale=STEEP).then_inc(S["steep_row"], 1)
                    act.wait_ge(S["t2_ready"], 1)
                    nc.scalar.activation(v2[:, :, :].rearrange("p t h -> p (t h)"), t2[:, 0, :], ACT.Exp, scale=SLOPE)\
                        .then_inc(S["bvexp_ready"], 1)
                    nc.scalar.activation(kexp[:, 1, :], kexp[:, 0, :], ACT.Exp, scale=STEEP).then_inc(S["bvexp_ready"], 1)
                    nc.scalar.activation(b2[:, :, :].rearrange("p t h -> p (t h)"), t2[:, 1, :], ACT.Exp, scale=STEEP)\
                        .then_inc(S["bvexp_ready"], 1)
                    for k in range(NT // 2):
                        two = slice(2 * k, 2 * k + 2)
                        if k < NT // 4:
                            act.wait_ge(S["vm_wide_front"], 2 * k + 2)
                        else:
                            act.wait_ge(S["vm_wide_back"], k - NT // 4 + 1)
                        nc.scalar.activation(vmH[:, two, :], vm_wide[:, two, :], ACT.Copy).then_inc(S["vm_hi"], 1)
                    act.wait_ge(S["kappa_ready"], 1)
                    act.wait_ge(S["bvexp_ready"], 3)

                    def den_copy(hg):
                        act.wait_ge(S["group_done"], NT * (hg + 1))
                        nc.scalar.activation(pbuf[:, 1, :], pair[2 * hg + 1][:, :], ACT.Copy).then_inc(S["den_copied"], 1)

                    for u in range(UNITS):
                        g, r = u // HG, u % HG
                        hg, jt = g // NT, g % NT
                        h = hg * HG + r
                        act.wait_ge(S["masked_steep"], u + 1)
                        if g >= 2:
                            act.wait_ge(S["group_done"], g - 1)
                        nc.scalar.activation(R[:, g % 2, r, :], zbuf[:, u % 3, :], ACT.Relu, bias=kexp[:, 2, h:h + 1],
                                             scale=b2[:, jt, h:h + 1]).then_inc(S["r_ready"], 1)

                        if u == HG * NT + 5:
                            den_copy(0)
                    act.wait_ge(S["hout_ready"], 1)
                    den_copy(1)

                    def standardise(k):
                        act.wait_ge(S["shift4_ready"], k + 1)
                        for t in (2 * k, 2 * k + 1):
                            nc.scalar.activation(xn[:, t, :], xn[:, t, :], ACT.Identity, bias=shifts[:, t:t + 1],
                                                 scale=rstd[:, t:t + 1]).then_inc(S["z4_ready"], 1)

                    standardise(0)
                    standardise(1)
                    for k in range(NT // 2):
                        if k + 2 < NT // 2:
                            standardise(k + 2)
                        act.wait_ge(S["y_ready"], k + 1)
                        nc.scalar.activation(zbuf[:, k // 2, (k % 2) * 2 * D:(k % 2 + 1) * 2 * D],
                                             xn[:, 2 * k:2 * k + 2, :].rearrange("p t d -> p (t d)"), ACT.Exp)\
                            .then_inc(S["y_exp"], 1)
                    for k in range(NT // 2 + 1):
                        if k < NT // 2:
                            normalise(act, 3, k, x)
                        if k >= 1:
                            hT_pair(act, 3, k - 1, 4 + k - 1)
                    act.wait_ge(S["f3_ready"], 1)
                    nc.scalar.activation(zbuf[:, 1, :], pair[0][:, :], ACT.Exp, bias=f3[:, 2:3], scale=SLOPE)\
                        .then_inc(S["a3_ready"], 1)
                    nc.scalar.activation(zbuf[:, 0, :], pair[0][:, :], ACT.Exp, bias=f3[:, 1:2], scale=STEEP)\
                        .then_inc(S["a3_ready"], 1)
                    act.wait_ge(S["e3_ready"], 1)
                    nc.scalar.activation(b3[:, :], e3[:, 1, :], ACT.Exp, scale=STEEP).then_inc(S["b3_ready"], 1)
                    nc.scalar.activation(k3[:, :], e3[:, 2, :], ACT.Exp, scale=-STEEP).then_inc(S["b3_ready"], 1)
                    for k in range(NT // 2):
                        act.wait_ge(S["wh3_psum"], k + 1)
                        nc.scalar.activation(V[:, 2 * k:2 * k + 2, :].rearrange("p t d -> p (t d)"), bank[4 + k], ACT.Copy)\
                            .then_inc(S["wh3_copied"], 1)
                        cast_adjacency(act, k)
                    for t in range(NT // 2, NT):
                        cast_adjacency(act, t)
                    for k in range(NT // 2):
                        normalise(act, 0, k, x_next)
                    for k in range(NT // 2):
                        act.wait_ge(S["out3_psum"], k + 1)
                        nc.scalar.activation(zbuf[:, k // 2, (k % 2) * 512:(k % 2 + 1) * 512], bank[k], ACT.Exp)\
                            .then_inc(S["o_exp"], 1)
                    for k in range(NT // 2):
                        hT_pair(act, 0, k, 4 + k)

                @block.tensor
                def _(pe):
                    def project(out, L, t, weights):
                        if L > 0:
                            pe.wait_ge(S[f"hT_ready{L}"], t // 2 + 1)
                        for c in range(DT):
                            last = nc.tensor.matmul(out, hT[:, c, t * P:(t + 1) * P], weights[:, c, :],
                                                    start=(c == 0), stop=(c == DT - 1))
                        return last

                    def project_pair(L, k, weights, done):
                        for t in (2 * k, 2 * k + 1):
                            last = project(bank[4 + k][:, (t % 2) * D:(t % 2 + 1) * D], L, t, weights)
                        last.then_inc(done, 1)

                    for p in range(CHUNKS_BEFORE, 2 * DT * NH):
                        if p >= 4:
                            pe.wait_ge(S["qk_wide"], p - 3)
                        query_key_chunk(p).then_inc(S["qk_psum"], 1)

                    def scores(u):
                        g, r = unit(u)
                        h, it = g // NT * HG + r, g % NT
                        if it == 0:
                            pe.wait_ge(S[f"query_pairs{h}"], 4 * 16)
                            pe.wait_ge(S[f"key_pairs{h}"], 4 * 16)
                        if u >= 2:
                            pe.wait_ge(S["z_ready"], u - 1)
                        for nh in range(NH):
                            last = nc.tensor.matmul(pair[u % 2][:, nh * 512:(nh + 1) * 512], QP[:, h, it * P:(it + 1) * P],
                                                    KP[:, h, nh * 512:(nh + 1) * 512], start=True, stop=True)
                        last.then_inc(S["scores"], 1)

                    def turn(u):
                        pe.wait_ge(S["p_ready"], u + 1)
                        for half in range(2):
                            if u >= 1:
                                pe.wait_ge(S["pt_odd" if half else "pt_even"], u)
                            for q in range(4):
                                j = half * 4 + q
                                last = nc.tensor.transpose(bank[4 + half][:, q * P:(q + 1) * P],
                                                           pbuf[:, u % 3, j * P:(j + 1) * P], identF[:, :])
                            last.then_inc(S["turned"], 1)

                    def weigh_values(g, quarter):
                        hg = g // NT
                        if quarter == 0:
                            pe.wait_ge(S["pt_even"], units_until(g))
                            pe.wait_ge(S["pt_odd"], units_until(g))
                            if g >= 2:
                                pe.wait_ge(S["ctx_ready"], g - 1)
                            if g >= NT + 2:
                                pe.wait_ge(S["x_done0"], g - NT - 1)
                        for j in (2 * quarter, 2 * quarter + 1):
                            for r in range(HG):
                                h = hg * HG + r
                                last = nc.tensor.matmul(bank[6 + g % 2][r * HD:(r + 1) * HD, 0:P],
                                                        V[:, j, h * HD:(h + 1) * HD], PT[:, g % 2, r, j, :],
                                                        start=(j == 0), stop=(j == NT - 1))
                        if quarter == 3:
                            last.then_inc(S["pv_done"], 1)
                            pe.wait_ge(S["rden_ready"], g + 1)
                            for r in range(HG):
                                last = nc.tensor.matmul(bank[6 + g % 2][r * HD:(r + 1) * HD, P:2 * P],
                                                        rden[:, HG * g + r:HG * g + r + 1].to_broadcast([P, HD]),
                                                        identF[:, :], start=True, stop=True)
                            last.then_inc(S["sums_spread"], 1)

                    def project_out(g):
                        it = g - NT
                        pe.wait_ge(S["ctx_ready"], g + 1)
                        for c in range(NG):
                            last = nc.tensor.matmul(bank[6 + g % 2][:, 256:256 + D], hT[:, c, it * P:(it + 1) * P],
                                                    wo[:, c, :], start=(c == 0), stop=(c == NG - 1))
                        last.then_inc(S["projected"], 1)

                    for k in range(NT // 2):
                        pe.wait_ge(S["qk_wide"], 2 * DT * NH - 3 + k)
                        project_pair(0, k, wv, S["v_psum"])
                        if k == 1:
                            scores(0)
                    for u in range(UNITS + 13):
                        if u == 2:
                            pe.wait_ge(S["v_ready"], NT // 2)
                        if 2 <= u < UNITS + 2:
                            turn(u - 2)
                        if u + 1 < UNITS:
                            scores(u + 1)
                        if u >= 12 and (u - 12) % HG == 0 and NT <= (u - 12) // HG < GROUPS:
                            project_out((u - 12) // HG)
                        if u == 9:
                            for quarter in range(4):
                                weigh_values(0, quarter)
                        if u >= 10 and (u - 6) // HG < GROUPS:
                            weigh_values((u - 6) // HG, (u - 6) % HG)

                    for k in range(NT // 2 + 1):
                        if k < NT // 2:
                            ln_pair(pe, 1, k, k)
                        if k >= 1:
                            project_pair(1, k - 1, wmsg, S["msg_psum"])
                    pe.wait_ge(S["ones_set"], 1)
                    for j in range(NT):
                        if j in (NT - 3, NT - 1):
                            ln_pair(pe, 2, (j - NT + 3) // 2, 4 + (j - NT + 3) // 2)
                        if j >= 2:
                            pe.wait_ge(S["x_done1"], j - 1)
                        for i in range(NT):
                            if j == 0:
                                pe.wait_ge(S["msg_parts"], i // 2 + 1)
                            nc.tensor.matmul(bank[j % 2][:, 0:D + 1], adjN[:, i, j * P:(j + 1) * P], msgH[:, i, 0:D + 1],
                                             start=(i == 0), stop=False)
                            last = nc.tensor.matmul(bank[j % 2][:, 0:D], adjN[:, i, j * P:(j + 1) * P], msgL[:, i, :],
                                                    start=False, stop=(i == NT - 1))
                        last.then_inc(S["agg_psum"], 1)
                        project(bank[2 + j % 2][:, 0:D], 1, j, wupd).then_inc(S["upd_psum"], 1)
                        if j >= 2:
                            pe.wait_ge(S["adjT_ready"], j - 1)
                        for i in range(NT):
                            last = nc.tensor.transpose(bank[6 + j % 2].bitcast(f16)[:, i * P:(i + 1) * P],
                                                       adjN[:, i, j * P:(j + 1) * P], identH[:, :])
                        last.then_inc(S["adjT_psum"], 1)


                    def score_rows(nh):
                        for c in range(DT):
                            last = nc.tensor.matmul(pair[0][0:2 * H, nh * 512:(nh + 1) * 512],
                                                    wa2[:, c, :, :].rearrange("p k h -> p (k h)"),
                                                    hT[:, c, nh * 512:(nh + 1) * 512], start=(c == 0), stop=(c == DT - 1))
                        last.then_inc(S["s_rows"], 1)

                    def score_cols(t):
                        for c in range(DT):
                            last = nc.tensor.matmul(bank[2][:, t * H:(t + 1) * H], hT[:, c, t * P:(t + 1) * P],
                                                    wa2[:, c, 1, :], start=(c == 0), stop=(c == DT - 1))
                        return last

                    pe.wait_ge(S["hT_ready2"], NT // 4)
                    pe.wait_ge(S["x_done1"], NT - 1)
                    score_rows(0)
                    for t in range(NT // 2):
                        score_cols(t)
                    pe.wait_ge(S["adjT_ready"], NT - 1)
                    ln_pair(pe, 2, 2, 6)
                    pe.wait_ge(S["adjT_ready"], NT)
                    ln_pair(pe, 2, 3, 7)
                    pe.wait_ge(S["hT_ready2"], NT // 2 - 1)
                    for t in range(NT // 2, NT - 2):
                        score_cols(t)
                    pe.wait_ge(S["x_done1"], NT)
                    pe.wait_ge(S["hT_ready2"], NT // 2)
                    score_rows(1)
                    for t in range(NT - 2, NT):
                        last = score_cols(t)
                    last.then_inc(S["s_cols"], 1)
                    pe.wait_ge(S["gmax_ready"], 1)
                    nc.tensor.matmul(bank[3][:, 0:H], gmax[0:2 * H, 0:1].to_broadcast([2 * H, P]),
                                     identF[0:2 * H, H:2 * H], start=True, stop=True)
                    nc.tensor.matmul(bank[3][:, H:2 * H], gmax[0:2 * H, 0:1].to_broadcast([2 * H, P]),
                                     both[0:2 * H, :], start=True, stop=True).then_inc(S["gmax_spread"], 1)
                    for k in range(NT // 2):
                        project_pair(2, k, w2, S["wh_psum"])
                    pe.wait_ge(S["kv_ready"], 1)
                    pe.wait_ge(S["wh_scaled"], NT // 2)
                    for t in range(NT):
                        for j in range(NT):
                            last = nc.tensor.matmul(bank[6][:, t * 2 * H:(t + 1) * 2 * H], adjT[:, j, t * P:(t + 1) * P],
                                                    kvHL[:, j, :], start=(j == 0), stop=(j == NT - 1))
                    last.then_inc(S["den_cols"], 1)
                    pe.wait_ge(S["steep_row"], 1)
                    pe.wait_ge(S["t2_ready"], 1)

                    def back(hg):
                        pe.wait_ge(S["num_copied"], hg + 1)
                        pe.wait_ge(S["den_copied"], hg + 1)
                        if hg == 1:
                            pe.wait_ge(S["hout_ready"], 1)
                        for t in range(NT):
                            last = nc.tensor.transpose(pair[0][:, t * P:(t + 1) * P], pbuf[:, 0, t * P:(t + 1) * P],
                                                       identF[:, :])
                        for t in range(NT):
                            last = nc.tensor.transpose(pair[1][:, t * P:(t + 1) * P], pbuf[:, 1, t * P:(t + 1) * P],
                                                       identF[:, :])
                        last.then_inc(S["back_turned"], 1)

                    def steep_share(g):
                        hg, jt = g // NT, g % NT
                        num, dnm = pair[2 * hg], pair[2 * hg + 1]
                        pe.wait_ge(S["r_ready"], HG * g + HG)
                        if g == NT:
                            pe.wait_ge(S["den_cols_read"], 1)
                        for nh in range(NH):
                            n5 = slice(nh * 512, (nh + 1) * 512)
                            for r in range(HG):
                                h = hg * HG + r
                                nc.tensor.matmul(num[r * HD:(r + 1) * HD, n5], V[:, jt, h * HD:(h + 1) * HD],
                                                 R[:, g % 2, r, n5], start=False, stop=(jt == NT - 1))
                            for r in range(HG):
                                h = hg * HG + r
                                last = nc.tensor.matmul(dnm[r * HD:(r + 1) * HD, n5],
                                                        v2[:, jt, h:h + 1].to_broadcast([P, HD]),
                                                        R[:, g % 2, r, n5], start=(jt == 0), stop=(jt == NT - 1))
                        last.then_inc(S["group_done"], 1)

                    def edge_share(g):
                        hg, jt = g // NT, g % NT
                        if hg == 0:
                            pe.wait_ge(S["vm_lo"], jt // 2 + 1)
                        for nh in range(NH):
                            n5 = slice(nh * 512, (nh + 1) * 512)
                            for vm in (vmH, vmL):
                                nc.tensor.matmul(pair[2 * hg][:, n5], vm[:, jt, hg * P:(hg + 1) * P], adjT[:, jt, n5],
                                                 start=(jt == 0 and vm is vmH), stop=False)

                    for g in range(AHEAD):
                        edge_share(g)
                    for g in range(GROUPS):
                        steep_share(g)
                        if g + AHEAD < GROUPS:
                            edge_share(g + AHEAD)
                        if g == NT + 3:
                            back(0)
                    back(1)

                    def first_rows(nh):
                        for c in range(DT):
                            last = nc.tensor.matmul(pair[0][:, nh * 512:(nh + 1) * 512], wa3[:, c, 0:1].to_broadcast([P, P]),
                                                    hT[:, c, nh * 512:(nh + 1) * 512], start=(c == 0), stop=(c == DT - 1))
                        last.then_inc(S["a3_psum"], 1)

                    def second_cols(t):
                        for c in range(DT):
                            last = nc.tensor.matmul(bank[2][:, t:t + 1], hT[:, c, t * P:(t + 1) * P],
                                                    wa3[:, c, 1:2], start=(c == 0), stop=(c == DT - 1))
                        return last

                    for k in range(NT // 2):
                        ln_pair(pe, 3, k, 4 + k)

                        if k == 2:
                            pe.wait_ge(S["hT_ready3"], NT // 4)
                            first_rows(0)
                    for t in range(NT // 2):
                        second_cols(t)
                    pe.wait_ge(S["hT_ready3"], NT // 2)
                    first_rows(1)
                    for t in range(NT // 2, NT):
                        last = second_cols(t)
                    last.then_inc(S["f3_cols"], 1)
                    for k in range(NT // 2):
                        project_pair(3, k, w3, S["wh3_psum"])
                    pe.wait_ge(S["a3_ready"], 2)
                    pe.wait_ge(S["e3_ready"], 1)
                    for j in range(NT):
                        pe.wait_ge(S["g3_ready"], j + 1)
                        for i in range(NT):
                            last = nc.tensor.matmul(pair[i // 4][:, (i % 4) * D:(i % 4 + 1) * D], PU[:, j, i * P:(i + 1) * P],
                                                    V[:, j, :], start=(j == 0 and i % 2 == 0), stop=(j == NT - 1),
                                                    skip_group_check=True)
                            if j == NT - 1 and i % 2 == 1:
                                last.then_inc(S["out3_psum"], 1)
                    start_layer0(pe)

                @block.vector
                def _(dve):
                    steps = Steps(dve, S["dve_steps"])

                    for p in range(2 * DT * NH):
                        c, isk, nh = p // 4, (p // 2) % 2, p % 2
                        hi, lo = (KH, KL) if isk else (QH, QL)
                        ready = S["k_parts" if isk else "q_parts"]
                        n5 = slice(nh * 512, (nh + 1) * 512)
                        if p == 2:
                            dve.wait_ge(S["x_taken"], 1)
                        dve.wait_ge(S["qk_wide"], p + 1)
                        nc.vector.tensor_copy(hi[:, c, n5], whole[:, p % 4, :]).then_inc(ready, 1)
                        dve.wait_ge(ready, 4 * c + 2 * nh + 1)
                        nc.vector.tensor_tensor(lo[:, c, n5], whole[:, p % 4, :], hi[:, c, n5], ALU.subtract).then_inc(ready, 1)

                    def values(k):
                        dve.wait_ge(S["v_psum"], k + 1)
                        nc.vector.tensor_tensor(V[:, 2 * k:2 * k + 2, :], bank[4 + k].rearrange("p (t d) -> p t d", t=2),
                                                bv_b[:, :].unsqueeze(1).to_broadcast([P, 2, D]), ALU.add)\
                            .then_inc(S["v_ready"], 1)

                    def mask_and_max(u):
                        it = unit(u)[0] % NT
                        dve.wait_ge(S["scores"], u + 1)
                        if u >= 3:
                            dve.wait_ge(S["p_ready"], u - 2)
                        nc.vector.tensor_tensor_reduce(out=zbuf[:, u % 3, :], in0=pair[u % 2][:, :], in1=maskN[:, it, :],
                                                       scale=-1.0, scalar=3e38, op0=ALU.add, op1=ALU.min,
                                                       accum_out=nmax[:, u:u + 1]).then_inc(S["z_ready"], 1)

                    def turned_even(u):
                        g, r = unit(u)
                        dve.wait_ge(S["turned"], 2 * u + 1)
                        if g >= 2:
                            dve.wait_ge(S["pv_done"], g - 1)
                        nc.vector.tensor_copy(PT[:, g % 2, r, 0:4, :].rearrange("p t n -> p (t n)"), bank[4])\
                            .then_inc(S["pt_even"], 1)

                    def inverse_sums(g):
                        dve.wait_ge(S["p_ready"], units_until(g))
                        nc.vector.reciprocal(rden[:, HG * g:HG * g + HG], den[:, HG * g:HG * g + HG]).then_inc(S["rden_ready"], 1)

                    def context(g):
                        hg, it = g // NT, g % NT
                        dve.wait_ge(S["sums_copied"], g + 1)
                        if g == 0:
                            dve.wait_ge(S["v_psum"], NT // 2)
                        nc.vector.tensor_tensor(hT[:, hg, it * P:(it + 1) * P], bank[6 + g % 2][:, 0:P], bcS[:, g % 2, :],
                                                ALU.mult).then_inc(S["ctx_ready"], 1)

                    def residual0(it):
                        dve.wait_ge(S["projected"], it + 1)
                        nc.vector.tensor_tensor(x[:, it, :], bank[6 + it % 2][:, 256:256 + D], x[:, it, :], ALU.add)\
                            .then_inc(S["x_done0"], 1)
                        if it == 0:
                            for h in range(H):
                                dve.wait_ge(S[f"query_pairs{h}"], 4 * 16)
                                dve.wait_ge(S[f"key_pairs{h}"], 4 * 16)
                        dve.wait_ge(S["x_done0"], it + 1)
                        if it % 2 == 1:
                            norm_stats(dve, steps, 1, it // 2, x)

                    for k in range(2):
                        values(k)
                    for u in range(UNITS + 13):
                        if u < UNITS:
                            mask_and_max(u)
                        if u == 0:
                            for k in range(2, NT // 2):
                                values(k)
                        if 2 <= u < UNITS + 2:
                            turned_even(u - 2)
                        if u == 8:
                            inverse_sums(0)
                        if u >= 9 and (u - 5) % HG == 0 and (u - 5) // HG < GROUPS:
                            inverse_sums((u - 5) // HG)
                        if u >= 11 and (u - 11) % HG == 0 and (u - 11) // HG < GROUPS:
                            context((u - 11) // HG)
                        if u >= 13 and (u - 13) % HG == 0 and NT <= (u - 13) // HG < GROUPS:
                            residual0((u - 13) // HG - NT)
                        if u >= 15 and (u - 15) % HG == 0 and (u - 15) // HG >= NT:
                            it = (u - 15) // HG - NT
                            if it % 2 == 1:
                                norm_apply(dve, 1, it // 2, x)

                    dve.wait_ge(S["scores"], UNITS)
                    nc.vector.memset(msgH[:, :, D:D + 1], 1.0).then_inc(S["ones_set"], 1)
                    for k in range(NT // 2):
                        dve.wait_ge(S["msg_hi"], k + 1)
                        nc.vector.tensor_tensor(msgL[:, 2 * k:2 * k + 2, :], bank[4 + k].rearrange("p (t d) -> p t d", t=2),
                                                msgH[:, 2 * k:2 * k + 2, 0:D], ALU.subtract).then_inc(S["msg_parts"], 1)
                    for j in range(NT):
                        u_j = zbuf[:, j % 2, 0:D]
                        dve.wait_ge(S["agg_psum"], j + 1)
                        n = steps.did(nc.vector.tensor_scalar(deg[:, j, 0:1], bank[j % 2][:, D:D + 1], 1.0, None, ALU.max))
                        dve.wait_ge(S["upd_psum"], j + 1)
                        m = steps.did(nc.vector.tensor_tensor(u_j, bank[2 + j % 2][:, 0:D], b1_b[:, :], ALU.add))
                        steps.after(n)
                        n = steps.did(nc.vector.reciprocal(deg[:, j, 1:2], deg[:, j, 0:1]))
                        steps.after(n)
                        n = steps.did(nc.vector.scalar_tensor_tensor(u_j, bank[j % 2][:, 0:D], deg[:, j, 1:2], u_j,
                                                                     ALU.mult, ALU.add))
                        steps.after(n)
                        nc.vector.scalar_tensor_tensor(x[:, j, :], u_j, 0.0, x[:, j, :], ALU.max, ALU.add)\
                            .then_inc(S["x_done1"], 1)
                        dve.wait_ge(S["x_done1"], j + 1)
                        if j % 2 == 1:
                            norm_stats(dve, steps, 2, j // 2, x)
                        elif j >= 2:
                            norm_apply(dve, 2, j // 2 - 1, x)
                    norm_apply(dve, 2, NT // 2 - 1, x)

                    for nh in range(NH):
                        dve.wait_ge(S["s_rows"], nh + 1)
                        n = steps.did(nc.vector.reduce_max(gmax[0:2 * H, 2 + nh:3 + nh],
                                                           pair[0][0:2 * H, nh * 512:(nh + 1) * 512], AX.X))
                    steps.after(n)
                    n = steps.did(nc.vector.reduce_max(gmax[0:2 * H, 0:1], gmax[0:2 * H, 2:2 + NH], AX.X))
                    steps.after(n)
                    nc.vector.tensor_scalar(gmax[0:H, 1:2], gmax[0:H, 0:1], -STEEP, None, ALU.mult)\
                        .then_inc(S["gmax_ready"], 1)
                    dve.wait_ge(S["gmax_spread"], 1)
                    n = steps.did(nc.vector.tensor_copy(gmaxB[:, 0:H], bank[3][:, 0:H]))
                    n = steps.did(nc.vector.tensor_tensor(gmaxB[:, H:2 * H], bank[3][:, H:2 * H], edge_b[:, :], ALU.add))
                    steps.after(n)
                    m = steps.did(nc.vector.tensor_scalar(kexp[:, 2, :], gmaxB[:, H:2 * H], GMAX, None, ALU.min))
                    steps.after(m)
                    n = steps.did(nc.vector.tensor_tensor(kexp[:, 0, :], kexp[:, 2, :], gmaxB[:, H:2 * H], ALU.subtract))
                    dve.wait_ge(S["s_cols"], 1)
                    t2v = t2[:, 0, :].rearrange("p (t h) -> p t h", t=NT)
                    t2w = t2[:, 1, :].rearrange("p (t h) -> p t h", t=NT)
                    n = steps.did(nc.vector.tensor_tensor(t2v, bank[2][:, 0:NT * H].rearrange("p (t h) -> p t h", t=NT),
                                                          gmaxB[:, 0:H].unsqueeze(1).to_broadcast([P, NT, H]), ALU.subtract))
                    steps.after(n)
                    nc.vector.tensor_tensor(t2w, t2v, kexp[:, 2, :].unsqueeze(1).to_broadcast([P, NT, H]), ALU.add)\
                        .then_inc(S["t2_ready"], 1)
                    dve.wait_ge(S["bvexp_ready"], 2)
                    n = steps.did(nc.vector.tensor_tensor(kv[:, :, :], v2[:, :, :],
                                                          kexp[:, 1, :].unsqueeze(1).to_broadcast([P, NT, H]), ALU.mult))
                    nc.vector.tensor_scalar(kexp[:, 2, :], kexp[:, 1, :], -1.0, None, ALU.mult).then_inc(S["kappa_ready"], 1)
                    steps.after(n)
                    n = steps.did(nc.vector.tensor_copy(kvHL[:, :, 0:H], kv[:, :, :]))
                    steps.after(n)
                    nc.vector.tensor_tensor(kvHL[:, :, H:2 * H], kv[:, :, :], kvHL[:, :, 0:H], ALU.subtract)\
                        .then_inc(S["kv_ready"], 1)

                    def heads(ap, tiles=1):
                        return ap.rearrange("p (h d) -> p h d", h=tiles * H)

                    def wh_scale(k):
                        two = slice(2 * k, 2 * k + 2)
                        dve.wait_ge(S["wh_psum"], k + 1)
                        nc.vector.tensor_tensor(V[:, two, :].rearrange("p t (h d) -> p (t h) d", h=H), heads(bank[4 + k], 2),
                                                v2[:, two, :].rearrange("p t h -> p (t h)").unsqueeze(2)
                                                .to_broadcast([P, 2 * H, HD]), ALU.mult).then_inc(S["wh_scaled"], 1)

                    def edge_sums():
                        dens = bank[6][:, 0:NT * 2 * H].rearrange("p (t k) -> p t k", t=NT)
                        dve.wait_ge(S["den_cols"], 1)
                        n = steps.did(nc.vector.tensor_copy(kv[:, :, :], dens[:, :, 0:H]))
                        steps.after(n)
                        nc.vector.tensor_tensor(kv[:, :, :], kv[:, :, :], dens[:, :, H:2 * H], ALU.add)\
                            .then_inc(S["den_cols_read"], 1)

                    def num_copy(hg):
                        dve.wait_ge(S["group_done"], NT * (hg + 1))
                        nc.vector.tensor_copy(pbuf[:, 0, :], pair[2 * hg][:, :]).then_inc(S["num_copied"], 1)

                    def hout(hg):
                        dve.wait_ge(S["back_turned"], hg + 1)
                        hs = slice(hg * HG, (hg + 1) * HG)
                        n = steps.did(nc.vector.tensor_tensor(
                            sums[:, :, hs], pair[1][:, :].rearrange("p (t h d) -> p t h d", t=NT, h=HG)[:, :, :, 0],
                            kv[:, :, hs], ALU.add))
                        steps.after(n)
                        n = steps.did(nc.vector.reciprocal(rsums[:, :, hs], sums[:, :, hs]))
                        steps.after(n)
                        for half in range(2):
                            ts = slice(half * NT // 2, (half + 1) * NT // 2)
                            last = nc.vector.tensor_tensor(
                                xn[:, ts, hg * P:(hg + 1) * P].rearrange("p t (h d) -> p t h d", h=HG),
                                pair[0][:, half * 512:(half + 1) * 512].rearrange("p (t h d) -> p t h d", t=NT // 2, h=HG),
                                rsums[:, ts, hs].unsqueeze(3).to_broadcast([P, NT // 2, HG, HD]), ALU.mult)
                        last.then_inc(S["hout_ready"], 1)

                    def mask_steep(u):
                        g, r = u // HG, u % HG
                        hg, jt = g // NT, g % NT
                        h = hg * HG + r
                        if u == 0:
                            dve.wait_ge(S["steep_out"], 16)
                        if jt == 0:
                            dve.wait_ge(S[f"steep_in{h}"], 16)
                        if u >= 3:
                            dve.wait_ge(S["r_ready"], u - 2)
                        nc.vector.tensor_tensor(zbuf[:, u % 3, :], steepT[:, h, :], adjT[:, jt, :], ALU.mult)\
                            .then_inc(S["masked_steep"], 1)

                    for k in range(NT // 2):
                        wh_scale(k)
                    for t in range(NT // 2):
                        dve.wait_ge(S["wh_scaled"], t // 2 + 1)
                        nc.vector.tensor_tensor(heads(vm_wide[:, t, :]), heads(V[:, t, :]),
                                                kexp[:, 1, :].unsqueeze(2).to_broadcast([P, H, HD]), ALU.mult)\
                            .then_inc(S["vm_wide_front"], 1)
                    for u in range(UNITS):
                        mask_steep(u)
                        if u == 12:
                            edge_sums()
                        if u == HG * NT + 5:
                            num_copy(0)
                        if u == HG * (NT + 6) + 2:
                            hout(0)
                    dve.wait_ge(S["back_turned"], 1)
                    num_copy(1)
                    hout(1)
                    dve.wait_ge(S["hout_ready"], NG)

                    def times_gamma(k):
                        two = slice(2 * k, 2 * k + 2)
                        dve.wait_ge(S["z4_ready"], 2 * k + 2)
                        nc.vector.tensor_tensor(xn[:, two, :], xn[:, two, :],
                                                gam_b[:, :].unsqueeze(1).to_broadcast([P, 2, D]), ALU.mult)\
                            .then_inc(S["gamma_done"], 1)

                    def residual2(k):
                        y = xn[:, 2 * k:2 * k + 2, :].rearrange("p t d -> p (t d)")
                        xh = x[:, 2 * k:2 * k + 2, :].rearrange("p t d -> p (t d)")
                        dve.wait_ge(S["x_less_one"], 1)
                        dve.wait_ge(S["y_exp"], k + 1)
                        n = steps.did(nc.vector.scalar_tensor_tensor(xh, zbuf[:, k // 2, (k % 2) * 2 * D:(k % 2 + 1) * 2 * D],
                                                                     1.0, xh, ALU.min, ALU.add))
                        steps.after(n)
                        nc.vector.scalar_tensor_tensor(xh, y, 0.0, xh, ALU.max, ALU.add).then_inc(S["x_done2"], 1)

                    def next_stats(k):
                        dve.wait_ge(S["x_done2"], k + 1)
                        norm_stats(dve, steps, 3, k, x)

                    HALVES = NT // 2
                    for k in range(HALVES + 2):
                        if k < HALVES:
                            norm_stats(dve, steps, 4, k, xn)
                        if 1 <= k < HALVES + 1:
                            shift(dve, 4, k - 1)
                        if k >= 2:
                            times_gamma(k - 2)
                        if k == HALVES:
                            residual2(0)
                    for k in range(1, HALVES + 2):
                        if k < HALVES:
                            residual2(k)
                        if 2 <= k < HALVES + 2:
                            shift(dve, 3, k - 2)
                        if 1 <= k < HALVES + 1:
                            next_stats(k - 1)
                    for nh in range(NH):
                        dve.wait_ge(S["a3_psum"], nh + 1)
                        n = steps.did(nc.vector.reduce_max(f3[:, 3 + nh:4 + nh], pair[0][:, nh * 512:(nh + 1) * 512], AX.X))
                    steps.after(n)
                    n = steps.did(nc.vector.reduce_max(f3[:, 0:1], f3[:, 3:3 + NH], AX.X))
                    steps.after(n)
                    n = steps.did(nc.vector.tensor_scalar(f3[:, 1:2], f3[:, 0:1], -STEEP, None, ALU.mult))
                    nc.vector.tensor_scalar(f3[:, 2:3], f3[:, 0:1], -SLOPE, None, ALU.mult).then_inc(S["f3_ready"], 1)
                    dve.wait_ge(S["f3_cols"], 1)
                    n = steps.did(nc.vector.tensor_scalar(e3[:, 0, :], bank[2][:, 0:NT], f3[:, 0:1], None, ALU.add))
                    steps.after(n)
                    nc.vector.tensor_scalar(e3[:, 1, :], e3[:, 0, :], 0.0, None, ALU.min)
                    nc.vector.tensor_scalar(e3[:, 2, :], e3[:, 0, :], 0.0, None, ALU.max).then_inc(S["e3_ready"], 1)
                    dve.wait_ge(S["a3_ready"], 2)
                    dve.wait_ge(S["b3_ready"], 2)
                    for j in range(NT):
                        n = steps.did(nc.vector.tensor_scalar(PU[:, j, :], zbuf[:, 0, :], b3[:, j:j + 1], k3[:, j:j + 1],
                                                              ALU.mult, ALU.max))
                        steps.after(n)
                        dve.wait_ge(S["mu_ready"], j + 1)
                        nc.vector.tensor_tensor_reduce(out=PU[:, j, :], in0=PU[:, j, :], in1=pbuf[:, j % 3, :], scale=1.0,
                                                       scalar=0.0, op0=ALU.mult, op1=ALU.add,
                                                       accum_out=den3[:, j:j + 1]).then_inc(S["pu_ready"], 1)
                        dve.wait_ge(S["pu_ready"], j + 1)
                        n = steps.did(nc.vector.reciprocal(rden3[:, j:j + 1], den3[:, j:j + 1]))
                        steps.after(n)
                        dve.wait_ge(S["wh3_copied"], j // 2 + 1)
                        nc.vector.tensor_scalar(V[:, j, :], V[:, j, :], rden3[:, j:j + 1], None, ALU.mult)\
                            .then_inc(S["g3_ready"], 1)
                        if j >= 1:
                            make_mask(dve, j - 1)
                        if j == 1:
                            dve.wait_ge(S["x_in"], 16)
                        if j % 2 == 1:
                            norm_stats(dve, steps, 0, j // 2, x_next)
                        elif j >= 2:
                            shift(dve, 0, j // 2 - 1)
                    make_mask(dve, NT - 1)
                    shift(dve, 0, NT // 2 - 1)

                    dve.wait_ge(S["x_less_one"], 2)
                    for k in range(NT // 2):
                        xh = x[:, 2 * k:2 * k + 2, :].rearrange("p t d -> p (t d)")
                        dve.wait_ge(S["o_exp"], k + 1)
                        n = steps.did(nc.vector.scalar_tensor_tensor(xh, zbuf[:, k // 2, (k % 2) * 512:(k % 2 + 1) * 512],
                                                                     1.0, xh, ALU.min, ALU.add))
                        steps.after(n)
                        nc.vector.scalar_tensor_tensor(xh, bank[k], 0.0, xh, ALU.max, ALU.add).then_inc(S["x_done3"], 1)

            clear_signals()

        with nc.Block() as block:
            @block.sync
            def _(sp):
                sp.wait_ge(out_written, OUT_WRITTEN)


_WEIGHTS = ["L0_gnn_Wq", "L0_gnn_bq", "L0_gnn_Wk", "L0_gnn_bk", "L0_gnn_Wv", "L0_gnn_bv", "L0_gnn_Wo", "L0_gnn_bo",
            "L1_gnn_W_msg", "L1_gnn_W_upd", "L1_gnn_bias", "L2_gnn_W", "L2_gnn_a1", "L2_gnn_a2", "L2_gnn_edge_emb",
            "L2_gnn_ln_gamma", "L2_gnn_ln_beta", "L3_gnn_W", "L3_gnn_a"]


def kernel(**inputs):
    import concourse.bacc as _bacc
    from concourse.bass_utils import run_bass_kernel_spmd as _run

    nc = _bacc.Bacc("TRN2", target_bir_lowering=False, num_devices=1)
    arrays, args = {}, {}
    for name in ["x", "adj"] + _WEIGHTS:
        a = np.ascontiguousarray(inputs[name])
        arrays[f"in_{name}"] = a
        args[name] = nc.dram_tensor(f"in_{name}", a.shape, mybir.dt.from_np(a.dtype), kind="ExternalInput").ap()
    out = nc.dram_tensor("out", inputs["x"].shape, mybir.dt.float32, kind="ExternalOutput").ap()
    build_program(nc, args["x"], args["adj"], args, out)
    r = _run(nc, [arrays], core_ids=[0])
    return r.results[0]["out"]
```
